# Optimizing a Trainium2 kernel written in Bass

```python
import numpy as np
import jax
import jax.numpy as jnp

def _softmax(x, axis=-1):
    return jax.nn.softmax(x, axis=axis)

def _gelu(x):
    return jax.nn.gelu(x, approximate=True)

def _silu(x):
    return jax.nn.silu(x)

def _sigmoid(x):
    return jax.nn.sigmoid(x)

def _layernorm(x, axis=-1, eps=1e-05):
    m = jnp.mean(x, axis=axis, keepdims=True)
    v = jnp.var(x, axis=axis, keepdims=True)
    return (x - m) / jnp.sqrt(v + eps)

def _scatter_add(tgt, idx, src, axis=0):
    return tgt.at[idx].add(src)

def _segment_sum(src, seg, n):
    return jax.ops.segment_sum(src, seg, n)
kernel_name = 'mk_macaron_d2_jaxref_r8_a8c8f8'

def setup_inputs(seed: int=0):
    np.random.seed(seed)
    _w = jnp.asarray

    def _L0_attn_setup():
        import jax, jax.numpy as jnp
        import numpy as np
        B, N, D = (2, 1024, 128)
        H = 16
        HD = D // H
        EPS = 1e-06

        def _feature_map(a):
            return jax.nn.elu(a) + 1.0
        key = jax.random.key(seed)
        ks = jax.random.split(key, 5)
        scale = 1.0 / np.sqrt(D)
        return {'x': jax.random.normal(ks[0], (B, N, D), dtype=jnp.float32), 'Wq': jax.random.normal(ks[1], (D, D), dtype=jnp.float32) * scale, 'Wk': jax.random.normal(ks[2], (D, D), dtype=jnp.float32) * scale, 'Wv': jax.random.normal(ks[3], (D, D), dtype=jnp.float32) * scale, 'Wo': jax.random.normal(ks[4], (D, D), dtype=jnp.float32) * scale}
    _L0_attn_in = _L0_attn_setup()

    def _L0_ffn_setup():
        import jax, jax.numpy as jnp
        import numpy as np
        B, T, D, E, TOP_K = (4, 512, 128, 8, 2)
        CAPACITY_FACTOR = 1.5
        key = jax.random.key(seed)
        k1, k2, k3 = jax.random.split(key, 3)
        x = jax.random.normal(k1, (B, T, D), dtype=jnp.float32)
        Wr = jax.random.normal(k2, (E, D), dtype=jnp.float32) * 0.02
        We = jax.random.normal(k3, (E, D, D), dtype=jnp.float32) * 0.02
        return {'x': x, 'Wr': Wr, 'We': We}
    _L0_ffn_in = _L0_ffn_setup()

    def _L1_attn_setup():
        import jax, jax.numpy as jnp
        import numpy as np
        import math
        D_MODEL = 128
        NUM_HEADS = 16
        D_K = D_MODEL // NUM_HEADS
        B, S = (2, 256)

        def _linear_weight(key, out_f, in_f):
            return jax.random.normal(key, (out_f, in_f), jnp.float32) * math.sqrt(2.0 / in_f)
        key = jax.random.key(seed)
        ks = jax.random.split(key, 5)
        x = jax.random.normal(ks[0], (B, S, D_MODEL), jnp.float32)
        return {'x': x, 'Wq': _linear_weight(ks[1], D_MODEL, D_MODEL), 'bq': jnp.zeros((D_MODEL,), jnp.float32), 'Wk': _linear_weight(ks[2], D_MODEL, D_MODEL), 'bk': jnp.zeros((D_MODEL,), jnp.float32), 'Wv': _linear_weight(ks[3], D_MODEL, D_MODEL), 'bv': jnp.zeros((D_MODEL,), jnp.float32), 'Wo': _linear_weight(ks[4], D_MODEL, D_MODEL), 'bo': jnp.zeros((D_MODEL,), jnp.float32)}
    _L1_attn_in = _L1_attn_setup()

    def _L1_ffn_setup():
        import jax, jax.numpy as jnp
        import numpy as np
        B, S, D, E, H = (4, 256, 128, 8, 512)
        key = jax.random.key(seed)
        ks = jax.random.split(key, 7)
        scale_d = 1.0 / np.sqrt(D)
        scale_h = 1.0 / np.sqrt(H)
        return {'x': jax.random.normal(ks[0], (B, S, D), dtype=jnp.float32), 'Wr': jax.random.uniform(ks[1], (D, E), jnp.float32, -scale_d, scale_d), 'br': jnp.zeros((E,), jnp.float32), 'W1': jax.random.uniform(ks[2], (E, D, H), jnp.float32, -scale_d, scale_d), 'b1': jax.random.uniform(ks[3], (E, H), jnp.float32, -scale_d, scale_d), 'W2': jax.random.uniform(ks[4], (E, H, D), jnp.float32, -scale_h, scale_h), 'b2': jax.random.uniform(ks[5], (E, D), jnp.float32, -scale_h, scale_h)}
    _L1_ffn_in = _L1_ffn_setup()
    _d = {'L0_attn_x': _L0_attn_in['x'], 'L0_attn_Wq': _L0_attn_in['Wq'], 'L0_attn_Wk': _L0_attn_in['Wk'], 'L0_attn_Wv': _L0_attn_in['Wv'], 'L0_attn_Wo': _L0_attn_in['Wo'], 'L0_ffn_Wr': _L0_ffn_in['Wr'], 'L0_ffn_We': _L0_ffn_in['We'], 'L1_attn_Wq': _L1_attn_in['Wq'], 'L1_attn_bq': _L1_attn_in['bq'], 'L1_attn_Wk': _L1_attn_in['Wk'], 'L1_attn_bk': _L1_attn_in['bk'], 'L1_attn_Wv': _L1_attn_in['Wv'], 'L1_attn_bv': _L1_attn_in['bv'], 'L1_attn_Wo': _L1_attn_in['Wo'], 'L1_attn_bo': _L1_attn_in['bo'], 'L1_ffn_Wr': _L1_ffn_in['Wr'], 'L1_ffn_br': _L1_ffn_in['br'], 'L1_ffn_W1': _L1_ffn_in['W1'], 'L1_ffn_b1': _L1_ffn_in['b1'], 'L1_ffn_W2': _L1_ffn_in['W2'], 'L1_ffn_b2': _L1_ffn_in['b2']}
    _x0 = _d['L0_attn_x']
    _d['L0_attn_x'] = jax.random.normal(jax.random.fold_in(jax.random.key(seed), 1), (1, 2048, 128), dtype=_x0.dtype)
    del _x0
    return _d

def reference(L0_attn_x, L0_attn_Wq, L0_attn_Wk, L0_attn_Wv, L0_attn_Wo, L0_ffn_Wr, L0_ffn_We, L1_attn_Wq, L1_attn_bq, L1_attn_Wk, L1_attn_bk, L1_attn_Wv, L1_attn_bv, L1_attn_Wo, L1_attn_bo, L1_ffn_Wr, L1_ffn_br, L1_ffn_W1, L1_ffn_b1, L1_ffn_W2, L1_ffn_b2):

    def _L0_attn_ref(x, Wq, Wk, Wv, Wo):
        import jax, jax.numpy as jnp
        import numpy as np
        B, N, D = (2, 1024, 128)
        H = 16
        HD = D // H
        EPS = 1e-06

        def _feature_map(a):
            return jax.nn.elu(a) + 1.0
        b, n, d = x.shape
        q = _feature_map((x @ Wq.T).reshape(b, n, H, HD))
        k = _feature_map((x @ Wk.T).reshape(b, n, H, HD))
        v = (x @ Wv.T).reshape(b, n, H, HD)
        kv = jnp.einsum('bnhd,bnhm->bhdm', k, v)
        k_sum = k.sum(axis=1)
        numerator = jnp.einsum('bnhd,bhdm->bnhm', q, kv)
        denominator = jnp.einsum('bnhd,bhd->bnh', q, k_sum)[..., None]
        out = numerator / (denominator + EPS)
        out = out.reshape(b, n, d)
        return out @ Wo.T

    def _L0_ffn_ref(x, Wr, We):
        import jax, jax.numpy as jnp
        import numpy as np
        B, T, D, E, TOP_K = (4, 512, 128, 8, 2)
        CAPACITY_FACTOR = 1.5
        Bb, Tt, Dd = x.shape
        Ee = Wr.shape[0]
        K = TOP_K
        C = int(Tt * K / Ee * CAPACITY_FACTOR) + 1
        logits = jnp.einsum('btd,ed->bte', x, Wr)
        top_vals, top_idx = jax.lax.top_k(logits, K)
        w = jax.nn.softmax(top_vals, axis=-1)
        flat_e = top_idx.reshape(Bb, Tt * K)
        oh = jax.nn.one_hot(flat_e, Ee, dtype=jnp.int32)
        pos_all = jnp.cumsum(oh, axis=1) - oh
        pos = jnp.take_along_axis(pos_all, flat_e[..., None], axis=-1)[..., 0]
        keep = pos < C
        b_idx = jnp.arange(Bb, dtype=jnp.int32)[:, None]
        dst = (b_idx * Ee + flat_e) * C + pos
        dst = jnp.where(keep, dst, Bb * Ee * C).reshape(-1)
        x_rep = jnp.repeat(x, K, axis=1).reshape(-1, Dd)
        buf = jnp.zeros((Bb * Ee * C, Dd), dtype=x.dtype).at[dst].add(x_rep, mode='drop')
        expert_in = buf.reshape(Bb, Ee, C, Dd)
        expert_out = jnp.einsum('becd,edf->becf', expert_in, We)
        gathered = jnp.take(expert_out.reshape(Bb * Ee * C, Dd), dst, axis=0, mode='fill', fill_value=0.0)
        gathered = gathered.reshape(Bb, Tt, K, Dd)
        out = jnp.einsum('btk,btkd->btd', w, gathered)
        return out

    def _L1_attn_ref(x, Wq, bq, Wk, bk, Wv, bv, Wo, bo):
        import jax, jax.numpy as jnp
        import numpy as np
        import math
        D_MODEL = 128
        NUM_HEADS = 16
        D_K = D_MODEL // NUM_HEADS
        B, S = (2, 256)

        def _linear_weight(key, out_f, in_f):
            return jax.random.normal(key, (out_f, in_f), jnp.float32) * math.sqrt(2.0 / in_f)
        b, s, _ = x.shape
        q = jnp.einsum('bsd,ed->bse', x, Wq) + bq
        k = jnp.einsum('bsd,ed->bse', x, Wk) + bk
        v = jnp.einsum('bsd,ed->bse', x, Wv) + bv
        q = q.reshape(b, s, NUM_HEADS, D_K).transpose(0, 2, 1, 3)
        k = k.reshape(b, s, NUM_HEADS, D_K).transpose(0, 2, 1, 3)
        v = v.reshape(b, s, NUM_HEADS, D_K).transpose(0, 2, 1, 3)
        scores = jnp.einsum('bhqd,bhkd->bhqk', q, k) / math.sqrt(D_K)
        attn = jax.nn.softmax(scores, axis=-1)
        out = jnp.einsum('bhqk,bhkd->bhqd', attn, v)
        out = out.transpose(0, 2, 1, 3).reshape(b, s, D_MODEL)
        return jnp.einsum('bsd,ed->bse', out, Wo) + bo

    def _L1_ffn_ref(x, Wr, br, W1, b1, W2, b2):
        import jax, jax.numpy as jnp
        import numpy as np
        B, S, D, E, H = (4, 256, 128, 8, 512)
        route_logits = jnp.einsum('bsd,de->bse', x, Wr) + br
        routing_weights = jax.nn.softmax(route_logits, axis=-1)
        selected_expert = jnp.argmax(routing_weights, axis=-1)
        num_experts = W1.shape[0]
        out = jnp.zeros_like(x)
        for e in range(num_experts):
            h = jax.nn.gelu(jnp.einsum('bsd,dh->bsh', x, W1[e]) + b1[e], approximate=False)
            y = jnp.einsum('bsh,hd->bsd', h, W2[e]) + b2[e]
            out = jnp.where((selected_expert == e)[..., None], y, out)
        return out
    x = L0_attn_x
    x = x + 0.5 * _L0_ffn_ref(_layernorm(x, axis=-1), L0_ffn_Wr, L0_ffn_We)
    x = x + _L0_attn_ref(_layernorm(x, axis=-1), L0_attn_Wq, L0_attn_Wk, L0_attn_Wv, L0_attn_Wo)
    x = x + 0.5 * _L0_ffn_ref(_layernorm(x, axis=-1), L0_ffn_Wr, L0_ffn_We)
    x = x + 0.5 * _L1_ffn_ref(_layernorm(x, axis=-1), L1_ffn_Wr, L1_ffn_br, L1_ffn_W1, L1_ffn_b1, L1_ffn_W2, L1_ffn_b2)
    x = x + _L1_attn_ref(_layernorm(x, axis=-1), L1_attn_Wq, L1_attn_bq, L1_attn_Wk, L1_attn_bk, L1_attn_Wv, L1_attn_bv, L1_attn_Wo, L1_attn_bo)
    x = x + 0.5 * _L1_ffn_ref(_layernorm(x, axis=-1), L1_ffn_Wr, L1_ffn_br, L1_ffn_W1, L1_ffn_b1, L1_ffn_W2, L1_ffn_b2)
    return x

_drawn_inputs = setup_inputs


def setup_inputs(seed=0):
    import zlib

    import numpy as np

    out = dict(_drawn_inputs(seed))
    spreads = {'L1_attn_bq': (0.0, 0.1),
     'L1_attn_bk': (0.0, 0.8),
     'L1_attn_bv': (0.0, 0.1),
     'L1_attn_bo': (0.0, 0.1),
     'L1_ffn_br': (0.0, 0.1)}
    factors = {'L1_ffn_b1': 2.881}
    for name, (base, spread) in spreads.items():
        noise = np.random.default_rng([zlib.crc32(name.encode()), seed]).standard_normal(out[name].shape)
        drawn = base * np.exp(spread * noise) if base else spread * noise
        out[name] = jnp.asarray(drawn.astype(out[name].dtype))
    for name, factor in factors.items():
        out[name] = (out[name] * factor).astype(out[name].dtype)
    return out
```

```python
from contextlib import ExitStack

import concourse.bass as bass
from concourse import mybir

F32 = mybir.dt.float32
BF16 = mybir.dt.bfloat16
I32 = mybir.dt.int32
U32 = mybir.dt.uint32
ALU = mybir.AluOpType
ACT = mybir.ActivationFunctionType
AX = mybir.AxisListType

P = 128
D = 128
N = 2048
T = N // P
BANK = 512
NC = N // BANK
TC = BANK // P
EPS = 1e-5
E = 8
CAP = int(N * 2 / E * 1.5) + 1
BIG = 3.0e38
LA_EPS = 1e-6
H = 16
HD = D // H
HID = 512
HC = HID // P
NT = N // P + E
SCALE = float(HD) ** -0.5

LAYERS = ["top2", "linear", "top2", "top1", "softmax", "top1"]

GH = 4
UNITS = (H // GH) * NC
TERMS = 9
KROWS = TERMS * HD
KPAD = 96
KFULL = KPAD + 2
KEY_TILES = N // P
STEPS = KEY_TILES * GH
RING = 8
SLOTS = GH * TC * 2
AHEAD = 6


def macaron(nc, x_in, wq0, wk0, wv0, wo0, wr0, we0, wq1, bq1, wk1, bk1, wv1, bv1, wo1, bo1,
            wr1, br1, w11, b11, w21, b21, out):
    with ExitStack() as ctx:
        def sb(name, shape, dt=F32):
            return ctx.enter_context(nc.sbuf_tensor(name, shape, dt))

        def sem(name):
            return ctx.enter_context(nc.semaphore(name))

        X = sb("X", [P, N])
        XN = sb("XN", [P, N])
        XT = sb("XT", [P, N])
        WQKV0 = sb("WQKV0", [P, 3 * D])
        WO0 = sb("WO0", [P, D])
        WR0 = sb("WR0", [P, E])
        WE0 = sb("WE0", [P, E * D])
        WQKV1 = sb("WQKV1", [P, 3 * D])
        WO1 = sb("WO1", [P, D])
        QKV_BIAS = sb("QKV_BIAS", [P, 3])
        BO1 = sb("BO1", [P, D])
        WR1 = sb("WR1", [P, E])
        BR1 = sb("BR1", [P, E])
        W1 = sb("W1", [P, E * HID])
        W2 = sb("W2", [P, E * HC * D])
        ident = sb("ident", [P, P])
        upper = sb("upper", [P, P], BF16)
        ones = sb("ones", [P, P], BF16)
        desc = sb("desc", [P, T * E])
        block_diag = sb("block_diag", [P, D])
        steps128 = sb("steps128", [P, E * T])
        tile_no = sb("tile_no", [P, NT * E])
        ones8 = sb("ones8", [P, E])
        zeros = sb("zeros", [P, D])
        stats = sb("stats", [P, T * 6])
        small = sb("small", [P, 12 * T])
        route = sb("route", [P, 7 * T * E])
        mask = sb("mask", [P, (T + 1) * E], BF16)
        gate = sb("gate", [P, T * E])
        dest = sb("dest", [P, T], U32)
        tile_expert = sb("tile_expert", [P, NT], I32)
        plan = sb("plan", [P, 8 * E])
        plan_big = sb("plan_big", [P, NT * E])
        arena = sb("arena", [P, 16384])
        probs = sb("probs", [P, RING * BANK])
        osb = sb("osb", [P, UNITS * BANK])
        VCUR = sb("VCUR", [P, 2 * KEY_TILES * GH * 32])
        VALL = XN

        psum = ctx.enter_context(nc.psum_tensor("psum", [P, 8 * BANK], F32))

        def bank(b, n=1):
            return psum[:, b * BANK:(b + n) * BANK]

        sorted_in = nc.dram_tensor("sorted_in", [NT * P, D], F32, kind="Internal").ap()
        sorted_out = nc.dram_tensor("sorted_out", [NT * P, D], F32, kind="Internal").ap()
        parts_dram = [nc.dram_tensor(f"{side}_parts", [H, 3, HD, N], BF16, kind="Internal").ap()
                      for side in ("q", "k")]

        def col(i, n=T):
            return small[:, i * T:i * T + n]

        def te(i):
            return route[:, i * T * E:(i + 1) * T * E].rearrange("p (t e) -> p t e", e=E)

        def over_experts(ap, m=T):
            return ap.unsqueeze(2).broadcast_to([P, m, E])

        x_loaded = [sem(f"x_loaded{c}") for c in range(NC)]
        consts_done = sem("consts_done")
        w_router = sem("w_router")
        w_top2 = sem("w_top2")
        w_linear = sem("w_linear")
        w_top1 = sem("w_top1")
        w_softmax = sem("w_softmax")
        zero_rows_done = sem("zero_rows_done")
        out_stored = sem("out_stored")
        CONSTS = 23

        stats_done, moments, var_ready, std_ready, normed, turned, xt_ready = (
            sem(n) for n in ("stats_done", "moments", "var_ready", "std_ready", "normed", "turned", "xt_ready"))
        MOMENTS = 7

        def layer_sems(k, kind):
            names = []
            if kind in ("top2", "top1"):
                names += ["logits_ready", "routing", "mask_ready", "ranks_ready", "gate_ready"]
            if kind == "top2":
                names += ["gap_ready", "gap_exp", "y_ready", "added"]
            if kind == "linear":
                names += ["q_raw", "q_neg", "q_exp", "q_done", "kv_raw", "k_neg", "k_exp", "k_done",
                          "v_done", "kv_sum", "kv_blocks", "num_ready", "den_free", "norm_chain",
                          "o_ready", "out_ready", "added"]
            if kind == "top1":
                names += ["rows_scattered", "biases_in", "t1_done", "xs_ready", "h_done", "bias_done",
                          "gelu_done", "t2_done", "ht_ready", "y_done", "y_ready", "rows_gathered",
                          "added"]
                names += [f"xs_in{u}" for u in range(4)] + [f"ys_out{u}" for u in range(4)]
            if kind == "softmax":
                names += ["proj_raw", "proj_full", "part1", "rest1", "part2", "part3", "parts_out_q",
                          "parts_out_k", "v_raw", "v_all", "pads_done", "group_in", "v_cur", "o_bank_free", "max_raw",
                          "max_read", "max_ready", "max_turned", "shift_split", "shift_in", "score_ready",
                          "exp_done", "pv_done", "o_turned", "o_recip", "o_scaled", "a_turned",
                          "a_ready", "out_ready", "bo_added", "added"]
            return {"k": k, "kind": kind} | {n: sem(f"L{k}_{n}") for n in names}

        S = [layer_sems(k, kind) for k, kind in enumerate(LAYERS)]

        def wait_x(eng, k, t):
            if k == 0:
                eng.wait_ge(x_loaded[t // TC], 16)
            elif S[k - 1]["kind"] == "top2":
                eng.wait_ge(S[k - 1]["added"], 32 * (t // 4) + (16 if t % 4 < 2 else 32))
            elif S[k - 1]["kind"] == "top1":
                eng.wait_ge(S[k - 1]["added"], t + 1)
            else:
                eng.wait_ge(S[k - 1]["added"], t // TC + 1)

        def norm_vector(vec, s):
            st = stats[:, :].rearrange("p (t s) -> p t s", s=6)
            mean_even, m2_even, mean_odd, m2_odd = st[:, :, 1], st[:, :, 2], st[:, :, 4], st[:, :, 5]
            mean_sum, mean_dif, m2, mean, dif2, dvar, var, std, rstd = (col(i) for i in range(9))
            for t in range(T):
                wait_x(vec, s["k"], t)
                nc.vector.bn_stats(st[:, t, :], X[:, t * P:(t + 1) * P]).then_inc(stats_done, 1)
            vec.wait_ge(stats_done, s["k"] * T + T)
            nc.vector.tensor_tensor(mean_sum, mean_even, mean_odd, ALU.add).then_inc(moments, 1)
            nc.vector.tensor_tensor(mean_dif, mean_even, mean_odd, ALU.subtract).then_inc(moments, 1)
            nc.vector.tensor_tensor(m2, m2_even, m2_odd, ALU.add).then_inc(moments, 1)
            vec.wait_ge(moments, s["k"] * MOMENTS + 2)
            nc.vector.tensor_tensor(dif2, mean_dif, mean_dif, ALU.mult).then_inc(moments, 1)
            nc.vector.tensor_scalar(mean, mean_sum, 0.5, None, ALU.mult).then_inc(moments, 1)
            vec.wait_ge(moments, s["k"] * MOMENTS + 4)
            nc.vector.scalar_tensor_tensor(out=dvar, in0=dif2, scalar=D / 4, in1=m2, op0=ALU.mult,
                                           op1=ALU.add).then_inc(moments, 1)
            vec.wait_ge(moments, s["k"] * MOMENTS + 6)
            nc.vector.tensor_scalar(var, dvar, 1.0 / D, EPS, ALU.mult, ALU.add).then_inc(var_ready, 1)
            vec.wait_ge(std_ready, s["k"] + 1)
            nc.vector.reciprocal(rstd, std).then_inc(moments, 1)
            vec.wait_ge(moments, s["k"] * MOMENTS + 7)
            for t in range(T):
                nc.vector.tensor_scalar(XN[:, t * P:(t + 1) * P], X[:, t * P:(t + 1) * P], mean[:, t:t + 1],
                                        rstd[:, t:t + 1], ALU.subtract, ALU.mult).then_inc(normed, 1)

        def norm_scalar(act, s):
            act.wait_ge(var_ready, s["k"] + 1)
            nc.scalar.activation(col(7), col(6), ACT.Sqrt).then_inc(std_ready, 1)
            for c in range(NC):
                act.wait_ge(turned, s["k"] * NC + c + 1)
                nc.scalar.activation(XT[:, c * BANK:(c + 1) * BANK], bank(c), ACT.Copy).then_inc(xt_ready, 1)

        def norm_tensor(pe, s):
            pe.wait_ge(consts_done, CONSTS)
            for c in range(NC):
                pe.wait_ge(normed, s["k"] * T + TC * (c + 1))
                for i in range(TC):
                    t = c * TC + i
                    mm = nc.tensor.transpose(psum[:, t * P:(t + 1) * P], XN[:, t * P:(t + 1) * P], ident[:, :])
                mm.then_inc(turned, 1)

        LG = bank(6)[:, 0:T * E]
        RANK = bank(7)[:, 0:(T + 1) * E]

        def logits_tensor(pe, s, w):
            if w is WR0:
                pe.wait_ge(w_router, 16)
            else:
                pe.wait_ge(w_top1, 16 * 4)
            for t in range(T):
                pe.wait_ge(xt_ready, s["k"] * NC + t // TC + 1)
                mm = nc.tensor.matmul(LG[:, t * E:(t + 1) * E], XT[:, t * P:(t + 1) * P], w[:, :],
                                      start=True, stop=True)
            mm.then_inc(s["logits_ready"], 1)

        def ranks_tensor(pe, s):
            pe.wait_ge(s["mask_ready"], 1)
            nc.tensor.matmul(RANK, upper[:, :], mask[:, :], start=True, stop=False)
            for d in range(1, T + 1):
                mm = nc.tensor.matmul(RANK[:, d * E:], ones[:, :], mask[:, 0:(T + 1 - d) * E],
                                      start=False, stop=(d == T))
            mm.then_inc(s["ranks_ready"], 1)

        def pick(vec, s, n, logits, largest, one_hot, work, work_max):
            nc.vector.tensor_reduce(largest, logits, AX.X, ALU.max).then_inc(s["routing"], 1)
            vec.wait_ge(s["routing"], n + 1)
            nc.vector.tensor_tensor(work, logits, over_experts(largest), ALU.is_equal).then_inc(s["routing"], 1)
            vec.wait_ge(s["routing"], n + 2)
            nc.vector.tensor_tensor(work, work, desc[:, :].rearrange("p (t e) -> p t e", e=E),
                                    ALU.mult).then_inc(s["routing"], 1)
            vec.wait_ge(s["routing"], n + 3)
            nc.vector.tensor_reduce(work_max, work, AX.X, ALU.max).then_inc(s["routing"], 1)
            vec.wait_ge(s["routing"], n + 4)
            nc.vector.tensor_tensor(one_hot, work, over_experts(work_max), ALU.is_equal).then_inc(s["routing"], 1)
            vec.wait_ge(s["routing"], n + 5)
            return n + 5

        def top2_tensor(pe, s):
            norm_tensor(pe, s)
            logits_tensor(pe, s, WR0)
            pe.wait_ge(w_top2, 16)

            def experts(t):
                u = t % 4
                if t >= 4:
                    pe.wait_ge(s["added"], 32 * (t // 4 - 1) + (16 if u < 2 else 32))
                for half in range(2):
                    mm = nc.tensor.matmul(bank(2 * u + half), XT[:, t * P:(t + 1) * P],
                                          WE0[:, half * BANK:(half + 1) * BANK], start=True, stop=True)
                mm.then_inc(s["y_ready"], 1)

            pe.wait_ge(xt_ready, s["k"] * NC + NC)
            for t in range(2):
                experts(t)
            ranks_tensor(pe, s)
            experts(2)
            pe.wait_ge(s["gate_ready"], 1)
            for t in range(3, T):
                experts(t)

        def top2_vector(vec, s):
            norm_vector(vec, s)
            L, L2, first, second, work, g1, g2 = (te(i) for i in range(7))
            top, top2, work_max, gap, gap_e, total, w_first, w_second = (col(i) for i in range(8))
            vec.wait_ge(s["logits_ready"], 1)
            nc.vector.tensor_copy(route[:, 0:T * E], LG).then_inc(s["routing"], 1)
            vec.wait_ge(s["routing"], 1)
            n = pick(vec, s, 1, L, top, first, work, work_max)
            nc.vector.scalar_tensor_tensor(out=L2, in0=first, scalar=-BIG, in1=L, op0=ALU.mult,
                                           op1=ALU.add).then_inc(s["routing"], 1)
            n += 1
            vec.wait_ge(s["routing"], n)
            n = pick(vec, s, n, L2, top2, second, work, work_max)
            nc.vector.tensor_tensor(mask[:, 0:T * E].rearrange("p (t e) -> p t e", e=E), first, second,
                                    ALU.add).then_inc(s["mask_ready"], 1)
            nc.vector.tensor_tensor(gap, top2, top, ALU.subtract).then_inc(s["gap_ready"], 1)
            vec.wait_ge(s["gap_exp"], 1)
            nc.vector.tensor_scalar(total, gap_e, 1.0, 2.0, ALU.add, ALU.mult).then_inc(s["routing"], 1)
            vec.wait_ge(s["routing"], n + 1)
            nc.vector.reciprocal(w_first, total).then_inc(s["routing"], 1)
            vec.wait_ge(s["routing"], n + 2)
            nc.vector.tensor_tensor(w_second, w_first, gap_e, ALU.mult).then_inc(s["routing"], 1)
            nc.vector.tensor_tensor(g1, first, over_experts(w_first), ALU.mult).then_inc(s["routing"], 1)
            vec.wait_ge(s["routing"], n + 3)
            nc.vector.tensor_tensor(g2, second, over_experts(w_second), ALU.mult).then_inc(s["routing"], 1)
            vec.wait_ge(s["routing"], n + 5)
            nc.vector.tensor_tensor(g1, g1, g2, ALU.add).then_inc(s["routing"], 1)
            vec.wait_ge(s["routing"], n + 6)
            vec.wait_ge(s["ranks_ready"], 1)
            nc.vector.scalar_tensor_tensor(out=gate[:, :], in0=RANK[:, 0:T * E], scalar=float(CAP),
                                           in1=route[:, 5 * T * E:6 * T * E], op0=ALU.is_lt,
                                           op1=ALU.mult).then_inc(s["gate_ready"], 1)
            vec.wait_ge(s["gate_ready"], 1)
            with vec.Fori(0, T // 4) as i:
                for first_of_pair in (0, 2):
                    for e in range(E):
                        for u in (first_of_pair, first_of_pair + 1):
                            step = first_of_pair * E + 2 * e + u - first_of_pair
                            if e == 0:
                                vec.wait_ge(s["y_ready"], i * 4 + (u + 1))
                            else:
                                vec.wait_ge(s["added"], i * 32 + (step - 1))
                            x_tile = X[:, bass.ds(i * (4 * P) + u * P, P)]
                            nc.vector.scalar_tensor_tensor(
                                out=x_tile, in0=psum[:, (2 * u) * BANK + e * D:(2 * u) * BANK + (e + 1) * D],
                                scalar=gate[:, bass.ds(i * (4 * E) + (u * E + e), 1)], in1=x_tile,
                                op0=ALU.mult, op1=ALU.add).then_inc(s["added"], 1)

        def top2_scalar(act, s):
            norm_scalar(act, s)
            act.wait_ge(s["gap_ready"], 1)
            nc.scalar.activation(col(4), col(3), ACT.Exp).then_inc(s["gap_exp"], 1)

        QF = arena[:, 0:N]
        KF = arena[:, N:2 * N]
        VF = arena[:, 2 * N:2 * N + T * (D + 1)].rearrange("p (t d) -> p t d", d=D + 1)
        la = 3 * N + 64
        QNEG = arena[:, la:la + 2 * BANK]
        KNEG = arena[:, la + 2 * BANK:la + 4 * BANK]
        KV = arena[:, la + 4 * BANK:la + 4 * BANK + D]
        KSUM = arena[:, la + 4 * BANK + D:la + 4 * BANK + 2 * D]
        RDEN = arena[:, la + 5 * BANK:la + 7 * BANK]
        ON = arena[:, la + 7 * BANK:la + 9 * BANK]

        def linear_tensor(pe, s):
            norm_tensor(pe, s)
            pe.wait_ge(w_linear, 16 * 4)
            for c in range(NC):
                pe.wait_ge(xt_ready, s["k"] * NC + c + 1)
                if c >= 2:
                    pe.wait_ge(s["q_done"], c - 1)
                nc.tensor.matmul(bank(4 + c % 2), WQKV0[:, 0:D], XT[:, c * BANK:(c + 1) * BANK],
                                 start=True, stop=True).then_inc(s["q_raw"], 1)
                for pair in range(2):
                    n = 2 * c + pair
                    if n >= 2:
                        pe.wait_ge(s["k_done"], n - 1)
                        pe.wait_ge(s["v_done"], n - 1)
                    for i in range(2):
                        t = 2 * n + i
                        mm = nc.tensor.matmul(bank(6 + n % 2)[:, i * 2 * D:(i + 1) * 2 * D],
                                              XT[:, t * P:(t + 1) * P], WQKV0[:, D:3 * D],
                                              start=True, stop=True)
                    mm.then_inc(s["kv_raw"], 1)
            for t in range(T):
                if t % 2 == 0:
                    pe.wait_ge(s["k_done"], t // 2 + 1)
                    pe.wait_ge(s["v_done"], t // 2 + 1)
                mm = nc.tensor.matmul(bank(0)[:, 0:D + 1], KF[:, t * P:(t + 1) * P], VF[:, t, :],
                                      start=(t == 0), stop=(t == T - 1))
            mm.then_inc(s["kv_sum"], 1)

            def project(c):
                pe.wait_ge(s["o_ready"], c + 1)
                if c >= 2:
                    pe.wait_ge(s["added"], c - 1)
                for i in range(TC):
                    mm = nc.tensor.matmul(bank(5 + c % 2)[:, i * D:(i + 1) * D],
                                          ON[:, (c % 2) * BANK + i * P:(c % 2) * BANK + (i + 1) * P],
                                          WO0[:, :], start=True, stop=True)
                mm.then_inc(s["out_ready"], 1)

            pe.wait_ge(s["kv_blocks"], 2)
            pe.wait_ge(s["q_done"], NC)
            for c in range(NC):
                if c >= 2:
                    pe.wait_ge(s["o_ready"], c - 1)
                q = QF[:, c * BANK:(c + 1) * BANK]
                nc.tensor.matmul(bank(2 + 2 * (c % 2)), KSUM, q, start=True, stop=True)
                nc.tensor.matmul(bank(1 + 2 * (c % 2)), KV, q, start=True, stop=True).then_inc(s["num_ready"], 1)
                if c >= 1:
                    project(c - 1)
            project(NC - 1)

        def linear_vector(vec, s):
            norm_vector(vec, s)
            nc.vector.memset(VF[:, :, D:D + 1], 1.0).then_inc(s["k_neg"], 1)
            for c in range(NC):
                qn = QNEG[:, (c % 2) * BANK:(c % 2 + 1) * BANK]
                vec.wait_ge(s["q_raw"], c + 1)
                nc.vector.tensor_scalar(qn, bank(4 + c % 2), 0.0, None, ALU.min).then_inc(s["q_neg"], 1)

                def k_raw(n):
                    return bank(6 + n % 2).rearrange("p (i x) -> p i x", i=2)[:, :, 0:D]

                def k_neg(n):
                    return KNEG[:, (n % 2) * BANK:(n % 2) * BANK + 2 * D].rearrange("p (i x) -> p i x", i=2)

                for n in (2 * c, 2 * c + 1):
                    vec.wait_ge(s["kv_raw"], n + 1)
                    nc.vector.tensor_scalar(k_neg(n), k_raw(n), 0.0, None, ALU.min).then_inc(s["k_neg"], 1)
                vec.wait_ge(s["q_exp"], c + 1)
                nc.vector.scalar_tensor_tensor(out=QF[:, c * BANK:(c + 1) * BANK], in0=bank(4 + c % 2), scalar=0.0,
                                               in1=qn, op0=ALU.max, op1=ALU.add).then_inc(s["q_done"], 1)
                for n in (2 * c, 2 * c + 1):
                    vec.wait_ge(s["k_exp"], n + 1)
                    vec.wait_ge(s["v_done"], n + 1)
                    nc.vector.scalar_tensor_tensor(
                        out=KF[:, n * 2 * P:(n + 1) * 2 * P].rearrange("p (i x) -> p i x", i=2), in0=k_raw(n),
                        scalar=0.0, in1=k_neg(n), op0=ALU.max, op1=ALU.add).then_inc(s["k_done"], 1)
            vec.wait_ge(s["kv_sum"], 1)
            vec.wait_ge(consts_done, CONSTS)
            nc.vector.tensor_tensor(KV, bank(0)[:, 0:D], block_diag[:, :], ALU.mult).then_inc(s["kv_blocks"], 1)
            nc.vector.tensor_scalar(KSUM, block_diag[:, :], bank(0)[:, D:D + 1], None,
                                    ALU.mult).then_inc(s["kv_blocks"], 1)
            for c in range(NC + 1):
                if c < NC:
                    rden = RDEN[:, (c % 2) * BANK:(c % 2 + 1) * BANK]
                    vec.wait_ge(s["num_ready"], c + 1)
                    nc.vector.tensor_scalar(rden, bank(2 + 2 * (c % 2)), LA_EPS, None,
                                            ALU.add).then_inc(s["norm_chain"], 1)
                    vec.wait_ge(s["norm_chain"], 2 * c + 1)
                    nc.vector.reciprocal(rden, rden).then_inc(s["norm_chain"], 1)
                    vec.wait_ge(s["norm_chain"], 2 * c + 2)
                    if c >= 2:
                        vec.wait_ge(s["out_ready"], c - 1)
                    nc.vector.tensor_tensor(ON[:, (c % 2) * BANK:(c % 2 + 1) * BANK], bank(1 + 2 * (c % 2)), rden,
                                            ALU.mult).then_inc(s["o_ready"], 1)
                if c >= 1:
                    b = c - 1
                    vec.wait_ge(s["out_ready"], b + 1)
                    x_chunk = X[:, b * BANK:(b + 1) * BANK]
                    nc.vector.tensor_tensor(x_chunk, bank(5 + b % 2), x_chunk, ALU.add).then_inc(s["added"], 1)

        def linear_scalar(act, s):
            norm_scalar(act, s)
            for c in range(NC):
                qn = QNEG[:, (c % 2) * BANK:(c % 2 + 1) * BANK]
                act.wait_ge(s["q_neg"], c + 1)
                nc.scalar.activation(qn, qn, ACT.Exp).then_inc(s["q_exp"], 1)
                for n in (2 * c, 2 * c + 1):
                    kn = KNEG[:, (n % 2) * BANK:(n % 2) * BANK + 2 * D]
                    act.wait_ge(s["k_neg"], n + 2)
                    nc.scalar.activation(kn, kn, ACT.Exp).then_inc(s["k_exp"], 1)
                    nc.scalar.activation(VF[:, 2 * n:2 * n + 2, 0:D],
                                         bank(6 + n % 2).rearrange("p (i x) -> p i x", i=2)[:, :, D:2 * D],
                                         ACT.Copy).then_inc(s["v_done"], 1)

        B1 = arena[:, 0:E * HID]
        B2 = arena[:, E * HID:E * HID + E * D]
        o = E * HID + E * D
        XS_IN = [arena[:, o + u * P:o + (u + 1) * P] for u in range(4)]
        o += 4 * P
        XS = [arena[:, o + u * P:o + (u + 1) * P] for u in range(2)]
        o += 2 * P
        HB = [arena[:, o + u * HID:o + (u + 1) * HID] for u in range(2)]
        o += 2 * HID
        HG = [arena[:, o + u * HID:o + (u + 1) * HID] for u in range(2)]
        o += 2 * HID
        HT = [arena[:, o + u * HID:o + (u + 1) * HID] for u in range(2)]
        o += 2 * HID
        YS = [arena[:, o + u * D:o + (u + 1) * D] for u in range(4)]
        YG = XT

        def sorted_steps(eng, step):
            for j in range(6):
                step(j, j % 4, True, j)
            with eng.Fori(0, (NT - 8) // 4) as i:
                for j in range(6, 10):
                    step(i * 4 + j, j % 4, False, None)
            for j in range(NT - 2, NT + 2):
                step(j, j % 4, True, j)

        def expert_of(eng, j):
            where = tile_expert[0:1, j:j + 1] if isinstance(j, int) else tile_expert[0:1, bass.ds(j, 1)]
            return eng.value_load(where, min_val=0, max_val=E - 1)

        def top1_tensor(pe, s):
            norm_tensor(pe, s)
            logits_tensor(pe, s, WR1)
            ranks_tensor(pe, s)
            pe.wait_ge(s["gate_ready"], 2)
            pe.wait_ge(w_top1, 16 * 4)

            def step(j, u, static, at):
                def exists(lag):
                    return not static or 0 <= at - lag < NT

                def back(lag):
                    return not static or at - lag >= 0
                if exists(-1):
                    v = (u + 1) % 4
                    xs_in = (s["xs_in0"], s["xs_in1"], s["xs_in2"], s["xs_in3"])[v]
                    pe.wait_ge(xs_in, 4 * (j + 1 - v) + 16)
                    if back(1):
                        pe.wait_ge(s["xs_ready"], j)
                    nc.tensor.transpose(bank(v % 2)[:, 0:P], XS_IN[v], ident[:, :]).then_inc(s["t1_done"], 1)
                if exists(0):
                    e = expert_of(pe, j)
                    pe.wait_ge(s["xs_ready"], j + 1)
                    if back(2):
                        pe.wait_ge(s["bias_done"], j - 1)
                    nc.tensor.matmul(bank(2 + u % 2), XS[u % 2], W1[:, bass.ds(e * HID, HID)],
                                     start=True, stop=True).then_inc(s["h_done"], 1)
                if exists(1):
                    v = (u + 3) % 4
                    pe.wait_ge(s["gelu_done"], j)
                    if back(3):
                        pe.wait_ge(s["ht_ready"], j - 2)
                    for c in range(HC):
                        mm = nc.tensor.transpose(bank(4 + v % 2)[:, c * P:(c + 1) * P],
                                                 HG[v % 2][:, c * P:(c + 1) * P], ident[:, :])
                    mm.then_inc(s["t2_done"], 1)
                if exists(2):
                    v = (u + 2) % 4
                    e = expert_of(pe, j - 2)
                    pe.wait_ge(s["ht_ready"], j - 1)
                    if back(4):
                        pe.wait_ge(s["y_ready"], j - 3)
                    for c in range(HC):
                        mm = nc.tensor.matmul(bank(6 + v % 2)[:, 0:D], HT[v % 2][:, c * P:(c + 1) * P],
                                              W2[:, bass.ds(e * HID + c * D, D)], start=(c == 0),
                                              stop=(c == HC - 1))
                    mm.then_inc(s["y_done"], 1)

            pe.wait_ge(s["xs_in0"], 16)
            nc.tensor.transpose(bank(0)[:, 0:P], XS_IN[0], ident[:, :]).then_inc(s["t1_done"], 1)
            sorted_steps(pe, step)

        def top1_vector(vec, s):
            norm_vector(vec, s)
            L, first, work, ranked = te(0), te(2), te(4), te(5)
            top, work_max, slot = col(0), col(2), col(3)
            vec.wait_ge(s["logits_ready"], 1)
            vec.wait_ge(w_top1, 16 * 4)
            nc.vector.tensor_tensor(L, LG.rearrange("p (t e) -> p t e", e=E),
                                    BR1[:, :].unsqueeze(1).broadcast_to([P, T, E]), ALU.add).then_inc(s["routing"], 1)
            vec.wait_ge(s["routing"], 1)
            n = pick(vec, s, 1, L, top, first, work, work_max)
            nc.vector.tensor_copy(mask[:, 0:T * E].rearrange("p (t e) -> p t e", e=E), first).then_inc(s["mask_ready"], 1)
            counts, tiles, tiles_to, slot0 = (plan[:, i * E:(i + 1) * E] for i in range(4))
            vec.wait_ge(s["ranks_ready"], 1)
            nc.vector.tensor_copy(counts, RANK[:, T * E:(T + 1) * E]).then_inc(s["routing"], 1)
            vec.wait_ge(s["routing"], n + 1)
            full = te(6).rearrange("p t e -> p (t e)").rearrange("p (e j) -> p e j", e=E)
            nc.vector.tensor_tensor(full, counts.unsqueeze(2).broadcast_to([P, E, T]),
                                    steps128[:, :].rearrange("p (e j) -> p e j", e=E), ALU.is_gt).then_inc(s["routing"], 1)
            vec.wait_ge(s["routing"], n + 2)
            nc.vector.tensor_reduce(tiles, full, AX.X, ALU.add).then_inc(s["routing"], 1)
            vec.wait_ge(s["routing"], n + 3)
            nc.vector.tensor_tensor_scan(tiles_to, ones8[:, :], tiles, 0.0, ALU.mult, ALU.add).then_inc(s["routing"], 1)
            vec.wait_ge(s["routing"], n + 4)
            nc.vector.tensor_tensor(slot0, tiles_to, tiles, ALU.subtract).then_inc(s["routing"], 1)
            vec.wait_ge(s["routing"], n + 5)
            nc.vector.scalar_tensor_tensor(out=ranked, in0=slot0.unsqueeze(1).broadcast_to([P, T, E]),
                                           scalar=float(P), in1=RANK[:, 0:T * E].rearrange("p (t e) -> p t e", e=E),
                                           op0=ALU.mult, op1=ALU.add).then_inc(s["routing"], 1)
            vec.wait_ge(s["routing"], n + 6)
            nc.vector.tensor_tensor(ranked, ranked, first, ALU.mult).then_inc(s["routing"], 1)
            vec.wait_ge(s["routing"], n + 7)
            nc.vector.tensor_reduce(slot, ranked, AX.X, ALU.add).then_inc(s["routing"], 1)
            vec.wait_ge(s["routing"], n + 8)
            nc.vector.tensor_copy(dest[:, :], slot).then_inc(s["gate_ready"], 1)
            before = plan_big[:, :].rearrange("p (j e) -> p j e", e=E)
            nc.vector.tensor_tensor(before, tiles_to.unsqueeze(1).broadcast_to([P, NT, E]),
                                    tile_no[:, :].rearrange("p (j e) -> p j e", e=E), ALU.is_le).then_inc(s["routing"], 1)
            vec.wait_ge(s["routing"], n + 9)
            ended = small[:, 4 * T:4 * T + NT]
            nc.vector.tensor_reduce(ended, before, AX.X, ALU.add).then_inc(s["routing"], 1)
            vec.wait_ge(s["routing"], n + 10)
            nc.vector.tensor_scalar(tile_expert[:, :], ended, float(E - 1), None, ALU.min).then_inc(s["gate_ready"], 1)
            vec.wait_ge(s["gate_ready"], 2)
            vec.wait_ge(s["biases_in"], 32)

            def rows_out(j, v):
                nc.vector.tensor_copy(XS[v % 2], bank(v % 2)[:, 0:P]).then_inc(s["xs_ready"], 1)

            def step(j, u, static, at):
                def exists(lag):
                    return not static or 0 <= at - lag < NT

                def back(lag):
                    return not static or at - lag >= 0
                if exists(-1):
                    v = (u + 1) % 4
                    vec.wait_ge(s["t1_done"], j + 2)
                    if back(1):
                        vec.wait_ge(s["h_done"], j)
                    rows_out(j + 1, v)
                if exists(0):
                    e = expert_of(vec, j)
                    vec.wait_ge(s["h_done"], j + 1)
                    if back(2):
                        vec.wait_ge(s["gelu_done"], j - 1)
                    nc.vector.tensor_tensor(HB[u % 2], bank(2 + u % 2), B1[:, bass.ds(e * HID, HID)],
                                            ALU.add).then_inc(s["bias_done"], 1)
                if exists(2):
                    v = (u + 2) % 4
                    e = expert_of(vec, j - 2)
                    vec.wait_ge(s["y_done"], j - 1)
                    if back(6):
                        ys_out = (s["ys_out0"], s["ys_out1"], s["ys_out2"], s["ys_out3"])[v]
                        vec.wait_ge(ys_out, 4 * (j - 2 - v))
                    nc.vector.tensor_tensor(YS[v], bank(6 + v % 2)[:, 0:D], B2[:, bass.ds(e * D, D)],
                                            ALU.add).then_inc(s["y_ready"], 1)

            vec.wait_ge(s["t1_done"], 1)
            rows_out(0, 0)
            sorted_steps(vec, step)
            vec.wait_ge(s["rows_gathered"], 16 * T)
            for t in range(T):
                x_tile = X[:, t * P:(t + 1) * P]
                nc.vector.scalar_tensor_tensor(out=x_tile, in0=YG[:, t * P:(t + 1) * P], scalar=0.5, in1=x_tile,
                                               op0=ALU.mult, op1=ALU.add).then_inc(s["added"], 1)

        def top1_scalar(act, s):
            norm_scalar(act, s)

            def step(j, u, static, at):
                def exists(lag):
                    return not static or 0 <= at - lag < NT

                def back(lag):
                    return not static or at - lag >= 0
                if exists(1):
                    v = (u + 3) % 4
                    act.wait_ge(s["t2_done"], j)
                    if back(3):
                        act.wait_ge(s["y_done"], j - 2)
                    nc.scalar.activation(HT[v % 2], bank(4 + v % 2), ACT.Copy).then_inc(s["ht_ready"], 1)
                if exists(0):
                    act.wait_ge(s["bias_done"], j + 1)
                    if back(2):
                        act.wait_ge(s["t2_done"], j - 1)
                    nc.scalar.activation(HG[u % 2], HB[u % 2], ACT.Gelu).then_inc(s["gelu_done"], 1)

            sorted_steps(act, step)

        def top1_gpsimd(pool, s):
            pool.wait_ge(s["gate_ready"], 1)
            pool.wait_ge(normed, s["k"] * T + T)
            pool.wait_ge(zero_rows_done, 16 * NT)
            for before in S[:s["k"]]:
                if before["kind"] == "top1":
                    pool.wait_ge(before["t1_done"], NT)
            for t in range(T):
                nc.gpsimd.indirect_dma_start(sorted_in[:, :], bass.IndirectOffsetOnAxis(dest[:, t:t + 1], 0),
                                             XN[:, t * P:(t + 1) * P], None).then_inc(s["rows_scattered"], 16)
            ys_out = (s["ys_out0"], s["ys_out1"], s["ys_out2"], s["ys_out3"])
            with pool.Fori(0, NT // 4) as i:
                for u in range(4):
                    pool.wait_ge(s["y_ready"], i * 4 + (u + 1))
                    nc.gpsimd.dma_start(sorted_out[bass.ds(i * (4 * P) + u * P, P), :], YS[u]).then_inc(ys_out[u], 16)
            for u in range(4):
                pool.wait_ge(ys_out[u], 16 * (NT // 4))
            pool.wait_ge(s["logits_ready"], 1)
            for t in range(T):
                nc.gpsimd.indirect_dma_start(YG[:, t * P:(t + 1) * P], None, sorted_out[:, :],
                                             bass.IndirectOffsetOnAxis(dest[:, t:t + 1], 0)).then_inc(s["rows_gathered"], 16)

        def top1_sync(sp, s):
            wait_x(sp, s["k"], T - 1)
            sp.dma_start(B1, b11.partition_broadcast(P)).then_inc(s["biases_in"], 16)
            sp.dma_start(B2, b21.partition_broadcast(P)).then_inc(s["biases_in"], 16)
            sp.wait_ge(s["rows_scattered"], 16 * T)
            xs_in = (s["xs_in0"], s["xs_in1"], s["xs_in2"], s["xs_in3"])
            for u in range(4):
                sp.dma_start(XS_IN[u], sorted_in[u * P:(u + 1) * P, :]).then_inc(xs_in[u], 16)
            with sp.Fori(1, NT // 4) as i:
                for u in range(4):
                    sp.wait_ge(s["t1_done"], i * 4 + (u - 3))
                    sp.dma_start(XS_IN[u], sorted_in[bass.ds(i * (4 * P) + u * P, P), :]).then_inc(xs_in[u], 16)

        GCOLS = GH * 2 * N
        QS = arena[:, 0:GCOLS // 2].bitcast(BF16)
        KS = arena[:, GCOLS // 2:GCOLS].bitcast(BF16)
        PARTS = [osb[:, i * 3 * N // 2:(i + 1) * 3 * N // 2].bitcast(BF16) for i in range(2)]
        FULL = probs
        vcur = VCUR[:, :].rearrange("p (b t h c) -> p b t h c", b=2, t=KEY_TILES, h=GH)
        shift = stats
        halves = sb("halves", [P, SLOTS])
        minus_max = sb("minus_max", [P, GH * TC])
        shift_parts = sb("shift_parts", [GH * TC, 2 * P], BF16)
        AO = XN
        AOT = XT
        recips = sb("recips", [P, 2 * GH * TC])

        def q_at(u):
            return (u & 7) * (GH * BANK)

        def k_at(u):
            return ((u >> 2) & 1) * N

        def cols(buf, rows, base, at, n):
            if isinstance(at, int):
                return buf[0:rows, base + at:base + at + n]
            return buf[0:rows, bass.ds(at + base, n)]

        def turn_on_tensor(pe, s, u, more):
            pe.wait_ge(s["max_ready"], u + 1)
            if more:
                pe.wait_ge(s["max_read"], (u + 1) * SLOTS + 1)
            nc.tensor.transpose(bank(3)[0:GH * TC, 0:P], minus_max[:, :], ident[:, :]).then_inc(s["max_turned"], 1)

        def max_matmuls(pe, s, u, slot):
            head, tile, half = slot // (2 * TC), (slot // 2) % TC, slot % 2
            out_bank = 3 + 2 * (slot % 2)
            for part in range(2):
                if part == 0:
                    if slot == 0:
                        pe.wait_ge(s["group_in"], ((u >> 2) + 1) * (16 * 6 * GH))
                    if slot >= 2 or not (isinstance(u, int) and u == 0):
                        pe.wait_ge(s["max_read"], u * SLOTS + (slot - 1))
                    if slot == 2 and not (isinstance(u, int) and u == 0):
                        pe.wait_ge(s["shift_split"], u)
                mm = nc.tensor.matmul(bank(out_bank + part),
                                      cols(QS, KPAD, head * BANK + tile * P, q_at(u), P),
                                      cols(KS, KPAD, head * 2 * N + (2 * half + part) * BANK, k_at(u), BANK),
                                      start=True, stop=True)
                if part == 1:
                    mm.then_inc(s["max_raw"], 1)
                yield

        def softmax_tensor(pe, s):
            norm_tensor(pe, s)
            pe.wait_ge(w_softmax, 16 * 8)
            for i, side in enumerate((1, 0)):
                for c in range(NC):
                    n = i * NC + c
                    pe.wait_ge(xt_ready, s["k"] * NC + c + 1)
                    if n >= 2:
                        pe.wait_ge(s["proj_full"], n - 1)
                    nc.tensor.matmul(bank(4 + n % 2), WQKV1[:, side * D:(side + 1) * D],
                                     XT[:, c * BANK:(c + 1) * BANK], start=True, stop=True).then_inc(s["proj_raw"], 1)
            for c in range(NC):
                if c >= 2:
                    pe.wait_ge(s["v_all"], c - 1)
                for i in range(TC):
                    t = c * TC + i
                    mm = nc.tensor.matmul(bank(6 + c % 2)[:, i * D:(i + 1) * D], XT[:, t * P:(t + 1) * P],
                                          WQKV1[:, 2 * D:3 * D], start=True, stop=True)
                mm.then_inc(s["v_raw"], 1)

            def scores(n, kt, j):
                i = kt * GH + j
                if i == 0:
                    pe.wait_ge(s["shift_in"], (n + 1) * 32)
                elif i >= 3:
                    pe.wait_ge(s["exp_done"], n * STEPS + (i - 2))
                nc.tensor.matmul(bank(i % 3), cols(KS, KFULL, j * 2 * N + kt * P, k_at(n), P),
                                 cols(QS, KFULL, j * BANK, q_at(n), BANK), start=True,
                                 stop=True).then_inc(s["score_ready"], 1)

            def values(n, kt, parity):
                pe.wait_ge(s["exp_done"], n * STEPS + GH * (kt + 1))
                if kt == 0:
                    pe.wait_ge(s["v_cur"], n + 1)
                    pe.wait_ge(s["o_bank_free"], n + 1)
                for j in range(GH):
                    slot = (kt * GH + j) % RING
                    mm = nc.tensor.matmul(bank(7)[32 * j:32 * j + 32, :], vcur[:, parity, kt, j, :],
                                          probs[:, slot * BANK:(slot + 1) * BANK], start=(kt == 0),
                                          stop=(kt == KEY_TILES - 1))
                mm.then_inc(s["pv_done"], 1)

            def unit(n, parity, maxima, next_maxima):
                for kt in range(KEY_TILES):
                    fill = []
                    slot = AHEAD + 2 * kt
                    if kt == KEY_TILES - 2 and maxima:
                        turn_on_tensor(pe, s, n + 1, next_maxima)
                    if slot < SLOTS:
                        if maxima:
                            fill = [max_matmuls(pe, s, n + 1, slot), max_matmuls(pe, s, n + 1, slot + 1)]
                    elif next_maxima:
                        fill = [max_matmuls(pe, s, n + 2, slot - SLOTS), max_matmuls(pe, s, n + 2, slot + 1 - SLOTS)]
                    for j in range(GH):
                        scores(n, kt, j)
                        if fill:
                            next(fill[j // 2])
                    if kt >= 1:
                        values(n, kt - 1, parity)
                values(n, KEY_TILES - 1, parity)

            pe.wait_ge(s["proj_full"], 2 * NC)
            pe.wait_ge(s["v_all"], NC - 1)
            pe.wait_ge(s["o_bank_free"], 1)
            for slot in range(SLOTS):
                for _ in max_matmuls(pe, s, 0, slot):
                    pass
            for slot in range(AHEAD):
                if slot == 2:
                    turn_on_tensor(pe, s, 0, True)
                for _ in max_matmuls(pe, s, 1, slot):
                    pass
            with pe.Fori(0, UNITS // 2 - 1) as m:
                unit(m * 2, 0, True, True)
                unit(m * 2 + 1, 1, True, True)
            unit(UNITS - 2, 0, True, False)
            unit(UNITS - 1, 1, False, False)

            for c in range(NC):
                for g in range(H // GH):
                    pe.wait_ge(s["o_bank_free"], g * NC + c + 2)
                    if c >= 1:
                        pe.wait_ge(s["o_scaled"], (c - 1) * GH + g + 1)
                    for i in range(TC):
                        at = g * N + c * BANK + i * P
                        mm = nc.tensor.transpose(bank(g)[:, i * P:(i + 1) * P], osb[:, at:at + P], ident[:, :])
                    mm.then_inc(s["o_turned"], 1)
                pe.wait_ge(s["o_scaled"], (c + 1) * GH)
                if c >= 2:
                    pe.wait_ge(s["a_ready"], c - 1)
                for i in range(TC):
                    t = c * TC + i
                    mm = nc.tensor.transpose(bank(4 + c % 2)[:, i * P:(i + 1) * P], AO[:, t * P:(t + 1) * P],
                                             ident[:, :])
                mm.then_inc(s["a_turned"], 1)
                pe.wait_ge(s["a_ready"], c + 1)
                if c >= 2:
                    pe.wait_ge(s["added"], c - 1)
                for i in range(TC):
                    t = c * TC + i
                    mm = nc.tensor.matmul(bank(6 + c % 2)[:, i * D:(i + 1) * D], AOT[:, t * P:(t + 1) * P],
                                          WO1[:, :], start=True, stop=True)
                mm.then_inc(s["out_ready"], 1)

        def softmax_vector(vec, s):
            norm_vector(vec, s)
            nc.vector.memset(arena[64:P, :], 0.0).then_inc(s["pads_done"], 1)
            vec.wait_ge(s["pads_done"], 1)
            nc.vector.memset(KS[KPAD:KPAD + 2, :], 1.0).then_inc(s["pads_done"], 1)
            nc.vector.memset(VCUR[:, :], 0.0).then_inc(s["pads_done"], 1)
            vec.wait_ge(s["pads_done"], 3)
            nc.vector.memset(VCUR[:, :].rearrange("p (a c) -> p a c", c=32)[:, :, HD:HD + 1], 1.0).then_inc(s["pads_done"], 1)
            for i, side in enumerate((1, 0)):
                for c in range(NC):
                    n = i * NC + c
                    full = FULL[:, (n % 2) * BANK:(n % 2 + 1) * BANK]
                    parts = PARTS[side].rearrange("p (a n) -> p a n", a=3)[:, :, c * BANK:(c + 1) * BANK]
                    vec.wait_ge(s["part1"], n + 1)
                    nc.vector.tensor_tensor(full, full, parts[:, 0, :], ALU.subtract).then_inc(s["rest1"], 1)
                    vec.wait_ge(s["rest1"], n + 1)
                    nc.vector.tensor_copy(parts[:, 1, :], full).then_inc(s["part2"], 1)
                    vec.wait_ge(s["part2"], n + 1)
                    nc.vector.tensor_tensor(parts[:, 2, :], full, parts[:, 1, :], ALU.subtract).then_inc(s["part3"], 1)

            def read_max(u, slot):
                if slot == 0 and not (isinstance(u, int) and u == 0):
                    vec.wait_ge(s["max_ready"], u)
                vec.wait_ge(s["max_raw"], u * SLOTS + (slot + 1))
                nc.vector.tensor_reduce(halves[:, slot:slot + 1], bank(3 + 2 * (slot % 2), 2), AX.X,
                                        ALU.max).then_inc(s["max_read"], 1)

            def join_halves(u):
                vec.wait_ge(s["max_read"], (u + 1) * SLOTS)
                nc.vector.tensor_reduce(minus_max[:, :], halves[:, :].rearrange("p (m h) -> p m h", h=2), AX.X,
                                        ALU.max, negate=True).then_inc(s["max_ready"], 1)

            def split_shift(u):
                vec.wait_ge(s["max_turned"], u + 1)
                vec.wait_ge(s["shift_in"], u * 32)
                nc.vector.tensor_copy(shift_parts[:, 0:P], bank(3)[0:GH * TC, 0:P]).then_inc(s["rest1"], 1)
                vec.wait_ge(s["rest1"], 2 * NC + u + 1)
                nc.vector.tensor_tensor(shift_parts[:, P:2 * P], bank(3)[0:GH * TC, 0:P], shift_parts[:, 0:P],
                                        ALU.subtract).then_inc(s["shift_split"], 1)

            def unit(n, maxima, next_maxima):
                for kt in range(KEY_TILES):
                    slot = AHEAD + 2 * kt
                    if kt == KEY_TILES - 2 and maxima:
                        split_shift(n + 1)
                    if slot < SLOTS:
                        if maxima:
                            read_max(n + 1, slot)
                            read_max(n + 1, slot + 1)
                    elif next_maxima:
                        read_max(n + 2, slot - SLOTS)
                        read_max(n + 2, slot + 1 - SLOTS)
                    if slot + 2 == SLOTS and maxima:
                        join_halves(n + 1)

            for slot in range(SLOTS):
                read_max(0, slot)
            join_halves(0)
            for slot in range(AHEAD):
                if slot == 2:
                    split_shift(0)
                read_max(1, slot)
            with vec.Fori(0, UNITS - 2) as n:
                unit(n, True, True)
            unit(UNITS - 2, True, False)

            for c in range(NC):
                for g in range(H // GH):
                    n = c * GH + g
                    r = recips[:, (n % 2) * GH * TC:(n % 2 + 1) * GH * TC].rearrange("p (i j) -> p i j", i=TC)
                    turned = bank(g).rearrange("p (i j r) -> p i j r", i=TC, j=GH)
                    vec.wait_ge(s["o_turned"], n + 1)
                    nc.vector.reciprocal(r, turned[:, :, :, HD]).then_inc(s["o_recip"], 1)
                    vec.wait_ge(s["o_recip"], n + 1)
                    ao = AO[:, c * BANK:(c + 1) * BANK].rearrange("p (i g j d) -> p i g j d", i=TC, g=H // GH, j=GH)
                    nc.vector.tensor_tensor(ao[:, :, g, :, :], turned[:, :, :, 0:HD],
                                            r.unsqueeze(3).broadcast_to([P, TC, GH, HD]), ALU.mult).then_inc(s["o_scaled"], 1)
                if c == 0:
                    vec.wait_ge(s["bo_added"], T)
                if c >= 1:
                    add_chunk(vec, s, c - 1)
            add_chunk(vec, s, NC - 1)

        def add_chunk(vec, s, c):
            vec.wait_ge(s["out_ready"], c + 1)
            x_chunk = X[:, c * BANK:(c + 1) * BANK]
            nc.vector.tensor_tensor(x_chunk, bank(6 + c % 2), x_chunk, ALU.add).then_inc(s["added"], 1)

        def softmax_scalar(act, s):
            norm_scalar(act, s)
            for i, side in enumerate((1, 0)):
                for c in range(NC):
                    n = i * NC + c
                    full = FULL[:, (n % 2) * BANK:(n % 2 + 1) * BANK]
                    act.wait_ge(s["proj_raw"], n + 1)
                    if n >= 2:
                        act.wait_ge(s["part3"], n - 1)
                    nc.scalar.activation(full, bank(4 + n % 2), ACT.Identity,
                                         bias=QKV_BIAS[:, side:side + 1]).then_inc(s["proj_full"], 1)
                    act.wait_ge(s["proj_full"], n + 1)
                    nc.scalar.activation(PARTS[side][:, c * BANK:(c + 1) * BANK], full, ACT.Copy).then_inc(s["part1"], 1)
            for c in range(NC):
                act.wait_ge(s["v_raw"], c + 1)
                nc.scalar.activation(VALL[:, c * BANK:(c + 1) * BANK], bank(6 + c % 2),
                                     ACT.Copy).then_inc(s["v_all"] if c < NC - 1 else s["o_bank_free"], 1)

            def exponentials(n, i):
                act.wait_ge(s["score_ready"], n * STEPS + (i + 1))
                kt, j = i // GH, i % GH
                if j == 0 and kt >= RING // GH:
                    act.wait_ge(s["pv_done"], n * KEY_TILES + (kt - RING // GH + 1))
                slot = i % RING
                nc.scalar.activation(probs[:, slot * BANK:(slot + 1) * BANK], bank(i % 3), ACT.Exp,
                                     scale=SCALE).then_inc(s["exp_done"], 1)

            act.wait_ge(s["part3"], 2 * NC)
            with act.Fori(0, UNITS) as n:
                for i in range(STEPS):
                    exponentials(n, i)
                act.wait_ge(s["pv_done"], (n + 1) * KEY_TILES)
                nc.scalar.activation(osb[:, bass.ds(n * BANK, BANK)], bank(7), ACT.Copy).then_inc(s["o_bank_free"], 1)
            for c in range(NC):
                act.wait_ge(s["a_turned"], c + 1)
                nc.scalar.activation(AOT[:, c * BANK:(c + 1) * BANK], bank(4 + c % 2), ACT.Identity,
                                     bias=QKV_BIAS[:, 2:3]).then_inc(s["a_ready"], 1)

        def softmax_gpsimd(pool, s):
            v_heads = VALL[:, :].rearrange("p (t g h d) -> p t g h d", t=T, g=H // GH, h=GH)
            pool.wait_ge(s["v_all"], NC - 1)
            pool.wait_ge(s["o_bank_free"], 1)
            pool.wait_ge(s["pads_done"], 4)
            for n in range(2):
                nc.gpsimd.tensor_copy(vcur[:, n, :, :, 0:HD], v_heads[:, :, 0, :, :]).then_inc(s["v_cur"], 1)
            pool.wait_ge(normed, s["k"] * T + T)
            for t in range(T):
                x_tile = X[:, t * P:(t + 1) * P]
                nc.gpsimd.tensor_tensor(x_tile, x_tile, BO1[:, :], ALU.add).then_inc(s["bo_added"], 1)
            half = KEY_TILES * GH * 32
            with pool.Fori(0, UNITS - 2) as n:
                pool.wait_ge(s["pv_done"], (n + 1) * KEY_TILES)
                source = VALL[:, :].rearrange("p (t c) -> p t c", t=T)[:, :, bass.ds((((n + 2) >> 2) & 3) * (GH * HD), GH * HD)]
                source = source.rearrange("p t (h d) -> p t h d", h=GH)
                to = VCUR[:, bass.ds((n & 1) * half, half)].rearrange("p (t h c) -> p t h c", t=KEY_TILES, h=GH)
                nc.gpsimd.tensor_copy(to[:, :, :, 0:HD], source).then_inc(s["v_cur"], 1)

        def softmax_sync(sp, s):
            for i, (side, done) in enumerate(((1, s["parts_out_k"]), (0, s["parts_out_q"]))):
                sp.wait_ge(s["part1"], (i + 1) * NC)
                sp.wait_ge(s["part3"], (i + 1) * NC)
                for a in range(3):
                    sp.dma_start(parts_dram[side][:, a, :, :],
                                 PARTS[side][:, a * N:(a + 1) * N]).then_inc(done, 16)
            sp.wait_ge(s["parts_out_k"], 16 * 3)
            sp.wait_ge(s["parts_out_q"], 16 * 3)
            sp.wait_ge(s["pads_done"], 3)

            def load_group(g):
                if g >= 1:
                    sp.wait_ge(s["group_in"], g * (16 * 6 * GH))
                for j in range(GH):
                    head = parts_dram[0][g * GH + j].rearrange("a d (c n) -> (a d) c n", c=NC)
                    for i in range(3):
                        rows = slice(i * 3 * HD, (i + 1) * 3 * HD)
                        part = bass.AP(parts_dram[1].tensor, ((g * GH + j) * 3 + i) * HD * N,
                                       [[0, 3], [N, HD], [1, N]])
                        at = j * 2 * N + (g % 2) * N
                        sp.dma_start(KS[rows, at:at + N], part).then_inc(s["group_in"], 16)
                        to = QS[rows, :].rearrange("p (u h n) -> p u h n", h=GH, n=BANK)
                        sp.dma_start(to[:, (g % 2) * NC:(g % 2 + 1) * NC, j, :], head).then_inc(s["group_in"], 16)

            def put_shift(u, place):
                sp.wait_ge(s["shift_split"], u + 1)
                for part in range(2):
                    row = KPAD + part
                    sp.dma_start(QS[row:row + 1, bass.ds(place * (GH * BANK), GH * BANK)],
                                 shift_parts[:, part * P:(part + 1) * P]).then_inc(s["shift_in"], 16)

            load_group(0)
            load_group(1)
            with sp.Fori(0, 5) as u:
                put_shift(u, u)
            sp.wait_ge(s["pv_done"], 4 * KEY_TILES)
            load_group(2)
            with sp.Fori(5, 8) as u:
                put_shift(u, u)
            put_shift(8, 0)
            sp.wait_ge(s["pv_done"], 8 * KEY_TILES)
            load_group(3)
            with sp.Fori(9, UNITS) as u:
                put_shift(u, u - 8)

        tensor_of = {"top2": top2_tensor, "linear": linear_tensor, "top1": top1_tensor, "softmax": softmax_tensor}
        vector_of = {"top2": top2_vector, "linear": linear_vector, "top1": top1_vector, "softmax": softmax_vector}
        scalar_of = {"top2": top2_scalar, "linear": linear_scalar, "top1": top1_scalar, "softmax": softmax_scalar}

        block = ctx.enter_context(nc.Block())

        @block.sync
        def _(sp):
            x_rows = x_in.rearrange("a (t p) d -> p (a t) d", p=P)
            X3 = X[:, :].rearrange("p (t d) -> p t d", d=D)
            for c in range(NC):
                sp.dma_start(X3[:, c * TC:(c + 1) * TC, :], x_rows[:, c * TC:(c + 1) * TC, :]).then_inc(x_loaded[c], 16)
            sp.dma_start(WR0[:, :], wr0).then_inc(w_router, 16)
            sp.dma_start(WE0[:, :].rearrange("p (e f) -> p e f", e=E), we0.rearrange("e d f -> d e f")).then_inc(w_top2, 16)
            for i, w in enumerate((wq0, wk0, wv0)):
                sp.dma_start(WQKV0[:, i * D:(i + 1) * D], w).then_inc(w_linear, 16)
            sp.dma_start(WO0[:, :], wo0).then_inc(w_linear, 16)
            sp.dma_start(WR1[:, :], wr1).then_inc(w_top1, 16)
            sp.dma_start(BR1[:, :], br1.partition_broadcast(P)).then_inc(w_top1, 16)
            sp.dma_start(W1[:, :].rearrange("p (e h) -> p e h", e=E), w11.rearrange("e d h -> d e h")).then_inc(w_top1, 16)
            sp.dma_start(W2[:, :].rearrange("p (a d) -> p a d", d=D), w21.rearrange("e (c p) d -> p (e c) d", p=P)).then_inc(w_top1, 16)
            for i, w in enumerate((wq1, wk1, wv1)):
                sp.dma_start(WQKV1[:, i * D:(i + 1) * D], w).then_inc(w_softmax, 16)
            sp.dma_start(WO1[:, :], wo1).then_inc(w_softmax, 16)
            for i, b in enumerate((bq1, bk1, bv1)):
                sp.dma_start(QKV_BIAS[:, i:i + 1], b).then_inc(w_softmax, 16)
            sp.dma_start(BO1[:, :], bo1.partition_broadcast(P)).then_inc(w_softmax, 16)
            sp.wait_ge(consts_done, CONSTS)
            for j in range(NT):
                sp.dma_start(sorted_in[j * P:(j + 1) * P, :], zeros[:, :]).then_inc(zero_rows_done, 16)
            for s in S:
                if s["kind"] == "top1":
                    top1_sync(sp, s)
                if s["kind"] == "softmax":
                    softmax_sync(sp, s)
            out_rows = out.rearrange("a (t p) d -> p (a t) d", p=P)
            for c in range(NC):
                wait_x(sp, len(LAYERS), (c + 1) * TC - 1)
                sp.dma_start(out_rows[:, c * TC:(c + 1) * TC, :], X3[:, c * TC:(c + 1) * TC, :]).then_inc(out_stored, 16)
            sp.wait_ge(out_stored, 16 * NC)

        @block.gpsimd
        def _(pool):
            nc.gpsimd.memset(ident[:, :], 0.0).then_inc(consts_done, 1)
            nc.gpsimd.memset(upper[:, :], 1.0).then_inc(consts_done, 1)
            nc.gpsimd.memset(ones[:, :], 1.0).then_inc(consts_done, 1)
            nc.gpsimd.memset(block_diag[:, :], 1.0).then_inc(consts_done, 1)
            nc.gpsimd.memset(ones8[:, :], 1.0).then_inc(consts_done, 1)
            nc.gpsimd.memset(zeros[:, :], 0.0).then_inc(consts_done, 1)
            nc.gpsimd.memset(mask[:, T * E:], 0.0).then_inc(consts_done, 1)
            for e in range(E):
                nc.gpsimd.memset(desc[:, :].rearrange("p (t e) -> p t e", e=E)[:, :, e:e + 1],
                                 float(E - e)).then_inc(consts_done, 1)
            pool.wait_ge(consts_done, 15)
            nc.gpsimd.affine_select(out=ident[:, :], in_=ident[:, :], compare_op=ALU.not_equal, fill=1.0, base=0,
                                    pattern=[[-1, P]], channel_multiplier=1).then_inc(consts_done, 1)
            nc.gpsimd.affine_select(out=upper[:, :], in_=upper[:, :], compare_op=ALU.is_gt, fill=0.0, base=0,
                                    pattern=[[1, P]], channel_multiplier=-1).then_inc(consts_done, 1)
            blocks = block_diag[:, :].rearrange("p (h d) -> p h d", d=HD)
            nc.gpsimd.affine_select(out=blocks, in_=blocks, compare_op=ALU.is_ge, fill=0.0, base=0,
                                    pattern=[[-HD, H], [0, HD]], channel_multiplier=1).then_inc(consts_done, 1)
            pool.wait_ge(consts_done, 18)
            nc.gpsimd.affine_select(out=blocks, in_=blocks, compare_op=ALU.is_ge, fill=0.0, base=HD - 1,
                                    pattern=[[HD, H], [0, HD]], channel_multiplier=-1).then_inc(consts_done, 1)
            iota_a = route[:, 0:E * T].bitcast(I32)
            iota_b = plan_big[:, :].bitcast(I32)
            nc.gpsimd.iota(iota_a.rearrange("p (e j) -> p e j", e=E), [[0, E], [P, T]], base=0,
                           channel_multiplier=0).then_inc(consts_done, 1)
            nc.gpsimd.iota(iota_b.rearrange("p (j e) -> p j e", e=E), [[1, NT], [0, E]], base=0,
                           channel_multiplier=0).then_inc(consts_done, 1)
            pool.wait_ge(consts_done, 21)
            nc.gpsimd.tensor_copy(steps128[:, :], iota_a).then_inc(consts_done, 1)
            nc.gpsimd.tensor_copy(tile_no[:, :], iota_b).then_inc(consts_done, 1)
            for s in S:
                if s["kind"] == "top1":
                    top1_gpsimd(pool, s)
                if s["kind"] == "softmax":
                    softmax_gpsimd(pool, s)

        @block.tensor
        def _(pe):
            for s in S:
                tensor_of[s["kind"]](pe, s)

        @block.vector
        def _(vec):
            vec.wait_ge(consts_done, CONSTS)
            for s in S:
                vector_of[s["kind"]](vec, s)

        @block.scalar
        def _(act):
            for s in S:
                scalar_of[s["kind"]](act, s)


def kernel(L0_attn_x, L0_attn_Wq, L0_attn_Wk, L0_attn_Wv, L0_attn_Wo, L0_ffn_Wr, L0_ffn_We, L1_attn_Wq,
           L1_attn_bq, L1_attn_Wk, L1_attn_bk, L1_attn_Wv, L1_attn_bv, L1_attn_Wo, L1_attn_bo, L1_ffn_Wr,
           L1_ffn_br, L1_ffn_W1, L1_ffn_b1, L1_ffn_W2, L1_ffn_b2):
    import numpy as np
    import concourse.bacc as bacc
    from concourse.bass_utils import run_bass_kernel_spmd

    def a(x):
        return np.ascontiguousarray(x)

    def turned(x):
        return np.ascontiguousarray(np.asarray(x).T)

    def row(x):
        return np.ascontiguousarray(x).reshape(-1)

    def column(x):
        return np.ascontiguousarray(x).reshape(-1, 1)

    arrays = {
        "x_in": a(L0_attn_x),
        "wq0": turned(L0_attn_Wq), "wk0": turned(L0_attn_Wk), "wv0": turned(L0_attn_Wv), "wo0": turned(L0_attn_Wo),
        "wr0": turned(L0_ffn_Wr), "we0": a(L0_ffn_We),
        "wq1": turned(L1_attn_Wq), "bq1": column(L1_attn_bq), "wk1": turned(L1_attn_Wk), "bk1": column(L1_attn_bk),
        "wv1": turned(L1_attn_Wv), "bv1": column(L1_attn_bv), "wo1": turned(L1_attn_Wo), "bo1": row(L1_attn_bo),
        "wr1": a(L1_ffn_Wr), "br1": row(L1_ffn_br), "w11": a(L1_ffn_W1), "b11": row(L1_ffn_b1),
        "w21": a(L1_ffn_W2), "b21": row(L1_ffn_b2),
    }
    nc = bacc.Bacc("TRN2", target_bir_lowering=False, num_devices=1)
    args = [nc.dram_tensor(name, v.shape, mybir.dt.from_np(v.dtype), kind="ExternalInput").ap()
            for name, v in arrays.items()]
    out = nc.dram_tensor("out", (1, N, D), F32, kind="ExternalOutput").ap()
    macaron(nc, *args, out)
    r = run_bass_kernel_spmd(nc, [arrays], core_ids=[0])
    return r.results[0]["out"]
```

```python
from contextlib import ExitStack

import concourse.bass as bass
from concourse import mybir

F32 = mybir.dt.float32
BF16 = mybir.dt.bfloat16
I32 = mybir.dt.int32
U32 = mybir.dt.uint32
ALU = mybir.AluOpType
ACT = mybir.ActivationFunctionType
AX = mybir.AxisListType

P = 128
D = 128
N = 2048
T = N // P
BANK = 512
NC = N // BANK
TC = BANK // P
EPS = 1e-5
E = 8
CAP = int(N * 2 / E * 1.5) + 1
BIG = 3.0e38
LA_EPS = 1e-6
H = 16
HD = D // H
HID = 512
HC = HID // P
NT = N // P + E
SCALE = float(HD) ** -0.5

LAYERS = ["top2", "linear", "top2", "top1", "softmax", "top1"]

GH = 4
UNITS = (H // GH) * NC
TERMS = 9
KROWS = TERMS * HD
KFULL = KROWS + 2
PAD_FROM = KROWS // 32 * 32
KEY_TILES = N // P
STEPS = KEY_TILES * GH
RING = 8
SLOTS = GH * TC * 2
AHEAD = 8


def macaron(nc, x_in, wq0, wk0, wv0, wo0, wr0, we0, wq1, bq1, wk1, bk1, wv1, bv1, wo1, bo1,
            wr1, br1, w11, b11, w21, b21, out):
    with ExitStack() as ctx:
        def sb(name, shape, dt=F32):
            return ctx.enter_context(nc.sbuf_tensor(name, shape, dt))

        def sem(name):
            return ctx.enter_context(nc.semaphore(name))

        X = sb("X", [P, N])
        XN = sb("XN", [P, N])
        XT = sb("XT", [P, N])
        WQKV0 = sb("WQKV0", [P, 3 * D])
        WO0 = sb("WO0", [P, D])
        WR0 = sb("WR0", [P, E])
        WE0 = sb("WE0", [P, E * D])
        WQKV1 = sb("WQKV1", [P, 3 * D])
        WO1 = sb("WO1", [P, D])
        QKV_BIAS = sb("QKV_BIAS", [P, 3])
        BO1 = sb("BO1", [P, D])
        WR1 = sb("WR1", [P, E])
        BR1 = sb("BR1", [P, E])
        W1 = sb("W1", [P, E * HID])
        W2 = sb("W2", [P, E * HC * D])
        B1 = sb("B1", [P, E * HC])
        ident = sb("ident", [P, P])
        upper = sb("upper", [P, P], BF16)
        ones = sb("ones", [P, P], BF16)
        desc = sb("desc", [P, T * E])
        block_diag = sb("block_diag", [P, D])
        steps128 = sb("steps128", [P, E * T])
        tile_no = sb("tile_no", [P, NT * E])
        ones8 = sb("ones8", [P, E])
        zeros = sb("zeros", [P, D])
        stats = sb("stats", [P, T * 6])
        small = sb("small", [P, 12 * T])
        route = sb("route", [P, 7 * T * E])
        mask = sb("mask", [P, (T + 1) * E], BF16)
        gate = sb("gate", [P, T * E])
        dest = sb("dest", [P, T], U32)
        tile_expert = sb("tile_expert", [P, NT], I32)
        plan = sb("plan", [P, 8 * E])
        plan_big = sb("plan_big", [P, NT * E])
        arena = sb("arena", [P, 16384])
        probs = sb("probs", [P, RING * BANK])
        osb = sb("osb", [P, UNITS * BANK])
        VCUR = sb("VCUR", [P, 2 * KEY_TILES * GH * 32])
        VALL = XN

        psum = ctx.enter_context(nc.psum_tensor("psum", [P, 8 * BANK], F32))

        def bank(b, n=1):
            return psum[:, b * BANK:(b + n) * BANK]

        sorted_in = nc.dram_tensor("sorted_in", [NT * P, D], F32, kind="Internal").ap()
        sorted_out = nc.dram_tensor("sorted_out", [NT * P, D], F32, kind="Internal").ap()
        parts_dram = [nc.dram_tensor(f"{side}_parts", [3, D, N], BF16, kind="Internal").ap()
                      for side in ("q", "k")]

        def col(i, n=T):
            return small[:, i * T:i * T + n]

        def te(i):
            return route[:, i * T * E:(i + 1) * T * E].rearrange("p (t e) -> p t e", e=E)

        def over_experts(ap, m=T):
            return ap.unsqueeze(2).broadcast_to([P, m, E])

        x_loaded = [sem(f"x_loaded{c}") for c in range(NC)]
        consts_done = sem("consts_done")
        w_router = sem("w_router")
        w_top2 = sem("w_top2")
        w_linear = sem("w_linear")
        w_top1 = sem("w_top1")
        w_softmax = sem("w_softmax")
        zero_rows_done = sem("zero_rows_done")
        out_stored = sem("out_stored")
        CONSTS = 23

        stats_done, moments, var_ready, std_ready, normed, turned, xt_ready = (
            sem(n) for n in ("stats_done", "moments", "var_ready", "std_ready", "normed", "turned", "xt_ready"))
        MOMENTS = 7

        def layer_sems(k, kind):
            names = []
            if kind in ("top2", "top1"):
                names += ["logits_ready", "routing", "mask_ready", "ranks_ready", "gate_ready"]
            if kind == "top2":
                names += ["gap_ready", "gap_exp", "y_ready", "added"]
            if kind == "linear":
                names += ["q_raw", "q_neg", "q_exp", "q_done", "kv_raw", "k_neg", "k_exp", "k_done",
                          "v_done", "kv_sum", "kv_blocks", "num_ready", "den_free", "norm_chain",
                          "o_ready", "out_ready", "added"]
            if kind == "top1":
                names += ["rows_scattered", "bias_in", "t1_done", "xs_ready", "w1_ready", "h_done",
                          "bias_done", "gelu_done", "y_done", "y_ready", "added"]
                names += [f"rows_gathered{c}" for c in range(NC)]
                names += [f"xs_in{u}" for u in range(4)] + [f"ys_out{u}" for u in range(4)]
            if kind == "softmax":
                names += ["proj_raw", "part1", "rest1", "part2", "part3", "parts_out",
                          "first_head_in0", "first_head_in1", "first_head_in2", "first_head_in3", "v_raw", "v_all", "pads_done", "group_in", "v_cur", "o_bank_free", "max_raw",
                          "max_read", "max_ready", "max_turned", "shift_split", "shift_in", "score_ready",
                          "exp_done", "pv_done", "o_turned", "o_recip", "o_scaled", "a_turned",
                          "a_ready", "out_ready", "bo_added", "added"]
            return {"k": k, "kind": kind} | {n: sem(f"L{k}_{n}") for n in names}

        S = [layer_sems(k, kind) for k, kind in enumerate(LAYERS)]

        def wait_x(eng, k, t):
            if k == 0:
                eng.wait_ge(x_loaded[t // TC], 16)
            elif S[k - 1]["kind"] == "top2":
                eng.wait_ge(S[k - 1]["added"], 32 * (t // 4) + (16 if t % 4 < 2 else 32))
            elif S[k - 1]["kind"] == "top1":
                eng.wait_ge(S[k - 1]["added"], t + 1)
            else:
                eng.wait_ge(S[k - 1]["added"], t // TC + 1)

        def norm_vector(vec, s):
            st = stats[:, :].rearrange("p (t s) -> p t s", s=6)
            mean_even, m2_even, mean_odd, m2_odd = st[:, :, 1], st[:, :, 2], st[:, :, 4], st[:, :, 5]
            mean_sum, mean_dif, m2, mean, dif2, dvar, var, std, rstd = (col(i) for i in range(9))
            for t in range(T):
                wait_x(vec, s["k"], t)
                nc.vector.bn_stats(st[:, t, :], X[:, t * P:(t + 1) * P]).then_inc(stats_done, 1)
            vec.wait_ge(stats_done, s["k"] * T + T)
            nc.vector.tensor_tensor(mean_sum, mean_even, mean_odd, ALU.add).then_inc(moments, 1)
            nc.vector.tensor_tensor(mean_dif, mean_even, mean_odd, ALU.subtract).then_inc(moments, 1)
            nc.vector.tensor_tensor(m2, m2_even, m2_odd, ALU.add).then_inc(moments, 1)
            vec.wait_ge(moments, s["k"] * MOMENTS + 2)
            nc.vector.tensor_tensor(dif2, mean_dif, mean_dif, ALU.mult).then_inc(moments, 1)
            nc.vector.tensor_scalar(mean, mean_sum, 0.5, None, ALU.mult).then_inc(moments, 1)
            vec.wait_ge(moments, s["k"] * MOMENTS + 4)
            nc.vector.scalar_tensor_tensor(out=dvar, in0=dif2, scalar=D / 4, in1=m2, op0=ALU.mult,
                                           op1=ALU.add).then_inc(moments, 1)
            vec.wait_ge(moments, s["k"] * MOMENTS + 6)
            nc.vector.tensor_scalar(var, dvar, 1.0 / D, EPS, ALU.mult, ALU.add).then_inc(var_ready, 1)
            vec.wait_ge(std_ready, s["k"] + 1)
            nc.vector.reciprocal(rstd, std).then_inc(moments, 1)
            vec.wait_ge(moments, s["k"] * MOMENTS + 7)
            for t in range(T):
                nc.vector.tensor_scalar(XN[:, t * P:(t + 1) * P], X[:, t * P:(t + 1) * P], mean[:, t:t + 1],
                                        rstd[:, t:t + 1], ALU.subtract, ALU.mult).then_inc(normed, 1)

        def norm_scalar(act, s):
            act.wait_ge(var_ready, s["k"] + 1)
            nc.scalar.activation(col(7), col(6), ACT.Sqrt).then_inc(std_ready, 1)
            for c in range(NC):
                act.wait_ge(turned, s["k"] * NC + c + 1)
                nc.scalar.activation(XT[:, c * BANK:(c + 1) * BANK], bank(c), ACT.Copy).then_inc(xt_ready, 1)

        def norm_tensor(pe, s):
            pe.wait_ge(consts_done, CONSTS)
            for c in range(NC):
                pe.wait_ge(normed, s["k"] * T + TC * (c + 1))
                for i in range(TC):
                    t = c * TC + i
                    mm = nc.tensor.transpose(psum[:, t * P:(t + 1) * P], XN[:, t * P:(t + 1) * P], ident[:, :])
                mm.then_inc(turned, 1)

        LG = bank(6)[:, 0:T * E]
        RANK = bank(7)[:, 0:(T + 1) * E]

        def logits_tensor(pe, s, w):
            if w is WR0:
                pe.wait_ge(w_router, 16)
            else:
                pe.wait_ge(w_top1, 16 * 5)
            for t in range(T):
                pe.wait_ge(xt_ready, s["k"] * NC + t // TC + 1)
                mm = nc.tensor.matmul(LG[:, t * E:(t + 1) * E], XT[:, t * P:(t + 1) * P], w[:, :],
                                      start=True, stop=True)
            mm.then_inc(s["logits_ready"], 1)

        def ranks_tensor(pe, s):
            pe.wait_ge(s["mask_ready"], 1)
            nc.tensor.matmul(RANK, upper[:, :], mask[:, :], start=True, stop=False)
            for d in range(1, T + 1):
                mm = nc.tensor.matmul(RANK[:, d * E:], ones[:, :], mask[:, 0:(T + 1 - d) * E],
                                      start=False, stop=(d == T))
            mm.then_inc(s["ranks_ready"], 1)

        def pick(vec, s, n, logits, largest, one_hot, work, work_max):
            nc.vector.tensor_reduce(largest, logits, AX.X, ALU.max).then_inc(s["routing"], 1)
            vec.wait_ge(s["routing"], n + 1)
            nc.vector.tensor_tensor(work, logits, over_experts(largest), ALU.is_equal).then_inc(s["routing"], 1)
            vec.wait_ge(s["routing"], n + 2)
            nc.vector.tensor_tensor(work, work, desc[:, :].rearrange("p (t e) -> p t e", e=E),
                                    ALU.mult).then_inc(s["routing"], 1)
            vec.wait_ge(s["routing"], n + 3)
            nc.vector.tensor_reduce(work_max, work, AX.X, ALU.max).then_inc(s["routing"], 1)
            vec.wait_ge(s["routing"], n + 4)
            nc.vector.tensor_tensor(one_hot, work, over_experts(work_max), ALU.is_equal).then_inc(s["routing"], 1)
            vec.wait_ge(s["routing"], n + 5)
            return n + 5

        def top2_tensor(pe, s):
            norm_tensor(pe, s)
            logits_tensor(pe, s, WR0)
            pe.wait_ge(w_top2, 16)

            def experts(t):
                u = t % 4
                if t >= 4:
                    pe.wait_ge(s["added"], 32 * (t // 4 - 1) + (16 if u < 2 else 32))
                for half in range(2):
                    mm = nc.tensor.matmul(bank(2 * u + half), XT[:, t * P:(t + 1) * P],
                                          WE0[:, half * BANK:(half + 1) * BANK], start=True, stop=True)
                mm.then_inc(s["y_ready"], 1)

            pe.wait_ge(xt_ready, s["k"] * NC + NC)
            for t in range(2):
                experts(t)
            ranks_tensor(pe, s)
            experts(2)
            pe.wait_ge(s["gate_ready"], 1)
            for t in range(3, T):
                experts(t)

        def top2_vector(vec, s):
            norm_vector(vec, s)
            L, L2, first, second, work, g1, g2 = (te(i) for i in range(7))
            top, top2, work_max, gap, gap_e, total, w_first, w_second = (col(i) for i in range(8))
            vec.wait_ge(s["logits_ready"], 1)
            nc.vector.tensor_copy(route[:, 0:T * E], LG).then_inc(s["routing"], 1)
            vec.wait_ge(s["routing"], 1)
            n = pick(vec, s, 1, L, top, first, work, work_max)
            nc.vector.scalar_tensor_tensor(out=L2, in0=first, scalar=-BIG, in1=L, op0=ALU.mult,
                                           op1=ALU.add).then_inc(s["routing"], 1)
            n += 1
            vec.wait_ge(s["routing"], n)
            n = pick(vec, s, n, L2, top2, second, work, work_max)
            nc.vector.tensor_tensor(mask[:, 0:T * E].rearrange("p (t e) -> p t e", e=E), first, second,
                                    ALU.add).then_inc(s["mask_ready"], 1)
            nc.vector.tensor_tensor(gap, top2, top, ALU.subtract).then_inc(s["gap_ready"], 1)
            vec.wait_ge(s["gap_exp"], 1)
            nc.vector.tensor_scalar(total, gap_e, 1.0, 2.0, ALU.add, ALU.mult).then_inc(s["routing"], 1)
            vec.wait_ge(s["routing"], n + 1)
            nc.vector.reciprocal(w_first, total).then_inc(s["routing"], 1)
            vec.wait_ge(s["routing"], n + 2)
            nc.vector.tensor_tensor(w_second, w_first, gap_e, ALU.mult).then_inc(s["routing"], 1)
            nc.vector.tensor_tensor(g1, first, over_experts(w_first), ALU.mult).then_inc(s["routing"], 1)
            vec.wait_ge(s["routing"], n + 3)
            nc.vector.tensor_tensor(g2, second, over_experts(w_second), ALU.mult).then_inc(s["routing"], 1)
            vec.wait_ge(s["routing"], n + 5)
            nc.vector.tensor_tensor(g1, g1, g2, ALU.add).then_inc(s["routing"], 1)
            vec.wait_ge(s["routing"], n + 6)
            vec.wait_ge(s["ranks_ready"], 1)
            nc.vector.scalar_tensor_tensor(out=gate[:, :], in0=RANK[:, 0:T * E], scalar=float(CAP),
                                           in1=route[:, 5 * T * E:6 * T * E], op0=ALU.is_lt,
                                           op1=ALU.mult).then_inc(s["gate_ready"], 1)
            vec.wait_ge(s["gate_ready"], 1)
            with vec.Fori(0, T // 4) as i:
                for first_of_pair in (0, 2):
                    for e in range(E):
                        for u in (first_of_pair, first_of_pair + 1):
                            step = first_of_pair * E + 2 * e + u - first_of_pair
                            if e == 0:
                                vec.wait_ge(s["y_ready"], i * 4 + (u + 1))
                            else:
                                vec.wait_ge(s["added"], i * 32 + (step - 1))
                            x_tile = X[:, bass.ds(i * (4 * P) + u * P, P)]
                            nc.vector.scalar_tensor_tensor(
                                out=x_tile, in0=psum[:, (2 * u) * BANK + e * D:(2 * u) * BANK + (e + 1) * D],
                                scalar=gate[:, bass.ds(i * (4 * E) + (u * E + e), 1)], in1=x_tile,
                                op0=ALU.mult, op1=ALU.add).then_inc(s["added"], 1)

        def top2_scalar(act, s):
            norm_scalar(act, s)
            act.wait_ge(s["gap_ready"], 1)
            nc.scalar.activation(col(4), col(3), ACT.Exp).then_inc(s["gap_exp"], 1)

        QF = arena[:, 0:N]
        KF = arena[:, N:2 * N]
        VF = arena[:, 2 * N:2 * N + T * (D + 1)].rearrange("p (t d) -> p t d", d=D + 1)
        la = 3 * N + 64
        QNEG = arena[:, la:la + 2 * BANK]
        KNEG = arena[:, la + 2 * BANK:la + 4 * BANK]
        KV = arena[:, la + 4 * BANK:la + 4 * BANK + D]
        KSUM = arena[:, la + 4 * BANK + D:la + 4 * BANK + 2 * D]
        RDEN = arena[:, la + 5 * BANK:la + 7 * BANK]
        ON = arena[:, la + 7 * BANK:la + 9 * BANK]

        def linear_tensor(pe, s):
            norm_tensor(pe, s)
            pe.wait_ge(w_linear, 16 * 4)
            for c in range(NC):
                pe.wait_ge(xt_ready, s["k"] * NC + c + 1)
                if c >= 2:
                    pe.wait_ge(s["q_done"], c - 1)
                nc.tensor.matmul(bank(4 + c % 2), WQKV0[:, 0:D], XT[:, c * BANK:(c + 1) * BANK],
                                 start=True, stop=True).then_inc(s["q_raw"], 1)
                for pair in range(2):
                    n = 2 * c + pair
                    if n >= 2:
                        pe.wait_ge(s["k_done"], n - 1)
                        pe.wait_ge(s["v_done"], n - 1)
                    for i in range(2):
                        t = 2 * n + i
                        mm = nc.tensor.matmul(bank(6 + n % 2)[:, i * 2 * D:(i + 1) * 2 * D],
                                              XT[:, t * P:(t + 1) * P], WQKV0[:, D:3 * D],
                                              start=True, stop=True)
                    mm.then_inc(s["kv_raw"], 1)
            for t in range(T):
                if t % 2 == 0:
                    pe.wait_ge(s["k_done"], t // 2 + 1)
                    pe.wait_ge(s["v_done"], t // 2 + 1)
                mm = nc.tensor.matmul(bank(0)[:, 0:D + 1], KF[:, t * P:(t + 1) * P], VF[:, t, :],
                                      start=(t == 0), stop=(t == T - 1))
            mm.then_inc(s["kv_sum"], 1)

            def project(c):
                pe.wait_ge(s["o_ready"], c + 1)
                if c >= 2:
                    pe.wait_ge(s["added"], c - 1)
                for i in range(TC):
                    mm = nc.tensor.matmul(bank(5 + c % 2)[:, i * D:(i + 1) * D],
                                          ON[:, (c % 2) * BANK + i * P:(c % 2) * BANK + (i + 1) * P],
                                          WO0[:, :], start=True, stop=True)
                mm.then_inc(s["out_ready"], 1)

            pe.wait_ge(s["kv_blocks"], 2)
            pe.wait_ge(s["q_done"], NC)
            for c in range(NC):
                if c >= 2:
                    pe.wait_ge(s["o_ready"], c - 1)
                q = QF[:, c * BANK:(c + 1) * BANK]
                nc.tensor.matmul(bank(2 + 2 * (c % 2)), KSUM, q, start=True, stop=True)
                nc.tensor.matmul(bank(1 + 2 * (c % 2)), KV, q, start=True, stop=True).then_inc(s["num_ready"], 1)
                if c >= 1:
                    project(c - 1)
            project(NC - 1)

        def linear_vector(vec, s):
            norm_vector(vec, s)
            nc.vector.memset(VF[:, :, D:D + 1], 1.0).then_inc(s["k_neg"], 1)
            for c in range(NC):
                qn = QNEG[:, (c % 2) * BANK:(c % 2 + 1) * BANK]
                vec.wait_ge(s["q_raw"], c + 1)
                nc.vector.tensor_scalar(qn, bank(4 + c % 2), 0.0, None, ALU.min).then_inc(s["q_neg"], 1)

                def k_raw(n):
                    return bank(6 + n % 2).rearrange("p (i x) -> p i x", i=2)[:, :, 0:D]

                def k_neg(n):
                    return KNEG[:, (n % 2) * BANK:(n % 2) * BANK + 2 * D].rearrange("p (i x) -> p i x", i=2)

                for n in (2 * c, 2 * c + 1):
                    vec.wait_ge(s["kv_raw"], n + 1)
                    nc.vector.tensor_scalar(k_neg(n), k_raw(n), 0.0, None, ALU.min).then_inc(s["k_neg"], 1)
                vec.wait_ge(s["q_exp"], c + 1)
                nc.vector.scalar_tensor_tensor(out=QF[:, c * BANK:(c + 1) * BANK], in0=bank(4 + c % 2), scalar=0.0,
                                               in1=qn, op0=ALU.max, op1=ALU.add).then_inc(s["q_done"], 1)
                for n in (2 * c, 2 * c + 1):
                    vec.wait_ge(s["k_exp"], n + 1)
                    vec.wait_ge(s["v_done"], n + 1)
                    nc.vector.scalar_tensor_tensor(
                        out=KF[:, n * 2 * P:(n + 1) * 2 * P].rearrange("p (i x) -> p i x", i=2), in0=k_raw(n),
                        scalar=0.0, in1=k_neg(n), op0=ALU.max, op1=ALU.add).then_inc(s["k_done"], 1)
            vec.wait_ge(s["kv_sum"], 1)
            vec.wait_ge(consts_done, CONSTS)
            nc.vector.tensor_tensor(KV, bank(0)[:, 0:D], block_diag[:, :], ALU.mult).then_inc(s["kv_blocks"], 1)
            nc.vector.tensor_scalar(KSUM, block_diag[:, :], bank(0)[:, D:D + 1], None,
                                    ALU.mult).then_inc(s["kv_blocks"], 1)
            for c in range(NC + 1):
                if c < NC:
                    rden = RDEN[:, (c % 2) * BANK:(c % 2 + 1) * BANK]
                    vec.wait_ge(s["num_ready"], c + 1)
                    nc.vector.tensor_scalar(rden, bank(2 + 2 * (c % 2)), LA_EPS, None,
                                            ALU.add).then_inc(s["norm_chain"], 1)
                    vec.wait_ge(s["norm_chain"], 2 * c + 1)
                    nc.vector.reciprocal(rden, rden).then_inc(s["norm_chain"], 1)
                    vec.wait_ge(s["norm_chain"], 2 * c + 2)
                    if c >= 2:
                        vec.wait_ge(s["out_ready"], c - 1)
                    nc.vector.tensor_tensor(ON[:, (c % 2) * BANK:(c % 2 + 1) * BANK], bank(1 + 2 * (c % 2)), rden,
                                            ALU.mult).then_inc(s["o_ready"], 1)
                if c >= 1:
                    b = c - 1
                    vec.wait_ge(s["out_ready"], b + 1)
                    x_chunk = X[:, b * BANK:(b + 1) * BANK]
                    nc.vector.tensor_tensor(x_chunk, bank(5 + b % 2), x_chunk, ALU.add).then_inc(s["added"], 1)

        def linear_scalar(act, s):
            norm_scalar(act, s)
            for c in range(NC):
                qn = QNEG[:, (c % 2) * BANK:(c % 2 + 1) * BANK]
                act.wait_ge(s["q_neg"], c + 1)
                nc.scalar.activation(qn, qn, ACT.Exp).then_inc(s["q_exp"], 1)
                for n in (2 * c, 2 * c + 1):
                    kn = KNEG[:, (n % 2) * BANK:(n % 2) * BANK + 2 * D]
                    act.wait_ge(s["k_neg"], n + 2)
                    nc.scalar.activation(kn, kn, ACT.Exp).then_inc(s["k_exp"], 1)
                    nc.scalar.activation(VF[:, 2 * n:2 * n + 2, 0:D],
                                         bank(6 + n % 2).rearrange("p (i x) -> p i x", i=2)[:, :, D:2 * D],
                                         ACT.Copy).then_inc(s["v_done"], 1)

        B2 = arena[:, 0:E * D]
        o = E * D
        XS_IN = [arena[:, o + u * P:o + (u + 1) * P] for u in range(4)]
        o += 4 * P
        XS = [arena[:, o + u * P:o + (u + 1) * P] for u in range(2)]
        o += 2 * P
        YS = [arena[:, o + u * D:o + (u + 1) * D] for u in range(4)]
        HB = [probs[:, u * HID:(u + 1) * HID] for u in range(2)]
        HG = [probs[:, (2 + u) * HID:(3 + u) * HID] for u in range(2)]
        W1S = [probs[:, (4 + u) * HID:(5 + u) * HID] for u in range(2)]
        YG = XT

        def sorted_steps(eng, step):
            for j in range(6):
                step(j, j % 4, True, j)
            with eng.Fori(0, (NT - 8) // 4) as i:
                for j in range(6, 10):
                    step(i * 4 + j, j % 4, False, None)
            for j in range(NT - 2, NT + 1):
                step(j, j % 4, True, j)

        def expert_of(eng, j):
            where = tile_expert[0:1, j:j + 1] if isinstance(j, int) else tile_expert[0:1, bass.ds(j, 1)]
            return eng.value_load(where, min_val=0, max_val=E - 1)

        def top1_tensor(pe, s):
            norm_tensor(pe, s)
            logits_tensor(pe, s, WR1)
            ranks_tensor(pe, s)
            pe.wait_ge(s["gate_ready"], 2)
            pe.wait_ge(w_top1, 16 * 5)

            def step(j, u, static, at):
                def exists(lag):
                    return not static or 0 <= at - lag < NT

                def back(lag):
                    return not static or at - lag >= 0
                if exists(0):
                    pe.wait_ge(s["xs_ready"], j + 1)
                    pe.wait_ge(s["w1_ready"], j + 1)
                    if back(2):
                        pe.wait_ge(s["bias_done"], j - 1)
                    for c in range(HC):
                        mm = nc.tensor.matmul(bank(2 + u % 2)[:, c * P:(c + 1) * P], W1S[u % 2][:, c * P:(c + 1) * P],
                                              XS[u % 2], start=True, stop=True)
                    mm.then_inc(s["h_done"], 1)
                if exists(-1):
                    v = (u + 1) % 4
                    xs_in = (s["xs_in0"], s["xs_in1"], s["xs_in2"], s["xs_in3"])[v]
                    pe.wait_ge(xs_in, 4 * (j + 1 - v) + 16)
                    if back(1):
                        pe.wait_ge(s["xs_ready"], j)
                    nc.tensor.transpose(bank(v % 2)[:, 0:P], XS_IN[v], ident[:, :]).then_inc(s["t1_done"], 1)
                if exists(1):
                    v = (u + 3) % 4
                    e = expert_of(pe, j - 1)
                    pe.wait_ge(s["gelu_done"], j)
                    if back(3):
                        pe.wait_ge(s["y_ready"], j - 2)
                    for c in range(HC):
                        mm = nc.tensor.matmul(bank(6 + v % 2)[:, 0:D], HG[v % 2][:, c * P:(c + 1) * P],
                                              W2[:, bass.ds(e * HID + c * D, D)], start=(c == 0),
                                              stop=(c == HC - 1))
                    mm.then_inc(s["y_done"], 1)

            pe.wait_ge(s["xs_in0"], 16)
            nc.tensor.transpose(bank(0)[:, 0:P], XS_IN[0], ident[:, :]).then_inc(s["t1_done"], 1)
            sorted_steps(pe, step)

        def top1_vector(vec, s):
            norm_vector(vec, s)
            L, first, work, ranked = te(0), te(2), te(4), te(5)
            top, work_max, slot = col(0), col(2), col(3)
            vec.wait_ge(s["logits_ready"], 1)
            vec.wait_ge(w_top1, 16 * 5)
            nc.vector.tensor_tensor(L, LG.rearrange("p (t e) -> p t e", e=E),
                                    BR1[:, :].unsqueeze(1).broadcast_to([P, T, E]), ALU.add).then_inc(s["routing"], 1)
            vec.wait_ge(s["routing"], 1)
            n = pick(vec, s, 1, L, top, first, work, work_max)
            nc.vector.tensor_copy(mask[:, 0:T * E].rearrange("p (t e) -> p t e", e=E), first).then_inc(s["mask_ready"], 1)
            counts, tiles, tiles_to, slot0 = (plan[:, i * E:(i + 1) * E] for i in range(4))
            vec.wait_ge(s["ranks_ready"], 1)
            nc.vector.tensor_copy(counts, RANK[:, T * E:(T + 1) * E]).then_inc(s["routing"], 1)
            vec.wait_ge(s["routing"], n + 1)
            full = te(6).rearrange("p t e -> p (t e)").rearrange("p (e j) -> p e j", e=E)
            nc.vector.tensor_tensor(full, counts.unsqueeze(2).broadcast_to([P, E, T]),
                                    steps128[:, :].rearrange("p (e j) -> p e j", e=E), ALU.is_gt).then_inc(s["routing"], 1)
            vec.wait_ge(s["routing"], n + 2)
            nc.vector.tensor_reduce(tiles, full, AX.X, ALU.add).then_inc(s["routing"], 1)
            vec.wait_ge(s["routing"], n + 3)
            nc.vector.tensor_tensor_scan(tiles_to, ones8[:, :], tiles, 0.0, ALU.mult, ALU.add).then_inc(s["routing"], 1)
            vec.wait_ge(s["routing"], n + 4)
            nc.vector.tensor_tensor(slot0, tiles_to, tiles, ALU.subtract).then_inc(s["routing"], 1)
            vec.wait_ge(s["routing"], n + 5)
            nc.vector.scalar_tensor_tensor(out=ranked, in0=slot0.unsqueeze(1).broadcast_to([P, T, E]),
                                           scalar=float(P), in1=RANK[:, 0:T * E].rearrange("p (t e) -> p t e", e=E),
                                           op0=ALU.mult, op1=ALU.add).then_inc(s["routing"], 1)
            vec.wait_ge(s["routing"], n + 6)
            nc.vector.tensor_tensor(ranked, ranked, first, ALU.mult).then_inc(s["routing"], 1)
            vec.wait_ge(s["routing"], n + 7)
            nc.vector.tensor_reduce(slot, ranked, AX.X, ALU.add).then_inc(s["routing"], 1)
            vec.wait_ge(s["routing"], n + 8)
            nc.vector.tensor_copy(dest[:, :], slot).then_inc(s["gate_ready"], 1)
            before = plan_big[:, :].rearrange("p (j e) -> p j e", e=E)
            nc.vector.tensor_tensor(before, tiles_to.unsqueeze(1).broadcast_to([P, NT, E]),
                                    tile_no[:, :].rearrange("p (j e) -> p j e", e=E), ALU.is_le).then_inc(s["routing"], 1)
            vec.wait_ge(s["routing"], n + 9)
            ended = small[:, 4 * T:4 * T + NT]
            nc.vector.tensor_reduce(ended, before, AX.X, ALU.add).then_inc(s["routing"], 1)
            vec.wait_ge(s["routing"], n + 10)
            nc.vector.tensor_scalar(tile_expert[:, :], ended, float(E - 1), None, ALU.min).then_inc(s["gate_ready"], 1)
            vec.wait_ge(s["gate_ready"], 2)
            vec.wait_ge(s["bias_in"], 16)

            def rows_out(j, v):
                nc.vector.tensor_copy(XS[v % 2], bank(v % 2)[:, 0:P]).then_inc(s["xs_ready"], 1)

            def step(j, u, static, at):
                def exists(lag):
                    return not static or 0 <= at - lag < NT

                def back(lag):
                    return not static or at - lag >= 0
                if exists(0):
                    e = expert_of(vec, j)
                    vec.wait_ge(s["h_done"], j + 1)
                    if back(2):
                        vec.wait_ge(s["gelu_done"], j - 1)
                    hidden = bank(2 + u % 2).rearrange("p (c n) -> p c n", c=HC)
                    bias = B1[:, bass.ds(e * HC, HC)].unsqueeze(2).broadcast_to([P, HC, P])
                    nc.vector.tensor_tensor(HB[u % 2].rearrange("p (c n) -> p c n", c=HC), hidden, bias,
                                            ALU.add).then_inc(s["bias_done"], 1)
                if exists(-1):
                    v = (u + 1) % 4
                    vec.wait_ge(s["t1_done"], j + 2)
                    if back(1):
                        vec.wait_ge(s["h_done"], j)
                    rows_out(j + 1, v)
                if exists(1):
                    v = (u + 3) % 4
                    e = expert_of(vec, j - 1)
                    vec.wait_ge(s["y_done"], j)
                    if back(5):
                        ys_out = (s["ys_out0"], s["ys_out1"], s["ys_out2"], s["ys_out3"])[v]
                        vec.wait_ge(ys_out, 4 * (j - 1 - v))
                    nc.vector.tensor_tensor(YS[v], bank(6 + v % 2)[:, 0:D], B2[:, bass.ds(e * D, D)],
                                            ALU.add).then_inc(s["y_ready"], 1)

            vec.wait_ge(s["t1_done"], 1)
            rows_out(0, 0)
            sorted_steps(vec, step)
            for t in range(T):
                if t % TC == 0:
                    vec.wait_ge(s[f"rows_gathered{t // TC}"], 16 * TC)
                x_tile = X[:, t * P:(t + 1) * P]
                nc.vector.scalar_tensor_tensor(out=x_tile, in0=YG[:, t * P:(t + 1) * P], scalar=0.5, in1=x_tile,
                                               op0=ALU.mult, op1=ALU.add).then_inc(s["added"], 1)

        def top1_scalar(act, s):
            norm_scalar(act, s)

            def weights_out(j, v):
                e = expert_of(act, j)
                nc.scalar.activation(W1S[v % 2], W1[:, bass.ds(e * HID, HID)], ACT.Copy).then_inc(s["w1_ready"], 1)

            def step(j, u, static, at):
                def exists(lag):
                    return not static or 0 <= at - lag < NT

                def back(lag):
                    return not static or at - lag >= 0
                if exists(-1):
                    if back(1):
                        act.wait_ge(s["h_done"], j)
                    weights_out(j + 1, u + 1)
                if exists(0):
                    act.wait_ge(s["bias_done"], j + 1)
                    if back(2):
                        act.wait_ge(s["y_done"], j - 1)
                    nc.scalar.activation(HG[u % 2], HB[u % 2], ACT.Gelu).then_inc(s["gelu_done"], 1)

            act.wait_ge(s["gate_ready"], 2)
            act.wait_ge(w_top1, 16 * 5)
            weights_out(0, 0)
            sorted_steps(act, step)

        def top1_gpsimd(pool, s):
            pool.wait_ge(s["gate_ready"], 1)
            pool.wait_ge(normed, s["k"] * T + T)
            pool.wait_ge(zero_rows_done, 16 * NT)
            for before in S[:s["k"]]:
                if before["kind"] == "top1":
                    pool.wait_ge(before["t1_done"], NT)
            for t in range(T):
                nc.gpsimd.indirect_dma_start(sorted_in[:, :], bass.IndirectOffsetOnAxis(dest[:, t:t + 1], 0),
                                             XN[:, t * P:(t + 1) * P], None).then_inc(s["rows_scattered"], 16)
            ys_out = (s["ys_out0"], s["ys_out1"], s["ys_out2"], s["ys_out3"])
            with pool.Fori(0, NT // 4) as i:
                for u in range(4):
                    pool.wait_ge(s["y_ready"], i * 4 + (u + 1))
                    nc.gpsimd.dma_start(sorted_out[bass.ds(i * (4 * P) + u * P, P), :], YS[u]).then_inc(ys_out[u], 16)
            for u in range(4):
                pool.wait_ge(ys_out[u], 16 * (NT // 4))
            pool.wait_ge(s["logits_ready"], 1)
            for t in range(T):
                nc.gpsimd.indirect_dma_start(YG[:, t * P:(t + 1) * P], None, sorted_out[:, :],
                                             bass.IndirectOffsetOnAxis(dest[:, t:t + 1], 0)
                                             ).then_inc(s[f"rows_gathered{t // TC}"], 16)

        def top1_sync(sp, s):
            wait_x(sp, s["k"], T - 1)
            sp.dma_start(B2, b21.partition_broadcast(P)).then_inc(s["bias_in"], 16)
            sp.wait_ge(s["rows_scattered"], 16 * T)
            xs_in = (s["xs_in0"], s["xs_in1"], s["xs_in2"], s["xs_in3"])
            for u in range(4):
                sp.dma_start(XS_IN[u], sorted_in[u * P:(u + 1) * P, :]).then_inc(xs_in[u], 16)
            with sp.Fori(1, NT // 4) as i:
                for u in range(4):
                    sp.wait_ge(s["t1_done"], i * 4 + (u - 3))
                    sp.dma_start(XS_IN[u], sorted_in[bass.ds(i * (4 * P) + u * P, P), :]).then_inc(xs_in[u], 16)

        GCOLS = GH * 2 * N
        QS = arena[:, 0:GCOLS // 2].bitcast(BF16)
        KS = arena[:, GCOLS // 2:GCOLS].bitcast(BF16)
        PARTS = [osb[:, i * 3 * N // 2:(i + 1) * 3 * N // 2].bitcast(BF16) for i in range(2)]
        REST = probs
        vcur = VCUR[:, :].rearrange("p (b t h c) -> p b t h c", b=2, t=KEY_TILES, h=GH)
        VHALF = KEY_TILES * GH * 32
        halves = sb("halves", [P, SLOTS])
        minus_max = sb("minus_max", [P, GH * TC])
        shift_parts = sb("shift_parts", [GH * TC, 2 * P], BF16)
        AO = XN
        AOT = XT
        recips = sb("recips", [P, 2 * GH * TC])

        def q_at(u):
            return (u & 7) * (GH * BANK)

        def k_at(u):
            return ((u >> 2) & 1) * N

        def cols(buf, rows, base, at, n):
            if isinstance(at, int):
                return buf[0:rows, base + at:base + at + n]
            return buf[0:rows, bass.ds(at + base, n)]

        def cols_from(rows, at, n):
            return rows[:, at:at + n] if isinstance(at, int) else rows[:, bass.ds(at, n)]

        def turn_on_tensor(pe, s, u, more):
            pe.wait_ge(s["max_ready"], u + 1)
            if more:
                pe.wait_ge(s["max_read"], (u + 1) * SLOTS + 1)
            nc.tensor.transpose(bank(3)[0:GH * TC, 0:P], minus_max[:, :], ident[:, :]).then_inc(s["max_turned"], 1)

        HEAD_IN = 16 * 6
        REST_IN = 16 * 3 * (NC - 1) * GH
        GROUP_IN = 16 * 3 * (NC + 1) * GH

        def group_in(u):
            return (u >> 2) * GROUP_IN + REST_IN

        def max_matmuls(pe, s, u, slot):
            head, tile, half = slot // (2 * TC), (slot // 2) % TC, slot % 2
            first = isinstance(u, int) and u == 0
            for part in range(2):
                if part == 0:
                    if first and slot % (2 * TC) == 0:
                        pe.wait_ge(s[f"first_head_in{head}"], HEAD_IN)
                    if slot == 0 and not first:
                        pe.wait_ge(s["group_in"], group_in(u))
                    if slot >= 2 or not first:
                        pe.wait_ge(s["max_read"], u * SLOTS + (slot - 1))
                    if slot == 2 and not first:
                        pe.wait_ge(s["shift_split"], u)
                mm = nc.tensor.matmul(bank(3 + 2 * (slot % 2) + part),
                                      cols(QS, KROWS, head * BANK + tile * P, q_at(u), P),
                                      cols(KS, KROWS, head * 2 * N + (2 * half + part) * BANK, k_at(u), BANK),
                                      start=True, stop=True)
                if part == 1:
                    mm.then_inc(s["max_raw"], 1)
                yield

        OUT_STEPS = GH + 1

        def turn_outputs(pe, s, c, g):
            n = c * GH + g
            pe.wait_ge(s["o_bank_free"], g * NC + c + 2)
            if n >= 2:
                pe.wait_ge(s["o_scaled"], n - 1)
            for i in range(TC):
                at = (g * NC + c) * BANK + i * P
                mm = nc.tensor.transpose(bank(3 + n % 2)[:, i * P:(i + 1) * P], osb[:, at:at + P], ident[:, :])
            mm.then_inc(s["o_turned"], 1)

        def turn_heads(pe, s, c):
            pe.wait_ge(s["o_scaled"], (c + 1) * GH)
            if c >= 1:
                pe.wait_ge(s["a_ready"], c)
            for i in range(TC):
                t = c * TC + i
                mm = nc.tensor.transpose(bank(5)[:, i * P:(i + 1) * P], AO[:, t * P:(t + 1) * P], ident[:, :])
            mm.then_inc(s["a_turned"], 1)

        def project_chunk(pe, s, c):
            pe.wait_ge(s["a_ready"], c + 1)
            if c >= 1:
                pe.wait_ge(s["added"], c)
            for i in range(TC):
                t = c * TC + i
                mm = nc.tensor.matmul(bank(6)[:, i * D:(i + 1) * D], AOT[:, t * P:(t + 1) * P],
                                      WO1[:, :], start=True, stop=True)
            mm.then_inc(s["out_ready"], 1)

        def output_step(pe, s, at):
            c, g = at // OUT_STEPS, at % OUT_STEPS
            if g == 1 and c >= 1:
                project_chunk(pe, s, c - 1)
            if g == 0 and c >= 1:
                turn_heads(pe, s, c - 1)
            if g < GH and c < NC:
                turn_outputs(pe, s, c, g)

        def softmax_tensor(pe, s):
            norm_tensor(pe, s)
            pe.wait_ge(w_softmax, 16 * 8)
            for i, side in enumerate((1, 0)):
                for c in range(NC):
                    n = i * NC + c
                    pe.wait_ge(xt_ready, s["k"] * NC + c + 1)
                    if n >= 2:
                        pe.wait_ge(s["part1"], n - 1)
                        pe.wait_ge(s["rest1"], n - 1)
                    nc.tensor.matmul(bank(4 + n % 2), WQKV1[:, side * D:(side + 1) * D],
                                     XT[:, c * BANK:(c + 1) * BANK], start=True, stop=True).then_inc(s["proj_raw"], 1)
            for c in range(NC):
                if c >= 2:
                    pe.wait_ge(s["v_all"], c - 1)
                for i in range(TC):
                    t = c * TC + i
                    mm = nc.tensor.matmul(bank(6 + c % 2)[:, i * D:(i + 1) * D], XT[:, t * P:(t + 1) * P],
                                          WQKV1[:, 2 * D:3 * D], start=True, stop=True)
                mm.then_inc(s["v_raw"], 1)

            def scores(n, kt, j):
                i = kt * GH + j
                if i == 0:
                    pe.wait_ge(s["shift_in"], (n + 1) * 32)
                    if not (isinstance(n, int) and n == 0):
                        pe.wait_ge(s["exp_done"], n * STEPS)
                if i >= 3:
                    pe.wait_ge(s["exp_done"], n * STEPS + (i - 2))
                nc.tensor.matmul(bank(i % 3),
                                 cols(KS, KFULL, j * 2 * N + kt * P, k_at(n), P),
                                 cols(QS, KFULL, j * BANK, q_at(n), BANK), start=True,
                                 stop=True).then_inc(s["score_ready"], 1)
            def values(n, kt, parity):
                pe.wait_ge(s["exp_done"], n * STEPS + GH * (kt + 1))
                if kt == 0:
                    pe.wait_ge(s["v_cur"], n + 1)
                    pe.wait_ge(s["o_bank_free"], n + 1)
                for j in range(GH):
                    slot = (kt * GH + j) % RING
                    mm = nc.tensor.matmul(bank(7)[32 * j:32 * j + 32, :], vcur[:, parity, kt, j, :],
                                          probs[:, slot * BANK:(slot + 1) * BANK], start=(kt == 0),
                                          stop=(kt == KEY_TILES - 1))
                mm.then_inc(s["pv_done"], 1)

            def unit(n, parity, maxima, next_maxima):
                for kt in range(KEY_TILES):
                    fill = []
                    slot = AHEAD + 2 * kt
                    if slot < SLOTS:
                        if maxima:
                            fill = [max_matmuls(pe, s, n + 1, slot), max_matmuls(pe, s, n + 1, slot + 1)]
                    elif next_maxima:
                        fill = [max_matmuls(pe, s, n + 2, slot - SLOTS), max_matmuls(pe, s, n + 2, slot + 1 - SLOTS)]
                    turn = maxima and slot == SLOTS
                    values_after = 1 if turn else GH - 1 if maxima else GH - 2
                    for j in range(GH):
                        scores(n, kt, j)
                        if turn and j == 2:
                            turn_on_tensor(pe, s, n + 1, next_maxima)
                        if fill:
                            next(fill[j // 2])
                        if j == values_after:
                            if kt >= 1:
                                values(n, kt - 1, parity)
                            elif not (isinstance(n, int) and n == 0):
                                values(n - 1, KEY_TILES - 1, 1 - parity)
                    if not maxima:
                        output_step(pe, s, kt)

            for half_read in ("part1", "rest1"):
                pe.wait_ge(s[half_read], 2 * NC)
            pe.wait_ge(s["v_all"], NC - 1)
            pe.wait_ge(s["o_bank_free"], 1)
            for slot in range(SLOTS):
                for _ in max_matmuls(pe, s, 0, slot):
                    pass
            for slot in range(AHEAD):
                if slot == 2:
                    turn_on_tensor(pe, s, 0, True)
                for _ in max_matmuls(pe, s, 1, slot):
                    pass
            unit(0, 0, True, True)
            with pe.Fori(0, UNITS // 2 - 2) as m:
                unit(m * 2 + 1, 1, True, True)
                unit(m * 2 + 2, 0, True, True)
            unit(UNITS - 3, 1, True, True)
            unit(UNITS - 2, 0, True, False)
            pe.wait_ge(s["shift_split"], UNITS)
            pe.wait_ge(s["max_read"], UNITS * SLOTS)
            unit(UNITS - 1, 1, False, False)
            values(UNITS - 1, KEY_TILES - 1, 1)
            for at in range(KEY_TILES, OUT_STEPS * NC + 2):
                output_step(pe, s, at)

        def softmax_vector(vec, s):
            norm_vector(vec, s)
            for i, side in enumerate((1, 0)):
                for c in range(NC):
                    n = i * NC + c
                    rest = REST[:, (n % 2) * BANK:(n % 2 + 1) * BANK]
                    parts = PARTS[side].rearrange("p (a n) -> p a n", a=3)[:, :, c * BANK:(c + 1) * BANK]
                    vec.wait_ge(s["part1"], n + 1)
                    if n >= 2:
                        vec.wait_ge(s["part3"], n - 1)
                    nc.vector.scalar_tensor_tensor(out=rest, in0=bank(4 + n % 2), scalar=QKV_BIAS[:, side:side + 1],
                                                   in1=parts[:, 0, :], op0=ALU.add,
                                                   op1=ALU.subtract).then_inc(s["rest1"], 1)
                    vec.wait_ge(s["part2"], n + 1)
                    nc.vector.tensor_tensor(parts[:, 2, :], rest, parts[:, 1, :], ALU.subtract).then_inc(s["part3"], 1)

            def read_max(u, slot):
                if slot == 0 and not (isinstance(u, int) and u == 0):
                    vec.wait_ge(s["max_ready"], u)
                vec.wait_ge(s["max_raw"], u * SLOTS + (slot + 1))
                nc.vector.tensor_reduce(halves[:, slot:slot + 1], bank(3 + 2 * (slot % 2), 2), AX.X,
                                        ALU.max).then_inc(s["max_read"], 1)

            def join_halves(u):
                vec.wait_ge(s["max_read"], (u + 1) * SLOTS)
                nc.vector.tensor_reduce(minus_max[:, :], halves[:, :].rearrange("p (m h) -> p m h", h=2), AX.X,
                                        ALU.max, negate=True).then_inc(s["max_ready"], 1)

            def split_shift(u):
                vec.wait_ge(s["max_turned"], u + 1)
                if not (isinstance(u, int) and u == 0):
                    vec.wait_ge(s["shift_in"], u * 32)
                nc.vector.tensor_copy(shift_parts[:, 0:P], bank(3)[0:GH * TC, 0:P]).then_inc(s["rest1"], 1)
                vec.wait_ge(s["rest1"], 2 * NC + u + 1)
                nc.vector.tensor_tensor(shift_parts[:, P:2 * P], bank(3)[0:GH * TC, 0:P], shift_parts[:, 0:P],
                                        ALU.subtract).then_inc(s["shift_split"], 1)

            def unit(n, next_maxima):
                for slot in range(AHEAD, SLOTS):
                    read_max(n + 1, slot)
                join_halves(n + 1)
                if next_maxima:
                    read_max(n + 2, 0)
                split_shift(n + 1)
                if next_maxima:
                    for slot in range(1, AHEAD):
                        read_max(n + 2, slot)

            for slot in range(SLOTS):
                read_max(0, slot)
            join_halves(0)
            for slot in range(AHEAD):
                if slot == 2:
                    split_shift(0)
                read_max(1, slot)
            with vec.Fori(0, UNITS - 2) as n:
                unit(n, True)
            unit(UNITS - 2, False)

            vec.wait_ge(s["v_cur"], UNITS)
            for c in range(NC):
                if c == 1:
                    vec.wait_ge(s["bo_added"], T)
                for g in range(H // GH):
                    if g == 2 and c >= 1:
                        add_chunk(vec, s, c - 1)
                    n = c * GH + g
                    r = recips[:, (n % 2) * GH * TC:(n % 2 + 1) * GH * TC].rearrange("p (i j) -> p i j", i=TC)
                    turned = bank(3 + n % 2).rearrange("p (i j r) -> p i j r", i=TC, j=GH)
                    vec.wait_ge(s["o_turned"], n + 1)
                    nc.vector.reciprocal(r, turned[:, :, :, HD]).then_inc(s["o_recip"], 1)
                    vec.wait_ge(s["o_recip"], n + 1)
                    ao = AO[:, c * BANK:(c + 1) * BANK].rearrange("p (i g j d) -> p i g j d", i=TC, g=H // GH, j=GH)
                    nc.vector.tensor_tensor(ao[:, :, g, :, :], turned[:, :, :, 0:HD],
                                            r.unsqueeze(3).broadcast_to([P, TC, GH, HD]), ALU.mult).then_inc(s["o_scaled"], 1)
            add_chunk(vec, s, NC - 1)

        def add_chunk(vec, s, c):
            vec.wait_ge(s["out_ready"], c + 1)
            x_chunk = X[:, c * BANK:(c + 1) * BANK]
            nc.vector.tensor_tensor(x_chunk, bank(6), x_chunk, ALU.add).then_inc(s["added"], 1)

        def softmax_scalar(act, s):
            norm_scalar(act, s)
            for i, side in enumerate((1, 0)):
                for c in range(NC):
                    n = i * NC + c
                    parts = PARTS[side].rearrange("p (a n) -> p a n", a=3)[:, :, c * BANK:(c + 1) * BANK]
                    act.wait_ge(s["proj_raw"], n + 1)
                    nc.scalar.activation(parts[:, 0, :], bank(4 + n % 2), ACT.Identity,
                                         bias=QKV_BIAS[:, side:side + 1]).then_inc(s["part1"], 1)
                    act.wait_ge(s["rest1"], n + 1)
                    nc.scalar.activation(parts[:, 1, :], REST[:, (n % 2) * BANK:(n % 2 + 1) * BANK],
                                         ACT.Copy).then_inc(s["part2"], 1)
            for c in range(NC):
                act.wait_ge(s["v_raw"], c + 1)
                nc.scalar.activation(VALL[:, c * BANK:(c + 1) * BANK], bank(6 + c % 2),
                                     ACT.Copy).then_inc(s["v_all"] if c < NC - 1 else s["o_bank_free"], 1)

            def keep_outputs(n):
                act.wait_ge(s["pv_done"], (n + 1) * KEY_TILES)
                to = osb[:, n * BANK:(n + 1) * BANK] if isinstance(n, int) else osb[:, bass.ds(n * BANK, BANK)]
                nc.scalar.activation(to, bank(7), ACT.Copy).then_inc(s["o_bank_free"], 1)

            def unit(n, last):
                first = isinstance(n, int) and n == 0
                for i in range(STEPS):
                    kt = i // GH
                    act.wait_ge(s["score_ready"], n * STEPS + (i + 1))
                    if i % GH == 0 and not (first and kt < RING // GH):
                        act.wait_ge(s["pv_done"], n * KEY_TILES + (kt - RING // GH + 1))
                    slot = i % RING
                    nc.scalar.activation(probs[:, slot * BANK:(slot + 1) * BANK], bank(i % 3), ACT.Exp,
                                         scale=SCALE).then_inc(s["exp_done"], 1)
                    if i == GH - 1 and not first:
                        keep_outputs(n - 1)
                    if last and i % GH == GH - 1 and kt % OUT_STEPS == 0 and kt > 0:
                        heads_out(kt // OUT_STEPS - 1)

            def heads_out(c):
                act.wait_ge(s["a_turned"], c + 1)
                nc.scalar.activation(AOT[:, c * BANK:(c + 1) * BANK], bank(5), ACT.Identity,
                                     bias=QKV_BIAS[:, 2:3]).then_inc(s["a_ready"], 1)

            act.wait_ge(s["part3"], 2 * NC)
            unit(0, False)
            with act.Fori(1, UNITS - 1) as n:
                unit(n, False)
            unit(UNITS - 1, True)
            keep_outputs(UNITS - 1)
            heads_out(NC - 1)

        def softmax_pads(pool, s):
            for before in S[:s["k"]]:
                if before["kind"] == "linear":
                    pool.wait_ge(before["added"], NC)
            pool.wait_ge(consts_done, CONSTS)
            nc.gpsimd.memset(KS[PAD_FROM:KFULL, :], 1.0).then_inc(s["pads_done"], 1)
            pool.wait_ge(s["pads_done"], 1)
            nc.gpsimd.memset(VCUR[:, :], 0.0).then_inc(s["pads_done"], 1)
            pool.wait_ge(s["pads_done"], 2)
            nc.gpsimd.memset(VCUR[:, :].rearrange("p (a c) -> p a c", c=32)[:, :, HD:HD + 1], 1.0).then_inc(s["pads_done"], 1)

        def softmax_gpsimd(pool, s):
            v_heads = VALL[:, :].rearrange("p (t g h d) -> p t g h d", t=T, g=H // GH, h=GH)
            pool.wait_ge(s["v_all"], NC - 1)
            pool.wait_ge(s["o_bank_free"], 1)
            pool.wait_ge(s["pads_done"], 3)
            for n in range(2):
                nc.gpsimd.tensor_copy(vcur[:, n, :, :, 0:HD], v_heads[:, :, 0, :, :]).then_inc(s["v_cur"], 1)
            pool.wait_ge(normed, s["k"] * T + T)
            for t in range(T):
                x_tile = X[:, t * P:(t + 1) * P]
                nc.gpsimd.tensor_tensor(x_tile, x_tile, BO1[:, :], ALU.add).then_inc(s["bo_added"], 1)
            with pool.Fori(0, UNITS - 2) as n:
                pool.wait_ge(s["pv_done"], (n + 1) * KEY_TILES)
                source = VALL[:, :].rearrange("p (t c) -> p t c", t=T)[:, :, bass.ds((((n + 2) >> 2) & 3) * (GH * HD), GH * HD)]
                source = source.rearrange("p t (h d) -> p t h d", h=GH)
                to = VCUR[:, bass.ds((n & 1) * VHALF, VHALF)].rearrange("p (t h c) -> p t h c", t=KEY_TILES, h=GH)
                nc.gpsimd.tensor_copy(to[:, :, :, 0:HD], source).then_inc(s["v_cur"], 1)

        def softmax_sync(sp, s):
            for i, side in enumerate((1, 0)):
                for c in range(NC):
                    sp.wait_ge(s["part2"], i * NC + c + 1)
                    sp.wait_ge(s["part3"], i * NC + c + 1)
                    sp.dma_start(parts_dram[side].rearrange("a f n -> f a n")[:, :, c * BANK:(c + 1) * BANK],
                                 PARTS[side].rearrange("p (a n) -> p a n", a=3)[:, :, c * BANK:(c + 1) * BANK]
                                 ).then_inc(s["parts_out"], 16)
            sp.wait_ge(s["parts_out"], 16 * 2 * NC)
            sp.wait_ge(s["pads_done"], 3)

            def load_k(g, j, done):
                for i in range(3):
                    rows = slice(i * 3 * HD, (i + 1) * 3 * HD)
                    part = bass.AP(parts_dram[1].tensor, (i * D + (g * GH + j) * HD) * N, [[0, 3], [N, HD], [1, N]])
                    at = j * 2 * N + (g % 2) * N
                    sp.dma_start(KS[rows, at:at + N], part).then_inc(done, 16)

            def load_q(g, j, c, done):
                feature = (g * GH + j) * HD
                for i in range(3):
                    rows = slice(i * 3 * HD, (i + 1) * 3 * HD)
                    at = (((g % 2) * NC + c) * GH + j) * BANK
                    sp.dma_start(QS[rows, at:at + BANK],
                                 parts_dram[0][:, feature:feature + HD, c * BANK:(c + 1) * BANK]).then_inc(done, 16)

            def load_heads(g, heads):
                for j in heads:
                    load_k(g, j, s["group_in"])
                    for c in range(NC):
                        load_q(g, j, c, s["group_in"])

            def put_shift(u, place):
                sp.wait_ge(s["shift_split"], u + 1)
                for part in range(2):
                    row = KROWS + part
                    sp.dma_start(cols_from(QS[row:row + 1, :], place * (GH * BANK), GH * BANK),
                                 shift_parts[:, part * P:(part + 1) * P]).then_inc(s["shift_in"], 16)

            for j in range(GH):
                load_k(0, j, s[f"first_head_in{j}"])
                load_q(0, j, 0, s[f"first_head_in{j}"])
            for j in range(GH):
                for c in range(1, NC):
                    load_q(0, j, c, s["group_in"])
            put_shift(0, 0)
            sp.wait_ge(s["group_in"], group_in(0))
            load_heads(1, (0, 1))
            put_shift(1, 1)
            load_heads(1, (2, 3))
            with sp.Fori(2, GH + 1) as u:
                put_shift(u, u)
            for g in range(2, H // GH):
                sp.wait_ge(s["group_in"], group_in(GH * (g - 1)))
                sp.wait_ge(s["pv_done"], (g - 1) * NC * KEY_TILES)
                load_heads(g, (0, 1))
                put_shift((g - 1) * NC + 1, ((g - 1) * NC + 1) % 8)
                load_heads(g, (2, 3))
                for u in range((g - 1) * NC + 2, g * NC + 1):
                    put_shift(u, u % 8)
            for u in range(UNITS - 3, UNITS):
                put_shift(u, u % 8)

        tensor_of = {"top2": top2_tensor, "linear": linear_tensor, "top1": top1_tensor, "softmax": softmax_tensor}
        vector_of = {"top2": top2_vector, "linear": linear_vector, "top1": top1_vector, "softmax": softmax_vector}
        scalar_of = {"top2": top2_scalar, "linear": linear_scalar, "top1": top1_scalar, "softmax": softmax_scalar}

        block = ctx.enter_context(nc.Block())

        @block.sync
        def _(sp):
            x_rows = x_in.rearrange("a (t p) d -> p (a t) d", p=P)
            X3 = X[:, :].rearrange("p (t d) -> p t d", d=D)
            for c in range(NC):
                sp.dma_start(X3[:, c * TC:(c + 1) * TC, :], x_rows[:, c * TC:(c + 1) * TC, :]).then_inc(x_loaded[c], 16)
            sp.dma_start(WR0[:, :], wr0).then_inc(w_router, 16)
            sp.dma_start(WE0[:, :].rearrange("p (e f) -> p e f", e=E), we0.rearrange("e d f -> d e f")).then_inc(w_top2, 16)
            for i, w in enumerate((wq0, wk0, wv0)):
                sp.dma_start(WQKV0[:, i * D:(i + 1) * D], w).then_inc(w_linear, 16)
            sp.dma_start(WO0[:, :], wo0).then_inc(w_linear, 16)
            sp.dma_start(WR1[:, :], wr1).then_inc(w_top1, 16)
            sp.dma_start(BR1[:, :], br1.partition_broadcast(P)).then_inc(w_top1, 16)
            sp.dma_start(W1[:, :].rearrange("p (e h) -> p e h", e=E), w11.rearrange("e d h -> d e h")).then_inc(w_top1, 16)
            sp.dma_start(W2[:, :].rearrange("p (a d) -> p a d", d=D), w21.rearrange("e (c p) d -> p (e c) d", p=P)).then_inc(w_top1, 16)
            sp.dma_start(B1[:, :], b11).then_inc(w_top1, 16)
            for i, w in enumerate((wq1, wk1, wv1)):
                sp.dma_start(WQKV1[:, i * D:(i + 1) * D], w).then_inc(w_softmax, 16)
            sp.dma_start(WO1[:, :], wo1).then_inc(w_softmax, 16)
            for i, b in enumerate((bq1, bk1, bv1)):
                sp.dma_start(QKV_BIAS[:, i:i + 1], b).then_inc(w_softmax, 16)
            sp.dma_start(BO1[:, :], bo1.partition_broadcast(P)).then_inc(w_softmax, 16)
            sp.wait_ge(consts_done, CONSTS)
            for j in range(NT):
                sp.dma_start(sorted_in[j * P:(j + 1) * P, :], zeros[:, :]).then_inc(zero_rows_done, 16)
            for s in S:
                if s["kind"] == "top1":
                    top1_sync(sp, s)
                if s["kind"] == "softmax":
                    softmax_sync(sp, s)
            out_rows = out.rearrange("a (t p) d -> p (a t) d", p=P)
            for c in range(NC):
                wait_x(sp, len(LAYERS), (c + 1) * TC - 1)
                sp.dma_start(out_rows[:, c * TC:(c + 1) * TC, :], X3[:, c * TC:(c + 1) * TC, :]).then_inc(out_stored, 16)
            sp.wait_ge(out_stored, 16 * NC)

        @block.gpsimd
        def _(pool):
            nc.gpsimd.memset(ident[:, :], 0.0).then_inc(consts_done, 1)
            nc.gpsimd.memset(upper[:, :], 1.0).then_inc(consts_done, 1)
            nc.gpsimd.memset(ones[:, :], 1.0).then_inc(consts_done, 1)
            nc.gpsimd.memset(block_diag[:, :], 1.0).then_inc(consts_done, 1)
            nc.gpsimd.memset(ones8[:, :], 1.0).then_inc(consts_done, 1)
            nc.gpsimd.memset(zeros[:, :], 0.0).then_inc(consts_done, 1)
            nc.gpsimd.memset(mask[:, T * E:], 0.0).then_inc(consts_done, 1)
            for e in range(E):
                nc.gpsimd.memset(desc[:, :].rearrange("p (t e) -> p t e", e=E)[:, :, e:e + 1],
                                 float(E - e)).then_inc(consts_done, 1)
            pool.wait_ge(consts_done, 15)
            nc.gpsimd.affine_select(out=ident[:, :], in_=ident[:, :], compare_op=ALU.not_equal, fill=1.0, base=0,
                                    pattern=[[-1, P]], channel_multiplier=1).then_inc(consts_done, 1)
            nc.gpsimd.affine_select(out=upper[:, :], in_=upper[:, :], compare_op=ALU.is_gt, fill=0.0, base=0,
                                    pattern=[[1, P]], channel_multiplier=-1).then_inc(consts_done, 1)
            blocks = block_diag[:, :].rearrange("p (h d) -> p h d", d=HD)
            nc.gpsimd.affine_select(out=blocks, in_=blocks, compare_op=ALU.is_ge, fill=0.0, base=0,
                                    pattern=[[-HD, H], [0, HD]], channel_multiplier=1).then_inc(consts_done, 1)
            pool.wait_ge(consts_done, 18)
            nc.gpsimd.affine_select(out=blocks, in_=blocks, compare_op=ALU.is_ge, fill=0.0, base=HD - 1,
                                    pattern=[[HD, H], [0, HD]], channel_multiplier=-1).then_inc(consts_done, 1)
            iota_a = route[:, 0:E * T].bitcast(I32)
            iota_b = plan_big[:, :].bitcast(I32)
            nc.gpsimd.iota(iota_a.rearrange("p (e j) -> p e j", e=E), [[0, E], [P, T]], base=0,
                           channel_multiplier=0).then_inc(consts_done, 1)
            nc.gpsimd.iota(iota_b.rearrange("p (j e) -> p j e", e=E), [[1, NT], [0, E]], base=0,
                           channel_multiplier=0).then_inc(consts_done, 1)
            pool.wait_ge(consts_done, 21)
            nc.gpsimd.tensor_copy(steps128[:, :], iota_a).then_inc(consts_done, 1)
            nc.gpsimd.tensor_copy(tile_no[:, :], iota_b).then_inc(consts_done, 1)
            for s in S:
                for following in S[s["k"] + 1:s["k"] + 2]:
                    if following["kind"] == "softmax":
                        softmax_pads(pool, following)
                if s["kind"] == "softmax" and s["k"] == 0:
                    softmax_pads(pool, s)
                if s["kind"] == "top1":
                    top1_gpsimd(pool, s)
                if s["kind"] == "softmax":
                    softmax_gpsimd(pool, s)

        @block.tensor
        def _(pe):
            for s in S:
                tensor_of[s["kind"]](pe, s)

        @block.vector
        def _(vec):
            vec.wait_ge(consts_done, CONSTS)
            for s in S:
                vector_of[s["kind"]](vec, s)

        @block.scalar
        def _(act):
            for s in S:
                scalar_of[s["kind"]](act, s)


def kernel(L0_attn_x, L0_attn_Wq, L0_attn_Wk, L0_attn_Wv, L0_attn_Wo, L0_ffn_Wr, L0_ffn_We, L1_attn_Wq,
           L1_attn_bq, L1_attn_Wk, L1_attn_bk, L1_attn_Wv, L1_attn_bv, L1_attn_Wo, L1_attn_bo, L1_ffn_Wr,
           L1_ffn_br, L1_ffn_W1, L1_ffn_b1, L1_ffn_W2, L1_ffn_b2):
    import numpy as np
    import concourse.bacc as bacc
    from concourse.bass_utils import run_bass_kernel_spmd

    def a(x):
        return np.ascontiguousarray(x)

    def turned(x):
        return np.ascontiguousarray(np.asarray(x).T)

    def row(x):
        return np.ascontiguousarray(x).reshape(-1)

    def column(x):
        return np.ascontiguousarray(x).reshape(-1, 1)

    arrays = {
        "x_in": a(L0_attn_x),
        "wq0": turned(L0_attn_Wq), "wk0": turned(L0_attn_Wk), "wv0": turned(L0_attn_Wv), "wo0": turned(L0_attn_Wo),
        "wr0": turned(L0_ffn_Wr), "we0": a(L0_ffn_We),
        "wq1": turned(L1_attn_Wq), "bq1": column(L1_attn_bq), "wk1": turned(L1_attn_Wk), "bk1": column(L1_attn_bk),
        "wv1": turned(L1_attn_Wv), "bv1": column(L1_attn_bv), "wo1": turned(L1_attn_Wo), "bo1": row(L1_attn_bo),
        "wr1": a(L1_ffn_Wr), "br1": row(L1_ffn_br), "w11": a(L1_ffn_W1), "b11": np.ascontiguousarray(np.asarray(L1_ffn_b1).reshape(E * HC, P).T),
        "w21": a(L1_ffn_W2), "b21": row(L1_ffn_b2),
    }
    nc = bacc.Bacc("TRN2", target_bir_lowering=False, num_devices=1)
    args = [nc.dram_tensor(name, v.shape, mybir.dt.from_np(v.dtype), kind="ExternalInput").ap()
            for name, v in arrays.items()]
    out = nc.dram_tensor("out", (1, N, D), F32, kind="ExternalOutput").ap()
    macaron(nc, *args, out)
    r = run_bass_kernel_spmd(nc, [arrays], core_ids=[0])
    return r.results[0]["out"]
```

```python
from contextlib import ExitStack

import concourse.bass as bass
from concourse import mybir

F32 = mybir.dt.float32
BF16 = mybir.dt.bfloat16
I32 = mybir.dt.int32
U32 = mybir.dt.uint32
ALU = mybir.AluOpType
ACT = mybir.ActivationFunctionType
AX = mybir.AxisListType

P = 128
D = 128
N = 2048
T = N // P
BANK = 512
NC = N // BANK
TC = BANK // P
NORM_SPLIT = 10
EPS = 1e-5
E = 8
CAP = int(N * 2 / E * 1.5) + 1
BIG = 3.0e38
LA_EPS = 1e-6
H = 16
HD = D // H
HID = 512
HC = HID // P
ROW = D + 1
TOKENS_KEPT = 8
W1_COLS = HID + HC
NT = N // P + E
SCALE = float(HD) ** -0.5

LAYERS = ["top2", "linear", "top2", "top1", "softmax", "top1"]

GH = 4
UNITS = (H // GH) * NC
TERMS = 9
KROWS = TERMS * HD
KFULL = KROWS + 2
PAD_FROM = KROWS // 32 * 32
KEY_TILES = N // P
STEPS = KEY_TILES * GH
RING = 8
SLOTS = GH * TC * 2
FIRST_AHEAD = 4
AHEAD = 8


def macaron(nc, x_in, wq0, wk0, wv0, wo0, wr0, we0, wq1, bq1, wk1, bk1, wv1, bv1, wo1, bo1,
            wr1, br1, w11, b11, w21, b21, out):
    with ExitStack() as ctx:
        def sb(name, shape, dt=F32):
            return ctx.enter_context(nc.sbuf_tensor(name, shape, dt))

        def sem(name):
            return ctx.enter_context(nc.semaphore(name))

        X = sb("X", [P, N])
        XN = sb("XN", [P, N])
        XT = sb("XT", [P, N])
        WQKV0 = sb("WQKV0", [P, 3 * D])
        WO0 = sb("WO0", [P, D])
        WR0 = sb("WR0", [P, E])
        WE0 = sb("WE0", [P, E * D])
        WQKV1 = sb("WQKV1", [P, 3 * D])
        WO1 = sb("WO1", [P, D])
        QKV_BIAS = sb("QKV_BIAS", [P, 3])
        BO1 = sb("BO1", [P, D])
        WR1 = sb("WR1", [P, E])
        BR1 = sb("BR1", [P, E])
        W1 = sb("W1", [P, E * W1_COLS])
        W2 = sb("W2", [P, E * HC * D])
        ident = sb("ident", [P, P])
        upper = sb("upper", [P, P], BF16)
        ones = sb("ones", [P, P], BF16)
        desc = sb("desc", [P, T * E])
        block_diag = sb("block_diag", [P, D])
        steps128 = sb("steps128", [P, E * T])
        tile_no = sb("tile_no", [P, NT * E])
        ones8 = sb("ones8", [P, E])
        row_no = sb("row_no", [P, T + NT])
        stats = sb("stats", [P, T * 6])
        small = sb("small", [P, 12 * T])
        route = sb("route", [P, 7 * T * E])
        mask = sb("mask", [P, (T + 1) * E], BF16)
        gate = sb("gate", [P, T * E])
        dest = sb("dest", [P, T], U32)
        slot_token = sb("slot_token", [P, TOKENS_KEPT], U32)
        tile_expert = sb("tile_expert", [P, NT], I32)
        plan = sb("plan", [P, 8 * E])
        plan_big = sb("plan_big", [P, NT * E])
        arena = sb("arena", [P, 16384])
        probs = sb("probs", [P, RING * BANK])
        osb = sb("osb", [P, UNITS * BANK])
        VCUR = sb("VCUR", [P, 2 * KEY_TILES * GH * 32])
        blank_rows = osb[:, 0:NT * ROW].rearrange("p (j r) -> p j r", r=ROW)
        VALL = XN

        psum = ctx.enter_context(nc.psum_tensor("psum", [P, 8 * BANK], F32))

        def bank(b, n=1):
            return psum[:, b * BANK:(b + n) * BANK]

        sorted_in = {k: nc.dram_tensor(f"sorted_in{k}", [NT * P, ROW], F32, kind="Internal").ap()
                     for k, kind in enumerate(LAYERS) if kind == "top1"}
        y_dram = nc.dram_tensor("y_rows", [N + NT * P, D], F32, kind="Internal").ap()
        q_dram = nc.dram_tensor("q_parts", [H, 3, HD, N], BF16, kind="Internal").ap()
        k_dram = nc.dram_tensor("k_parts", [3, D, N], BF16, kind="Internal").ap()

        def col(i, n=T):
            return small[:, i * T:i * T + n]

        def te(i):
            return route[:, i * T * E:(i + 1) * T * E].rearrange("p (t e) -> p t e", e=E)

        def over_experts(ap, m=T):
            return ap.unsqueeze(2).broadcast_to([P, m, E])

        x_loaded = [sem(f"x_loaded{c}") for c in range(NC)]
        consts_done = sem("consts_done")
        w_router = sem("w_router")
        w_top2 = sem("w_top2")
        w_linear = sem("w_linear")
        w_top1 = sem("w_top1")
        w_softmax = sem("w_softmax")
        blank_rows_ready = sem("blank_rows_ready")
        zero_rows_done = sem("zero_rows_done")
        out_stored = sem("out_stored")
        y_in = [sem(f"y_in{c}") for c in range(NC)]
        CONSTS = 24

        stats_done, moments, var_ready, std_ready, normed, turned, xt_ready = (
            sem(n) for n in ("stats_done", "moments", "var_ready", "std_ready", "normed", "turned", "xt_ready"))
        offset_ready, normed_too = sem("offset_ready"), sem("normed_too")
        MOMENTS = 7

        def wait_normed(eng, s, tiles):
            eng.wait_ge(normed, s["k"] * NORM_SPLIT + min(tiles, NORM_SPLIT))
            if tiles > NORM_SPLIT:
                eng.wait_ge(normed_too, s["k"] * (T - NORM_SPLIT) + tiles - NORM_SPLIT)

        def layer_sems(k, kind):
            names = []
            if kind in ("top2", "top1"):
                names += ["logits_ready", "routing", "mask_ready", "ranks_ready", "gate_ready"]
            if kind == "top2":
                names += ["gap_ready", "gap_exp", "y_ready", "weighted", "added", "added_too"]
            if kind == "linear":
                names += ["q_raw", "q_neg", "q_exp", "q_done", "kv_raw", "k_neg", "k_exp", "k_done",
                          "v_done", "kv_sum", "kv_blocks", "num_ready", "den_free", "norm_chain",
                          "o_ready", "o_turned", "ot_ready", "out_ready", "added"]
            if kind == "top1":
                names += ["rows_scattered", "bias_in", "t1_done", "xs_ready", "tokens_ready", "pool_steps", "w1_ready", "b2_ready", "h_done",
                          "bias_done", "gelu_done", "y_done", "y_ready", "added"]
                names += [f"xs_in{u}" for u in range(4)] + [f"ys_out{u}" for u in range(4)]
            if kind == "softmax":
                names += ["proj_raw", "part1", "rest1", "part2", "part3", "parts_out",
                          "first_head_in0", "first_head_in1", "first_head_in2", "first_head_in3", "v_raw", "v_all", "pads_done", "group_in", "v_cur", "o_bank_free", "max_raw",
                          "max_read", "max_ready", "max_turned", "shift_split", "shift_in", "exp_loaded", "score_ready",
                          "exp_done", "pv_done", "o_turned", "o_recip", "o_scaled", "a_turned",
                          "a_ready", "out_ready", "bo_added", "added"]
            return {"k": k, "kind": kind} | {n: sem(f"L{k}_{n}") for n in names}

        S = [layer_sems(k, kind) for k, kind in enumerate(LAYERS)]

        def wait_x(eng, k, t):
            if k == 0:
                eng.wait_ge(x_loaded[t // TC], 16)
            elif S[k - 1]["kind"] == "top2":
                eng.wait_ge(S[k - 1]["added_too"], 8 * (t // 4 + 1))
                if t >= 2:
                    eng.wait_ge(S[k - 1]["added"], 16 * ((t + 2) // 4))
            elif S[k - 1]["kind"] == "top1":
                eng.wait_ge(S[k - 1]["added"], 3 * (t // 4) + min(t % 4 + 1, 3))
                if t >= 3:
                    eng.wait_ge(S[k - 1]["pool_steps"], 1 + (t + 1) // 4)
            else:
                eng.wait_ge(S[k - 1]["added"], t // TC + 1)

        ROWS_AT = 2 * N

        def xn_tile(s, t):
            if s["kind"] == "top1":
                return arena[:, ROWS_AT + t * ROW:ROWS_AT + t * ROW + D]
            return XN[:, t * D:(t + 1) * D]

        def chunk_stats(vec, k, c):
            st = stats[:, :].rearrange("p (t s) -> p t s", s=6)
            if k == len(LAYERS):
                return
            for t in range(c * TC, (c + 1) * TC):
                wait_x(vec, k, t)
                nc.vector.bn_stats(st[:, t, :], X[:, t * P:(t + 1) * P]).then_inc(stats_done, 1)

        def norm_vector(vec, s):
            st = stats[:, :].rearrange("p (t s) -> p t s", s=6)
            mean_even, m2_even, mean_odd, m2_odd = st[:, :, 1], st[:, :, 2], st[:, :, 4], st[:, :, 5]
            mean_sum, mean_dif, m2, mean, dif2, dvar, var, std, rstd, offset = (col(i) for i in range(10))
            if s["k"] == 0 or LAYERS[s["k"] - 1] in ("top2", "linear"):
                for c in range(NC):
                    chunk_stats(vec, s["k"], c)
            vec.wait_ge(stats_done, s["k"] * T + T)
            nc.vector.tensor_tensor(mean_sum, mean_even, mean_odd, ALU.add).then_inc(moments, 1)
            nc.vector.tensor_tensor(mean_dif, mean_even, mean_odd, ALU.subtract).then_inc(moments, 1)
            nc.vector.tensor_tensor(m2, m2_even, m2_odd, ALU.add).then_inc(moments, 1)
            vec.wait_ge(moments, s["k"] * MOMENTS + 2)
            nc.vector.tensor_tensor(dif2, mean_dif, mean_dif, ALU.mult).then_inc(moments, 1)
            nc.vector.tensor_scalar(mean, mean_sum, 0.5, None, ALU.mult).then_inc(moments, 1)
            vec.wait_ge(moments, s["k"] * MOMENTS + 4)
            nc.vector.scalar_tensor_tensor(out=dvar, in0=dif2, scalar=D / 4, in1=m2, op0=ALU.mult,
                                           op1=ALU.add).then_inc(moments, 1)
            vec.wait_ge(moments, s["k"] * MOMENTS + 6)
            nc.vector.tensor_scalar(var, dvar, 1.0 / D, EPS, ALU.mult, ALU.add).then_inc(var_ready, 1)
            vec.wait_ge(std_ready, s["k"] + 1)
            nc.vector.reciprocal(rstd, std).then_inc(moments, 1)
            vec.wait_ge(moments, s["k"] * MOMENTS + 7)
            nc.vector.scalar_tensor_tensor(out=offset, in0=mean, scalar=-1.0, in1=rstd, op0=ALU.mult,
                                           op1=ALU.mult).then_inc(offset_ready, 1)
            for t in range(NORM_SPLIT):
                nc.vector.tensor_scalar(xn_tile(s, t), X[:, t * P:(t + 1) * P], mean[:, t:t + 1],
                                        rstd[:, t:t + 1], ALU.subtract, ALU.mult).then_inc(normed, 1)

        def norm_scalar(act, s):
            act.wait_ge(var_ready, s["k"] + 1)
            nc.scalar.activation(col(7), col(6), ACT.Sqrt).then_inc(std_ready, 1)
            rstd, offset = col(8), col(9)
            act.wait_ge(offset_ready, s["k"] + 1)
            for t in range(NORM_SPLIT, T):
                nc.scalar.activation(xn_tile(s, t), X[:, t * P:(t + 1) * P], ACT.Identity,
                                     bias=offset[:, t:t + 1], scale=rstd[:, t:t + 1]).then_inc(normed_too, 1)
            for c in range(NC):
                act.wait_ge(turned, s["k"] * NC + c + 1)
                nc.scalar.activation(XT[:, c * BANK:(c + 1) * BANK], bank(c), ACT.Copy).then_inc(xt_ready, 1)

        def warm_up(n):
            for _ in range(n):
                nc.tensor.matmul(bank(0), ones[:, :], ones[:, :].unsqueeze(1).broadcast_to([P, BANK // P, P]),
                                 start=True, stop=True)

        def norm_tensor(pe, s):
            pe.wait_ge(consts_done, CONSTS)
            if s["k"] > 0:
                pe.wait_ge(stats_done, s["k"] * T + T - 3)
            warm_up(8 if s["k"] > 0 else 13)
            for c in range(NC):
                wait_normed(pe, s, TC * (c + 1))
                for i in range(TC):
                    t = c * TC + i
                    mm = nc.tensor.transpose(psum[:, t * P:(t + 1) * P], xn_tile(s, t), ident[:, :])
                mm.then_inc(turned, 1)

        LG = bank(6)[:, 0:T * E]
        RANK = bank(7)[:, 0:(T + 1) * E]

        def logits_tensor(pe, s, w):
            if w is WR0:
                pe.wait_ge(w_router, 16)
            else:
                pe.wait_ge(w_top1, 16 * 5)
            for t in range(T):
                pe.wait_ge(xt_ready, s["k"] * NC + t // TC + 1)
                mm = nc.tensor.matmul(LG[:, t * E:(t + 1) * E], XT[:, t * P:(t + 1) * P], w[:, :],
                                      start=True, stop=True)
            mm.then_inc(s["logits_ready"], 1)

        def ranks_tensor(pe, s):
            pe.wait_ge(s["mask_ready"], 1)
            nc.tensor.matmul(RANK, upper[:, :], mask[:, :], start=True, stop=False)
            for d in range(1, T + 1):
                mm = nc.tensor.matmul(RANK[:, d * E:], ones[:, :], mask[:, 0:(T + 1 - d) * E],
                                      start=False, stop=(d == T))
            mm.then_inc(s["ranks_ready"], 1)

        def pick(vec, s, n, logits, largest, one_hot, work, work_max):
            vec.wait_ge(consts_done, CONSTS)
            nc.vector.tensor_reduce(largest, logits, AX.X, ALU.max).then_inc(s["routing"], 1)
            vec.wait_ge(s["routing"], n + 1)
            nc.vector.tensor_tensor(work, logits, over_experts(largest), ALU.is_equal).then_inc(s["routing"], 1)
            vec.wait_ge(s["routing"], n + 2)
            nc.vector.tensor_tensor(work, work, desc[:, :].rearrange("p (t e) -> p t e", e=E),
                                    ALU.mult).then_inc(s["routing"], 1)
            vec.wait_ge(s["routing"], n + 3)
            nc.vector.tensor_reduce(work_max, work, AX.X, ALU.max).then_inc(s["routing"], 1)
            vec.wait_ge(s["routing"], n + 4)
            nc.vector.tensor_tensor(one_hot, work, over_experts(work_max), ALU.is_equal).then_inc(s["routing"], 1)
            vec.wait_ge(s["routing"], n + 5)
            return n + 5

        ADD_ORDER = [(e, 2) for e in range(E // 2)]
        for e in range(E // 2):
            ADD_ORDER += [(e + E // 2, 2), (e, 3)]
        ADD_ORDER += [(e, 3) for e in range(E // 2, E)]

        def top2_tensor(pe, s):
            norm_tensor(pe, s)
            logits_tensor(pe, s, WR0)
            pe.wait_ge(w_top2, 16)

            def experts(t):
                u = t % 4
                if t >= 4 and u < 2:
                    pe.wait_ge(s["weighted"], E * (2 * (t // 4 - 1) + u + 1))
                if t >= 4 and u >= 2:
                    pe.wait_ge(s["added"], 16 * (t // 4 - 1) + ADD_ORDER.index((E - 1, u)) + 1)
                for half in range(2):
                    mm = nc.tensor.matmul(bank(2 * u + half), XT[:, t * P:(t + 1) * P],
                                          WE0[:, half * BANK:(half + 1) * BANK], start=True, stop=True)
                mm.then_inc(s["y_ready"], 1)

            pe.wait_ge(xt_ready, s["k"] * NC + NC)
            for t in range(2):
                experts(t)
            ranks_tensor(pe, s)
            experts(2)
            pe.wait_ge(s["gate_ready"], 1)
            for t in range(3, T):
                experts(t)

        def top2_vector(vec, s):
            norm_vector(vec, s)
            L, L2, first, second, work, g1, g2 = (te(i) for i in range(7))
            top, top2, work_max, gap, gap_e, total, w_first, w_second = (col(i) for i in range(8))
            vec.wait_ge(s["logits_ready"], 1)
            nc.vector.tensor_copy(route[:, 0:T * E], LG).then_inc(s["routing"], 1)
            vec.wait_ge(s["routing"], 1)
            n = pick(vec, s, 1, L, top, first, work, work_max)
            nc.vector.scalar_tensor_tensor(out=L2, in0=first, scalar=-BIG, in1=L, op0=ALU.mult,
                                           op1=ALU.add).then_inc(s["routing"], 1)
            n += 1
            vec.wait_ge(s["routing"], n)
            n = pick(vec, s, n, L2, top2, second, work, work_max)
            nc.vector.tensor_tensor(mask[:, 0:T * E].rearrange("p (t e) -> p t e", e=E), first, second,
                                    ALU.add).then_inc(s["mask_ready"], 1)
            nc.vector.tensor_tensor(gap, top2, top, ALU.subtract).then_inc(s["gap_ready"], 1)
            vec.wait_ge(s["gap_exp"], 1)
            nc.vector.tensor_scalar(total, gap_e, 1.0, 2.0, ALU.add, ALU.mult).then_inc(s["routing"], 1)
            vec.wait_ge(s["routing"], n + 1)
            nc.vector.reciprocal(w_first, total).then_inc(s["routing"], 1)
            vec.wait_ge(s["routing"], n + 2)
            nc.vector.tensor_tensor(w_second, w_first, gap_e, ALU.mult).then_inc(s["routing"], 1)
            nc.vector.tensor_tensor(g1, first, over_experts(w_first), ALU.mult).then_inc(s["routing"], 1)
            vec.wait_ge(s["routing"], n + 3)
            nc.vector.tensor_tensor(g2, second, over_experts(w_second), ALU.mult).then_inc(s["routing"], 1)
            vec.wait_ge(s["routing"], n + 5)
            nc.vector.tensor_tensor(g1, g1, g2, ALU.add).then_inc(s["routing"], 1)
            vec.wait_ge(s["routing"], n + 6)
            vec.wait_ge(s["ranks_ready"], 1)
            nc.vector.scalar_tensor_tensor(out=gate[:, :], in0=RANK[:, 0:T * E], scalar=float(CAP),
                                           in1=route[:, 5 * T * E:6 * T * E], op0=ALU.is_lt,
                                           op1=ALU.mult).then_inc(s["gate_ready"], 1)
            vec.wait_ge(s["gate_ready"], 1)
            with vec.Fori(0, T // 4) as i:
                for e, u in ADD_ORDER:
                    if e == 0:
                        vec.wait_ge(s["y_ready"], i * 4 + (u + 1))
                    else:
                        vec.wait_ge(s["added"], i * 16 + (ADD_ORDER.index((e - 1, u)) + 1))
                    x_tile = X[:, bass.ds(i * (4 * P) + u * P, P)]
                    nc.vector.scalar_tensor_tensor(
                        out=x_tile, in0=psum[:, 2 * u * BANK + e * D:2 * u * BANK + (e + 1) * D],
                        scalar=gate[:, bass.ds(i * (4 * E) + (u * E + e), 1)], in1=x_tile,
                        op0=ALU.mult, op1=ALU.add).then_inc(s["added"], 1)

        def weighted_at(i, u, first_expert, experts):
            return arena[:, bass.ds(i * (2 * E * D) + (u * E * D + first_expert * D), experts * D)]

        def top2_scalar(act, s):
            norm_scalar(act, s)
            act.wait_ge(s["gap_ready"], 1)
            nc.scalar.activation(col(4), col(3), ACT.Exp).then_inc(s["gap_exp"], 1)
            act.wait_ge(s["gate_ready"], 1)
            with act.Fori(0, T // 4) as i:
                for u in (0, 1):
                    act.wait_ge(s["y_ready"], i * 4 + (u + 1))
                    for e in range(E):
                        nc.scalar.activation(weighted_at(i, u, e, 1),
                                             psum[:, 2 * u * BANK + e * D:2 * u * BANK + (e + 1) * D], ACT.Copy,
                                             scale=gate[:, bass.ds(i * (4 * E) + (u * E + e), 1)]
                                             ).then_inc(s["weighted"], 1)

        def top2_gpsimd(pool, s):
            with pool.Fori(0, T // 4) as i:
                step = 0
                for experts in (4, 2, 1):
                    for u in (0, 1):
                        if experts == 4:
                            pool.wait_ge(s["weighted"], i * (2 * E) + E * (u + 1))
                        else:
                            pool.wait_ge(s["added_too"], i * 8 + (step - 1))
                        to = weighted_at(i, u, 0, experts)
                        nc.gpsimd.tensor_tensor(to, to, weighted_at(i, u, experts, experts),
                                                ALU.add).then_inc(s["added_too"], 1)
                        step += 1
                for u in (0, 1):
                    pool.wait_ge(s["added_too"], i * 8 + (step - 1))
                    x_tile = X[:, bass.ds(i * (4 * P) + u * P, P)]
                    nc.gpsimd.tensor_tensor(x_tile, x_tile, weighted_at(i, u, 0, 1), ALU.add).then_inc(s["added_too"], 1)
                    step += 1

        QF = arena[:, 0:N]
        KF = arena[:, N:2 * N]
        VF = arena[:, 2 * N:2 * N + T * (D + 1)].rearrange("p (t d) -> p t d", d=D + 1)
        la = 3 * N + 64
        QNEG = arena[:, la:la + 2 * BANK]
        KNEG = arena[:, la + 2 * BANK:la + 4 * BANK]
        KV = arena[:, la + 4 * BANK:la + 4 * BANK + D + H]
        DEN = arena[:, la + 5 * BANK:la + 5 * BANK + 2 * TC * H]
        ON = arena[:, la + 6 * BANK:la + 8 * BANK]
        ONT = arena[:, la + 8 * BANK:la + 10 * BANK]

        def q_bank(c):
            return bank((4, 5, 2, 3)[c])

        def kv_bank(n):
            return bank((6, 7, 0, 1)[n % 4])

        def k_rows(buf):
            return buf.rearrange("p (i x) -> p i x", i=2)[:, :, 0:D]

        def k_neg_of(n):
            return KNEG[:, (n % 4) * 2 * D:(n % 4 + 1) * 2 * D]

        def linear_tensor(pe, s):
            norm_tensor(pe, s)
            pe.wait_ge(w_linear, 16 * 4)
            for c in range(NC):
                pe.wait_ge(xt_ready, s["k"] * NC + c + 1)
                nc.tensor.matmul(q_bank(c), WQKV0[:, 0:D], XT[:, c * BANK:(c + 1) * BANK],
                                 start=True, stop=True).then_inc(s["q_raw"], 1)
                for pair in range(2):
                    n = 2 * c + pair
                    if n >= 4:
                        pe.wait_ge(s["k_done"], n - 3)
                        pe.wait_ge(s["v_done"], n - 3)
                    for i in range(2):
                        t = 2 * n + i
                        mm = nc.tensor.matmul(kv_bank(n)[:, i * 2 * D:(i + 1) * 2 * D],
                                              XT[:, t * P:(t + 1) * P], WQKV0[:, D:3 * D],
                                              start=True, stop=True)
                    mm.then_inc(s["kv_raw"], 1)
            pe.wait_ge(s["q_done"], 1)
            for t in range(T):
                if t % 2 == 0:
                    pe.wait_ge(s["k_done"], t // 2 + 1)
                    pe.wait_ge(s["v_done"], t // 2 + 1)
                mm = nc.tensor.matmul(bank(4)[:, 0:D + 1], KF[:, t * P:(t + 1) * P], VF[:, t, :],
                                      start=(t == 0), stop=(t == T - 1))
            mm.then_inc(s["kv_sum"], 1)

            def numerators(c):
                if c >= 2:
                    pe.wait_ge(s["o_ready"], 2 * (c - 1))
                for i in range(TC):
                    t = c * TC + i
                    at = (i % 2) * (D + H)
                    mm = nc.tensor.matmul(bank(1 + 2 * (c % 2) + i // 2)[:, at:at + D + H], QF[:, t * P:(t + 1) * P],
                                          KV, start=True, stop=True)
                mm.then_inc(s["num_ready"], 1)

            def turn(c):
                pe.wait_ge(s["o_ready"], 2 * (c + 1))
                if c >= 1:
                    pe.wait_ge(s["ot_ready"], c)
                for i in range(TC):
                    at = (c % 2) * BANK + i * P
                    mm = nc.tensor.transpose(bank(5)[:, i * P:(i + 1) * P], ON[:, at:at + P], ident[:, :])
                mm.then_inc(s["o_turned"], 1)

            def project(c):
                pe.wait_ge(s["ot_ready"], c + 1)
                if c >= 2:
                    pe.wait_ge(s["added"], c - 1)
                for i in range(TC):
                    at = (c % 2) * BANK + i * P
                    mm = nc.tensor.matmul(bank(6 + c % 2)[:, i * D:(i + 1) * D], ONT[:, at:at + P],
                                          WO0[:, :], start=True, stop=True)
                mm.then_inc(s["out_ready"], 1)

            pe.wait_ge(s["kv_blocks"], 2)
            pe.wait_ge(s["q_done"], NC)
            numerators(0)
            for c in range(NC):
                if c + 1 < NC:
                    numerators(c + 1)
                turn(c)
                if c >= 1:
                    project(c - 1)
            project(NC - 1)

        def linear_vector(vec, s):
            norm_vector(vec, s)
            nc.vector.memset(VF[:, :, D:D + 1], 1.0).then_inc(s["k_neg"], 1)
            for c in range(NC + 1):
                if c < NC:
                    vec.wait_ge(s["q_raw"], c + 1)
                    if c >= 2:
                        vec.wait_ge(s["q_done"], c - 1)
                    nc.vector.tensor_scalar(QNEG[:, (c % 2) * BANK:(c % 2 + 1) * BANK], q_bank(c), 0.0, None,
                                            ALU.min).then_inc(s["q_neg"], 1)
                    for n in (2 * c, 2 * c + 1):
                        vec.wait_ge(s["kv_raw"], n + 1)
                        if n >= 4:
                            vec.wait_ge(s["k_done"], n - 3)
                        nc.vector.tensor_scalar(k_neg_of(n).rearrange("p (i x) -> p i x", i=2), k_rows(kv_bank(n)),
                                                0.0, None, ALU.min).then_inc(s["k_neg"], 1)
                if c >= 1:
                    b = c - 1
                    vec.wait_ge(s["q_exp"], b + 1)
                    nc.vector.scalar_tensor_tensor(out=QF[:, b * BANK:(b + 1) * BANK], in0=q_bank(b), scalar=0.0,
                                                   in1=QNEG[:, (b % 2) * BANK:(b % 2 + 1) * BANK], op0=ALU.max,
                                                   op1=ALU.add).then_inc(s["q_done"], 1)
                    for n in (2 * b, 2 * b + 1):
                        vec.wait_ge(s["k_exp"], n + 1)
                        vec.wait_ge(s["v_done"], n + 1)
                        nc.vector.scalar_tensor_tensor(
                            out=KF[:, n * 2 * P:(n + 1) * 2 * P].rearrange("p (i x) -> p i x", i=2),
                            in0=k_rows(kv_bank(n)), scalar=0.0,
                            in1=k_neg_of(n).rearrange("p (i x) -> p i x", i=2), op0=ALU.max,
                            op1=ALU.add).then_inc(s["k_done"], 1)
            vec.wait_ge(s["kv_sum"], 1)
            vec.wait_ge(consts_done, CONSTS)
            nc.vector.tensor_tensor(KV[:, 0:D], bank(4)[:, 0:D], block_diag[:, :], ALU.mult).then_inc(s["kv_blocks"], 1)
            nc.vector.tensor_scalar(KV[:, D:].unsqueeze(2), block_diag[:, :].rearrange("p (h d) -> p h d", d=HD)[:, :, 0:1],
                                    bank(4)[:, D:D + 1], None, ALU.mult).then_inc(s["kv_blocks"], 1)
            for c in range(NC + 2):
                if c < NC:
                    den = DEN[:, (c % 2) * TC * H:(c % 2 + 1) * TC * H].rearrange("p (b i h) -> p b i h", b=2, i=2)
                    first = 1 + 2 * (c % 2)
                    both = bank(first, 2).rearrange("p (b x) -> p b x", b=2)[:, :, 0:2 * (D + H)]
                    both = both.rearrange("p b (i y) -> p b i y", i=2)
                    vec.wait_ge(s["num_ready"], c + 1)
                    nc.vector.tensor_scalar(den, both[:, :, :, D:], LA_EPS, None, ALU.add).then_inc(s["norm_chain"], 1)
                    vec.wait_ge(s["norm_chain"], 2 * c + 1)
                    nc.vector.reciprocal(den, den).then_inc(s["norm_chain"], 1)
                    vec.wait_ge(s["norm_chain"], 2 * c + 2)
                    if c >= 2:
                        vec.wait_ge(s["o_turned"], c - 1)
                    for b in range(2):
                        at = (c % 2) * BANK + b * 2 * D
                        nc.vector.tensor_tensor(
                            ON[:, at:at + 2 * D].rearrange("p (i h d) -> p i h d", i=2, h=H),
                            both[:, b, :, 0:D].rearrange("p i (h d) -> p i h d", h=H),
                            den[:, b, :, :].unsqueeze(3).broadcast_to([P, 2, H, HD]), ALU.mult).then_inc(s["o_ready"], 1)
                if c >= 2:
                    b = c - 2
                    vec.wait_ge(s["out_ready"], b + 1)
                    x_chunk = X[:, b * BANK:(b + 1) * BANK]
                    nc.vector.tensor_tensor(x_chunk, bank(6 + b % 2), x_chunk, ALU.add).then_inc(s["added"], 1)

        def linear_scalar(act, s):
            norm_scalar(act, s)
            for c in range(NC):
                qn = QNEG[:, (c % 2) * BANK:(c % 2 + 1) * BANK]
                act.wait_ge(s["q_neg"], c + 1)
                nc.scalar.activation(qn, qn, ACT.Exp).then_inc(s["q_exp"], 1)
                for n in (2 * c, 2 * c + 1):
                    kn = k_neg_of(n)
                    act.wait_ge(s["k_neg"], n + 2)
                    nc.scalar.activation(kn, kn, ACT.Exp).then_inc(s["k_exp"], 1)
                    nc.scalar.activation(VF[:, 2 * n:2 * n + 2, 0:D],
                                         kv_bank(n).rearrange("p (i x) -> p i x", i=2)[:, :, D:2 * D],
                                         ACT.Copy).then_inc(s["v_done"], 1)
            for c in range(NC):
                act.wait_ge(s["o_turned"], c + 1)
                if c >= 2:
                    act.wait_ge(s["out_ready"], c - 1)
                nc.scalar.activation(ONT[:, (c % 2) * BANK:(c % 2 + 1) * BANK], bank(5), ACT.Copy).then_inc(s["ot_ready"], 1)

        B2 = arena[:, 0:E * D]
        o = E * D
        XS_IN = [arena[:, o + u * ROW:o + (u + 1) * ROW] for u in range(4)]
        o += 4 * ROW
        XS = [arena[:, o + u * P:o + (u + 1) * P] for u in range(2)]
        o += 2 * P
        YS = [arena[:, o + u * D:o + (u + 1) * D] for u in range(4)]
        HB = [probs[:, u * HID:(u + 1) * HID] for u in range(2)]
        HG = [probs[:, (2 + u) * HID:(3 + u) * HID] for u in range(2)]
        o = 4 * HID
        W1S = [probs[:, o + u * W1_COLS:o + (u + 1) * W1_COLS] for u in range(2)]
        o += 2 * W1_COLS
        B2S = [probs[:, o + u * D:o + (u + 1) * D] for u in range(4)]
        YG = XT

        def sorted_steps(eng, step):
            for j in range(6):
                step(j, j % 4, True, j)
            with eng.Fori(0, (NT - 8) // 4) as i:
                for j in range(6, 10):
                    step(i * 4 + j, j % 4, False, None)
            for j in range(NT - 2, NT + 1):
                step(j, j % 4, True, j)

        def nth_top1(s):
            return LAYERS[:s["k"] + 1].count("top1")

        def expert_of(eng, j):
            where = tile_expert[0:1, j:j + 1] if isinstance(j, int) else tile_expert[0:1, bass.ds(j, 1)]
            return eng.value_load(where, min_val=0, max_val=E - 1)

        def top1_tensor(pe, s):
            norm_tensor(pe, s)
            logits_tensor(pe, s, WR1)
            ranks_tensor(pe, s)
            pe.wait_ge(s["gate_ready"], 2)
            pe.wait_ge(w_top1, 16 * 5)

            def step(j, u, static, at):
                def exists(lag):
                    return not static or 0 <= at - lag < NT

                def back(lag):
                    return not static or at - lag >= 0
                if exists(-1):
                    v = (u + 1) % 4
                    xs_in = (s["xs_in0"], s["xs_in1"], s["xs_in2"], s["xs_in3"])[v]
                    pe.wait_ge(xs_in, 4 * (j + 1 - v) + 16)
                    if back(1):
                        pe.wait_ge(s["xs_ready"], j)
                    nc.tensor.transpose(bank(v % 2)[:, 0:P], XS_IN[v][:, 0:D], ident[:, :]).then_inc(s["t1_done"], 1)
                if exists(0):
                    pe.wait_ge(s["xs_ready"], j + 1)
                    pe.wait_ge(s["w1_ready"], j + 1)
                    if back(2):
                        pe.wait_ge(s["bias_done"], j - 1)
                    for c in range(HC):
                        mm = nc.tensor.matmul(bank(2 + u % 2)[:, c * P:(c + 1) * P], W1S[u % 2][:, c * P:(c + 1) * P],
                                              XS[u % 2], start=True, stop=True)
                    mm.then_inc(s["h_done"], 1)
                if exists(1):
                    v = (u + 3) % 4
                    e = expert_of(pe, j - 1)
                    pe.wait_ge(s["gelu_done"], j)
                    if back(3):
                        pe.wait_ge(s["y_ready"], j - 2)
                    for c in range(HC):
                        mm = nc.tensor.matmul(bank(6 + v % 2)[:, 0:D], HG[v % 2][:, c * P:(c + 1) * P],
                                              W2[:, bass.ds(e * HID + c * D, D)], start=(c == 0),
                                              stop=(c == HC - 1))
                    mm.then_inc(s["y_done"], 1)

            pe.wait_ge(s["rows_scattered"], 16 * T)
            warm_up(8)
            pe.wait_ge(s["xs_in0"], 16)
            nc.tensor.transpose(bank(0)[:, 0:P], XS_IN[0][:, 0:D], ident[:, :]).then_inc(s["t1_done"], 1)
            sorted_steps(pe, step)

        def top1_vector(vec, s):
            norm_vector(vec, s)
            L, first, work, ranked = te(0), te(2), te(4), te(5)
            top, work_max, slot = col(0), col(2), col(3)
            vec.wait_ge(s["logits_ready"], 1)
            vec.wait_ge(w_top1, 16 * 5)
            nc.vector.tensor_tensor(L, LG.rearrange("p (t e) -> p t e", e=E),
                                    BR1[:, :].unsqueeze(1).broadcast_to([P, T, E]), ALU.add).then_inc(s["routing"], 1)
            vec.wait_ge(s["routing"], 1)
            n = pick(vec, s, 1, L, top, first, work, work_max)
            nc.vector.tensor_copy(mask[:, 0:T * E].rearrange("p (t e) -> p t e", e=E), first).then_inc(s["mask_ready"], 1)
            counts, tiles, tiles_to, slot0 = (plan[:, i * E:(i + 1) * E] for i in range(4))
            vec.wait_ge(s["ranks_ready"], 1)
            nc.vector.tensor_copy(counts, RANK[:, T * E:(T + 1) * E]).then_inc(s["routing"], 1)
            vec.wait_ge(s["routing"], n + 1)
            full = te(6).rearrange("p t e -> p (t e)").rearrange("p (e j) -> p e j", e=E)
            nc.vector.tensor_tensor(full, counts.unsqueeze(2).broadcast_to([P, E, T]),
                                    steps128[:, :].rearrange("p (e j) -> p e j", e=E), ALU.is_gt).then_inc(s["routing"], 1)
            vec.wait_ge(s["routing"], n + 2)
            nc.vector.tensor_reduce(tiles, full, AX.X, ALU.add).then_inc(s["routing"], 1)
            vec.wait_ge(s["routing"], n + 3)
            nc.vector.tensor_tensor_scan(tiles_to, ones8[:, :], tiles, 0.0, ALU.mult, ALU.add).then_inc(s["routing"], 1)
            vec.wait_ge(s["routing"], n + 4)
            nc.vector.tensor_tensor(slot0, tiles_to, tiles, ALU.subtract).then_inc(s["routing"], 1)
            vec.wait_ge(s["routing"], n + 5)
            nc.vector.scalar_tensor_tensor(out=ranked, in0=slot0.unsqueeze(1).broadcast_to([P, T, E]),
                                           scalar=float(P), in1=RANK[:, 0:T * E].rearrange("p (t e) -> p t e", e=E),
                                           op0=ALU.mult, op1=ALU.add).then_inc(s["routing"], 1)
            vec.wait_ge(s["routing"], n + 6)
            nc.vector.tensor_tensor(ranked, ranked, first, ALU.mult).then_inc(s["routing"], 1)
            vec.wait_ge(s["routing"], n + 7)
            nc.vector.tensor_reduce(slot, ranked, AX.X, ALU.add).then_inc(s["routing"], 1)
            vec.wait_ge(s["routing"], n + 8)
            nc.vector.tensor_copy(dest[:, :], slot).then_inc(s["gate_ready"], 1)
            before = plan_big[:, :].rearrange("p (j e) -> p j e", e=E)
            nc.vector.tensor_tensor(before, tiles_to.unsqueeze(1).broadcast_to([P, NT, E]),
                                    tile_no[:, :].rearrange("p (j e) -> p j e", e=E), ALU.is_le).then_inc(s["routing"], 1)
            vec.wait_ge(s["routing"], n + 9)
            ended = small[:, 4 * T:4 * T + NT]
            nc.vector.tensor_reduce(ended, before, AX.X, ALU.add).then_inc(s["routing"], 1)
            vec.wait_ge(s["routing"], n + 10)
            nc.vector.tensor_scalar(tile_expert[:, :], ended, float(E - 1), None, ALU.min).then_inc(s["gate_ready"], 1)
            vec.wait_ge(s["gate_ready"], 2)

            def rows_out(j, v):
                nc.vector.tensor_copy(XS[v % 2], bank(v % 2)[:, 0:P]).then_inc(s["xs_ready"], 1)
                at = slice(j % TOKENS_KEPT, j % TOKENS_KEPT + 1) if isinstance(j, int) else bass.ds(j & (TOKENS_KEPT - 1), 1)
                nc.vector.tensor_copy(slot_token[:, at], XS_IN[v][:, D:]).then_inc(s["tokens_ready"], 1)

            def step(j, u, static, at):
                def exists(lag):
                    return not static or 0 <= at - lag < NT

                def back(lag):
                    return not static or at - lag >= 0
                if exists(-1):
                    v = (u + 1) % 4
                    vec.wait_ge(s["t1_done"], j + 2)
                    if back(1):
                        vec.wait_ge(s["h_done"], j)
                    rows_out(j + 1, v)
                if exists(0):
                    vec.wait_ge(s["h_done"], j + 1)
                    vec.wait_ge(s["w1_ready"], j + 1)
                    if back(2):
                        vec.wait_ge(s["gelu_done"], j - 1)
                    hidden = bank(2 + u % 2).rearrange("p (c n) -> p c n", c=HC)
                    bias = W1S[u % 2][:, HID:].unsqueeze(2).broadcast_to([P, HC, P])
                    nc.vector.tensor_tensor(HB[u % 2].rearrange("p (c n) -> p c n", c=HC), hidden, bias,
                                            ALU.add).then_inc(s["bias_done"], 1)
                if exists(1):
                    v = (u + 3) % 4
                    vec.wait_ge(s["y_done"], j)
                    vec.wait_ge(s["b2_ready"], j)
                    if back(5):
                        ys_out = (s["ys_out0"], s["ys_out1"], s["ys_out2"], s["ys_out3"])[v]
                        vec.wait_ge(ys_out, 4 * (j - 1 - v))
                    nc.vector.scalar_tensor_tensor(out=YS[v], in0=bank(6 + v % 2)[:, 0:D], scalar=0.5, in1=B2S[v],
                                                   op0=ALU.mult, op1=ALU.add).then_inc(s["y_ready"], 1)

            vec.wait_ge(s["t1_done"], 1)
            rows_out(0, 0)
            sorted_steps(vec, step)
            add_outputs(vec, nc.vector, s, 0, s["added"])

        def add_outputs(eng, engine, s, first, added):
            for c in range(NC):
                eng.wait_ge(y_in[c], 16 * nth_top1(s))
                for i in (0, 1, 2) if first == 0 else (3,):
                    t = c * TC + i
                    x_tile = X[:, t * P:(t + 1) * P]
                    engine.tensor_tensor(x_tile, x_tile, YG[:, t * P:(t + 1) * P], ALU.add).then_inc(added, 1)
                if first == 0 and c >= 1:
                    chunk_stats(eng, s["k"] + 1, c - 1)
            if first == 0:
                chunk_stats(eng, s["k"] + 1, NC - 1)

        def top1_scalar(act, s):
            norm_scalar(act, s)

            def weights_out(j, v):
                e = expert_of(act, j)
                nc.scalar.activation(W1S[v % 2], W1[:, bass.ds(e * W1_COLS, W1_COLS)], ACT.Copy).then_inc(s["w1_ready"], 1)
                nc.scalar.activation(B2S[v % 4], B2[:, bass.ds(e * D, D)], ACT.Copy, scale=0.5).then_inc(s["b2_ready"], 1)

            def step(j, u, static, at):
                def exists(lag):
                    return not static or 0 <= at - lag < NT

                def back(lag):
                    return not static or at - lag >= 0
                if exists(-1):
                    if back(1):
                        act.wait_ge(s["h_done"], j)
                        act.wait_ge(s["bias_done"], j)
                    if back(3):
                        act.wait_ge(s["y_ready"], j - 2)
                    weights_out(j + 1, u + 1)
                if exists(0):
                    act.wait_ge(s["bias_done"], j + 1)
                    if back(2):
                        act.wait_ge(s["y_done"], j - 1)
                    nc.scalar.activation(HG[u % 2], HB[u % 2], ACT.Gelu).then_inc(s["gelu_done"], 1)

            act.wait_ge(s["gate_ready"], 2)
            act.wait_ge(w_top1, 16 * 5)
            act.wait_ge(s["bias_in"], 16)
            weights_out(0, 0)
            sorted_steps(act, step)

        def top1_gpsimd(pool, s):
            pool.wait_ge(stats_done, (s["k"] + 1) * T)
            rows = arena[:, ROWS_AT:ROWS_AT + T * ROW].rearrange("p (t r) -> p t r", r=ROW)
            nc.gpsimd.tensor_copy(rows[:, :, D:], row_no[:, 0:T].unsqueeze(2)).then_inc(s["pool_steps"], 1)
            pool.wait_ge(s["gate_ready"], 1)
            pool.wait_ge(s["pool_steps"], 1)
            wait_normed(pool, s, T)
            pool.wait_ge(zero_rows_done, 16 * len(sorted_in))
            for t in range(T):
                nc.gpsimd.indirect_dma_start(sorted_in[s["k"]], bass.IndirectOffsetOnAxis(dest[:, t:t + 1], 0),
                                             rows[:, t, :], None).then_inc(s["rows_scattered"], 16)
            for j in range(NT):
                at = j % TOKENS_KEPT
                pool.wait_ge(s["tokens_ready"], j + 1)
                pool.wait_ge(s["y_ready"], j + 1)
                nc.gpsimd.indirect_dma_start(y_dram, bass.IndirectOffsetOnAxis(slot_token[:, at:at + 1], 0),
                                             YS[j % 4], None).then_inc(s[f"ys_out{j % 4}"], 16)
            add_outputs(pool, nc.gpsimd, s, 3, s["pool_steps"])

        def top1_sync(sp, s):
            wait_x(sp, s["k"], T - 1)
            sp.dma_start(B2, b21.partition_broadcast(P)).then_inc(s["bias_in"], 16)
            sp.wait_ge(s["rows_scattered"], 16 * T)
            xs_in = (s["xs_in0"], s["xs_in1"], s["xs_in2"], s["xs_in3"])
            rows = sorted_in[s["k"]]
            for u in range(4):
                sp.dma_start(XS_IN[u], rows[u * P:(u + 1) * P, :]).then_inc(xs_in[u], 16)
            with sp.Fori(1, NT // 4) as i:
                for u in range(4):
                    sp.wait_ge(s["t1_done"], i * 4 + (u - 3))
                    sp.wait_ge(s["tokens_ready"], i * 4 + (u - 3))
                    sp.dma_start(XS_IN[u], rows[bass.ds(i * (4 * P) + u * P, P), :]).then_inc(xs_in[u], 16)
            for u in range(4):
                sp.wait_ge(s[f"ys_out{u}"], 16 * (NT // 4))
            sp.wait_ge(s["logits_ready"], 1)
            for c in range(NC):
                sp.dma_start(YG[:, c * BANK:(c + 1) * BANK].rearrange("p (t d) -> p t d", d=D),
                             y_dram[c * BANK:(c + 1) * BANK, :].rearrange("(t p) d -> p t d", p=P)).then_inc(y_in[c], 16)

        GCOLS = GH * 2 * N
        QS = arena[:, 0:GCOLS // 2].bitcast(BF16)
        KS = arena[:, GCOLS // 2:GCOLS].bitcast(BF16)
        PARTS = [osb[:, i * 3 * N // 2:(i + 1) * 3 * N // 2].bitcast(BF16) for i in range(2)]
        REST = probs
        vcur = VCUR[:, :].rearrange("p (b t h c) -> p b t h c", b=2, t=KEY_TILES, h=GH)
        VHALF = KEY_TILES * GH * 32
        halves = sb("halves", [P, SLOTS])
        minus_max = sb("minus_max", [P, GH * TC])
        shift_parts = sb("shift_parts", [GH * TC, 2 * P], BF16)
        warm_exp = sb("warm_exp", [P, E])
        AO = XN
        AOT = XT
        recips = sb("recips", [P, 2 * GH * TC])

        def side_of(n):
            return 1 - n // NC

        def parts_of(n):
            c = n % NC
            return PARTS[side_of(n)].rearrange("p (a n) -> p a n", a=3)[:, :, c * BANK:(c + 1) * BANK]

        def rest_of(n):
            return REST[:, (n % 2) * BANK:(n % 2 + 1) * BANK]

        def bias_of(n):
            return QKV_BIAS[:, side_of(n):side_of(n) + 1]

        def q_at(u):
            return (u & 7) * (GH * BANK)

        def k_at(u):
            return ((u >> 2) & 1) * N

        def cols(buf, rows, base, at, n):
            if isinstance(at, int):
                return buf[0:rows, base + at:base + at + n]
            return buf[0:rows, bass.ds(at + base, n)]

        def cols_from(rows, at, n):
            return rows[:, at:at + n] if isinstance(at, int) else rows[:, bass.ds(at, n)]

        def turn_on_tensor(pe, s, u, more):
            pe.wait_ge(s["max_ready"], u + 1)
            if more:
                pe.wait_ge(s["max_read"], (u + 1) * SLOTS + 1)
            nc.tensor.transpose(bank(3)[0:GH * TC, 0:P], minus_max[:, :], ident[:, :]).then_inc(s["max_turned"], 1)

        HEAD_IN = 16 * (3 + 1)
        REST_IN = 16 * (NC - 1) * GH
        GROUP_IN = 16 * (3 + NC) * GH

        def group_in(u):
            return (u >> 2) * GROUP_IN + REST_IN

        def max_matmuls(pe, s, u, slot):
            head, tile, half = slot // (2 * TC), (slot // 2) % TC, slot % 2
            first = isinstance(u, int) and u == 0
            second = isinstance(u, int) and u == 1
            for part in range(2):
                if part == 0:
                    if first and slot % (2 * TC) == 0:
                        pe.wait_ge(s[f"first_head_in{head}"], HEAD_IN)
                    if slot == 0 and not first:
                        pe.wait_ge(s["group_in"], group_in(u))
                    if slot >= 2 or not first:
                        pe.wait_ge(s["max_read"], u * SLOTS + (slot - 1))
                    if slot == (0 if second else 2) and not first:
                        pe.wait_ge(s["shift_split"], u)
                mm = nc.tensor.matmul(bank(3 + 2 * (slot % 2) + part),
                                      cols(QS, KROWS, head * BANK + tile * P, q_at(u), P),
                                      cols(KS, KROWS, head * 2 * N + (2 * half + part) * BANK, k_at(u), BANK),
                                      start=True, stop=True)
                if part == 1:
                    mm.then_inc(s["max_raw"], 1)
                yield

        OUT_STEPS = GH + 1

        def turn_outputs(pe, s, c, g):
            n = c * GH + g
            pe.wait_ge(s["o_bank_free"], g * NC + c + 2)
            if n >= 2:
                pe.wait_ge(s["o_scaled"], n - 1)
            for i in range(TC):
                at = (g * NC + c) * BANK + i * P
                mm = nc.tensor.transpose(bank(3 + n % 2)[:, i * P:(i + 1) * P], osb[:, at:at + P], ident[:, :])
            mm.then_inc(s["o_turned"], 1)

        def turn_heads(pe, s, c):
            pe.wait_ge(s["o_scaled"], (c + 1) * GH)
            if c >= 1:
                pe.wait_ge(s["a_ready"], c)
            for i in range(TC):
                t = c * TC + i
                mm = nc.tensor.transpose(bank(5)[:, i * P:(i + 1) * P], AO[:, t * P:(t + 1) * P], ident[:, :])
            mm.then_inc(s["a_turned"], 1)

        def project_chunk(pe, s, c):
            pe.wait_ge(s["a_ready"], c + 1)
            if c >= 1:
                pe.wait_ge(s["added"], c)
            for i in range(TC):
                t = c * TC + i
                mm = nc.tensor.matmul(bank(6)[:, i * D:(i + 1) * D], AOT[:, t * P:(t + 1) * P],
                                      WO1[:, :], start=True, stop=True)
            mm.then_inc(s["out_ready"], 1)

        def output_step(pe, s, at):
            c, g = at // OUT_STEPS, at % OUT_STEPS
            if g == 1 and c >= 1:
                project_chunk(pe, s, c - 1)
            if g == 0 and c >= 1:
                turn_heads(pe, s, c - 1)
            if g < GH and c < NC:
                turn_outputs(pe, s, c, g)

        def softmax_tensor(pe, s):
            norm_tensor(pe, s)
            pe.wait_ge(w_softmax, 16 * 8)
            for i, side in enumerate((1, 0)):
                for c in range(NC):
                    n = i * NC + c
                    pe.wait_ge(xt_ready, s["k"] * NC + c + 1)
                    if n >= 2:
                        pe.wait_ge(s["part1"], n - 1)
                        pe.wait_ge(s["rest1"], n - 1)
                    nc.tensor.matmul(bank(4 + n % 2), WQKV1[:, side * D:(side + 1) * D],
                                     XT[:, c * BANK:(c + 1) * BANK], start=True, stop=True).then_inc(s["proj_raw"], 1)
            for c in range(NC):
                if c >= 2:
                    pe.wait_ge(s["v_all"], c - 1)
                for i in range(TC):
                    t = c * TC + i
                    mm = nc.tensor.matmul(bank(6 + c % 2)[:, i * D:(i + 1) * D], XT[:, t * P:(t + 1) * P],
                                          WQKV1[:, 2 * D:3 * D], start=True, stop=True)
                mm.then_inc(s["v_raw"], 1)

            def scores(n, kt, j):
                i = kt * GH + j
                if i == 0:
                    pe.wait_ge(s["shift_in"], (n + 1) * 32)
                    if not (isinstance(n, int) and n == 0):
                        pe.wait_ge(s["exp_done"], n * STEPS)
                if i >= 3:
                    pe.wait_ge(s["exp_done"], n * STEPS + (i - 2))
                nc.tensor.matmul(bank(i % 3),
                                 cols(KS, KFULL, j * 2 * N + kt * P, k_at(n), P),
                                 cols(QS, KFULL, j * BANK, q_at(n), BANK), start=True,
                                 stop=True).then_inc(s["score_ready"], 1)
            def values(n, kt, parity):
                pe.wait_ge(s["exp_done"], n * STEPS + GH * (kt + 1))
                if kt == 0:
                    pe.wait_ge(s["v_cur"], n + 1)
                    pe.wait_ge(s["o_bank_free"], n + 1)
                for j in range(GH):
                    slot = (kt * GH + j) % RING
                    mm = nc.tensor.matmul(bank(7)[32 * j:32 * j + 32, :], vcur[:, parity, kt, j, :],
                                          probs[:, slot * BANK:(slot + 1) * BANK], start=(kt == 0),
                                          stop=(kt == KEY_TILES - 1))
                mm.then_inc(s["pv_done"], 1)

            def unit(n, parity, maxima, next_maxima):
                late = AHEAD - FIRST_AHEAD if isinstance(n, int) and n == 0 else 0
                catch_up = (SLOTS - AHEAD) // 2

                def slots_before(kt):
                    return AHEAD + 2 * kt - late * max(catch_up - kt, 0) // catch_up

                for kt in range(KEY_TILES):
                    slot = slots_before(kt)
                    fill = []
                    for at in range(slot, slots_before(kt + 1)):
                        if maxima and at < SLOTS:
                            fill.append(max_matmuls(pe, s, n + 1, at))
                        if next_maxima and at >= SLOTS:
                            fill.append(max_matmuls(pe, s, n + 2, at - SLOTS))
                    turn = maxima and slot == SLOTS
                    values_after = 1 if turn else GH - 1 if maxima else GH - 2
                    for j in range(GH):
                        scores(n, kt, j)
                        if turn and j == GH - 1:
                            turn_on_tensor(pe, s, n + 1, next_maxima)
                        for part in range(2 * len(fill) * j // GH, 2 * len(fill) * (j + 1) // GH):
                            next(fill[part // 2])
                        if j == values_after:
                            if kt >= 1:
                                values(n, kt - 1, parity)
                            elif not (isinstance(n, int) and n == 0):
                                values(n - 1, KEY_TILES - 1, 1 - parity)
                    if not maxima:
                        output_step(pe, s, kt)

            for half_read in ("part1", "rest1"):
                pe.wait_ge(s[half_read], 2 * NC)
            pe.wait_ge(s["v_all"], NC - 1)
            pe.wait_ge(s["o_bank_free"], 1)
            for slot in range(SLOTS):
                for _ in max_matmuls(pe, s, 0, slot):
                    pass
            turn_on_tensor(pe, s, 0, False)
            for slot in range(FIRST_AHEAD):
                for _ in max_matmuls(pe, s, 1, slot):
                    pass
            unit(0, 0, True, True)
            with pe.Fori(0, UNITS // 4 - 1) as m:
                for u in range(1, 5):
                    unit(m * 4 + u, u % 2, True, True)
            unit(UNITS - 3, 1, True, True)
            unit(UNITS - 2, 0, True, False)
            pe.wait_ge(s["shift_split"], UNITS)
            pe.wait_ge(s["max_read"], UNITS * SLOTS)
            unit(UNITS - 1, 1, False, False)
            values(UNITS - 1, KEY_TILES - 1, 1)
            for at in range(KEY_TILES, OUT_STEPS * NC + 2):
                output_step(pe, s, at)

        def softmax_vector(vec, s):
            norm_vector(vec, s)
            for n in range(2 * NC + 1):
                if n < 2 * NC:
                    vec.wait_ge(s["part1"], n + 1)
                    if n >= 2:
                        vec.wait_ge(s["part3"], n - 1)
                    nc.vector.scalar_tensor_tensor(out=rest_of(n), in0=bank(4 + n % 2), scalar=bias_of(n),
                                                   in1=parts_of(n)[:, 0, :], op0=ALU.add,
                                                   op1=ALU.subtract).then_inc(s["rest1"], 1)
                if n >= 1:
                    vec.wait_ge(s["part2"], n)
                    nc.vector.tensor_tensor(parts_of(n - 1)[:, 2, :], rest_of(n - 1), parts_of(n - 1)[:, 1, :],
                                            ALU.subtract).then_inc(s["part3"], 1)

            def read_max(u, slot):
                if slot == 0 and not (isinstance(u, int) and u == 0):
                    vec.wait_ge(s["max_ready"], u)
                vec.wait_ge(s["max_raw"], u * SLOTS + (slot + 1))
                nc.vector.tensor_reduce(halves[:, slot:slot + 1], bank(3 + 2 * (slot % 2), 2), AX.X,
                                        ALU.max).then_inc(s["max_read"], 1)

            def join_halves(u):
                vec.wait_ge(s["max_read"], (u + 1) * SLOTS)
                nc.vector.tensor_reduce(minus_max[:, :], halves[:, :].rearrange("p (m h) -> p m h", h=2), AX.X,
                                        ALU.max, negate=True).then_inc(s["max_ready"], 1)

            def split_shift(u):
                vec.wait_ge(s["max_turned"], u + 1)
                if not (isinstance(u, int) and u == 0):
                    vec.wait_ge(s["shift_in"], u * 32)
                nc.vector.tensor_copy(shift_parts[:, 0:P], bank(3)[0:GH * TC, 0:P]).then_inc(s["rest1"], 1)
                vec.wait_ge(s["rest1"], 2 * NC + u + 1)
                nc.vector.tensor_tensor(shift_parts[:, P:2 * P], bank(3)[0:GH * TC, 0:P], shift_parts[:, 0:P],
                                        ALU.subtract).then_inc(s["shift_split"], 1)

            def unit(n, next_maxima):
                for slot in range(AHEAD, SLOTS):
                    read_max(n + 1, slot)
                join_halves(n + 1)
                if next_maxima:
                    read_max(n + 2, 0)
                split_shift(n + 1)
                if next_maxima:
                    for slot in range(1, AHEAD):
                        read_max(n + 2, slot)

            for slot in range(SLOTS):
                read_max(0, slot)
            join_halves(0)
            split_shift(0)
            for slot in range(AHEAD):
                read_max(1, slot)
            with vec.Fori(0, UNITS - 2) as n:
                unit(n, True)
            unit(UNITS - 2, False)

            vec.wait_ge(s["v_cur"], UNITS)
            for c in range(NC):
                if c == 1:
                    vec.wait_ge(s["bo_added"], T)
                for g in range(H // GH):
                    if g == 2 and c >= 1:
                        add_chunk(vec, s, c - 1)
                    n = c * GH + g
                    r = recips[:, (n % 2) * GH * TC:(n % 2 + 1) * GH * TC].rearrange("p (i j) -> p i j", i=TC)
                    turned = bank(3 + n % 2).rearrange("p (i j r) -> p i j r", i=TC, j=GH)
                    vec.wait_ge(s["o_turned"], n + 1)
                    nc.vector.reciprocal(r, turned[:, :, :, HD]).then_inc(s["o_recip"], 1)
                    vec.wait_ge(s["o_recip"], n + 1)
                    ao = AO[:, c * BANK:(c + 1) * BANK].rearrange("p (i g j d) -> p i g j d", i=TC, g=H // GH, j=GH)
                    nc.vector.tensor_tensor(ao[:, :, g, :, :], turned[:, :, :, 0:HD],
                                            r.unsqueeze(3).broadcast_to([P, TC, GH, HD]), ALU.mult).then_inc(s["o_scaled"], 1)
            add_chunk(vec, s, NC - 1)

        def add_chunk(vec, s, c):
            vec.wait_ge(s["out_ready"], c + 1)
            x_chunk = X[:, c * BANK:(c + 1) * BANK]
            nc.vector.tensor_tensor(x_chunk, bank(6), x_chunk, ALU.add).then_inc(s["added"], 1)
            chunk_stats(vec, s["k"] + 1, c)

        def softmax_scalar(act, s):
            norm_scalar(act, s)
            if sorted_in:
                act.wait_ge(zero_rows_done, 16 * len(sorted_in))
            for n in range(2 * NC + 1):
                if n < 2 * NC:
                    act.wait_ge(s["proj_raw"], n + 1)
                    nc.scalar.activation(parts_of(n)[:, 0, :], bank(4 + n % 2), ACT.Identity,
                                         bias=bias_of(n)).then_inc(s["part1"], 1)
                if n >= 1:
                    act.wait_ge(s["rest1"], n)
                    nc.scalar.activation(parts_of(n - 1)[:, 1, :], rest_of(n - 1), ACT.Copy).then_inc(s["part2"], 1)
            for c in range(NC):
                act.wait_ge(s["v_raw"], c + 1)
                nc.scalar.activation(VALL[:, c * BANK:(c + 1) * BANK], bank(6 + c % 2),
                                     ACT.Copy).then_inc(s["v_all"] if c < NC - 1 else s["o_bank_free"], 1)

            def keep_outputs(n):
                act.wait_ge(s["pv_done"], (n + 1) * KEY_TILES)
                to = osb[:, n * BANK:(n + 1) * BANK] if isinstance(n, int) else osb[:, bass.ds(n * BANK, BANK)]
                nc.scalar.activation(to, bank(7), ACT.Copy).then_inc(s["o_bank_free"], 1)

            def unit(n, last):
                first = isinstance(n, int) and n == 0
                for i in range(STEPS):
                    kt = i // GH
                    act.wait_ge(s["score_ready"], n * STEPS + (i + 1))
                    if i % GH == 0 and not (first and kt < RING // GH):
                        act.wait_ge(s["pv_done"], n * KEY_TILES + (kt - RING // GH + 1))
                    slot = i % RING
                    nc.scalar.activation(probs[:, slot * BANK:(slot + 1) * BANK], bank(i % 3), ACT.Exp,
                                         scale=SCALE).then_inc(s["exp_done"], 1)
                    if i == GH - 1 and not first:
                        keep_outputs(n - 1)
                    if last and i % GH == GH - 1 and kt % OUT_STEPS == 0 and kt > 0:
                        heads_out(kt // OUT_STEPS - 1)

            def heads_out(c):
                act.wait_ge(s["a_turned"], c + 1)
                nc.scalar.activation(AOT[:, c * BANK:(c + 1) * BANK], bank(5), ACT.Identity,
                                     bias=QKV_BIAS[:, 2:3]).then_inc(s["a_ready"], 1)

            nc.scalar.activation(warm_exp[:, :], ones8[:, :], ACT.Exp).then_inc(s["exp_loaded"], 1)
            act.wait_ge(s["part3"], 2 * NC)
            unit(0, False)
            with act.Fori(1, UNITS - 1) as n:
                unit(n, False)
            unit(UNITS - 1, True)
            keep_outputs(UNITS - 1)
            heads_out(NC - 1)

        def softmax_pads(pool, s):
            for before in S[:s["k"]]:
                if before["kind"] == "linear":
                    pool.wait_ge(before["added"], NC)
            pool.wait_ge(consts_done, CONSTS)
            nc.gpsimd.memset(KS[PAD_FROM:KFULL, :], 1.0).then_inc(s["pads_done"], 1)
            pool.wait_ge(s["pads_done"], 1)
            nc.gpsimd.memset(VCUR[:, :], 0.0).then_inc(s["pads_done"], 1)
            pool.wait_ge(s["pads_done"], 2)
            nc.gpsimd.memset(VCUR[:, :].rearrange("p (a c) -> p a c", c=32)[:, :, HD:HD + 1], 1.0).then_inc(s["pads_done"], 1)

        def softmax_gpsimd(pool, s):
            v_heads = VALL[:, :].rearrange("p (t g h d) -> p t g h d", t=T, g=H // GH, h=GH)
            pool.wait_ge(s["v_all"], NC - 1)
            pool.wait_ge(s["o_bank_free"], 1)
            pool.wait_ge(s["pads_done"], 3)
            for n in range(2):
                nc.gpsimd.tensor_copy(vcur[:, n, :, :, 0:HD], v_heads[:, :, 0, :, :]).then_inc(s["v_cur"], 1)
            wait_normed(pool, s, T)
            for t in range(T):
                x_tile = X[:, t * P:(t + 1) * P]
                nc.gpsimd.tensor_tensor(x_tile, x_tile, BO1[:, :], ALU.add).then_inc(s["bo_added"], 1)
            with pool.Fori(0, UNITS - 2) as n:
                pool.wait_ge(s["pv_done"], (n + 1) * KEY_TILES)
                source = VALL[:, :].rearrange("p (t c) -> p t c", t=T)[:, :, bass.ds((((n + 2) >> 2) & 3) * (GH * HD), GH * HD)]
                source = source.rearrange("p t (h d) -> p t h d", h=GH)
                to = VCUR[:, bass.ds((n & 1) * VHALF, VHALF)].rearrange("p (t h c) -> p t h c", t=KEY_TILES, h=GH)
                nc.gpsimd.tensor_copy(to[:, :, :, 0:HD], source).then_inc(s["v_cur"], 1)

        def softmax_sync(sp, s):
            def parts_out(n):
                c = n % NC
                sp.wait_ge(s["part2"], n + 1)
                sp.wait_ge(s["part3"], n + 1)
                if n < NC:
                    sp.dma_start(k_dram.rearrange("a f n -> f a n")[:, :, c * BANK:(c + 1) * BANK],
                                 parts_of(n)).then_inc(s["parts_out"], 16)
                else:
                    for a in range(3):
                        sp.dma_start(q_dram[:, a, :, c * BANK:(c + 1) * BANK],
                                     parts_of(n)[:, a, :]).then_inc(s["parts_out"], 16)

            def load_k(g, j, done):
                for i in range(3):
                    rows = slice(i * 3 * HD, (i + 1) * 3 * HD)
                    part = bass.AP(k_dram.tensor, (i * D + (g * GH + j) * HD) * N, [[0, 3], [N, HD], [1, N]])
                    at = j * 2 * N + (g % 2) * N
                    sp.dma_start(KS[rows, at:at + N], part).then_inc(done, 16)

            def load_q(g, j, c, done):
                at = (((g % 2) * NC + c) * GH + j) * BANK
                head = bass.AP(q_dram.tensor, (g * GH + j) * 3 * HD * N + c * BANK, [[0, 3], [N, 3 * HD], [1, BANK]])
                sp.dma_start(QS[0:KROWS, at:at + BANK], head).then_inc(done, 16)

            def load_heads(g, heads):
                for j in heads:
                    load_k(g, j, s["group_in"])
                    for c in range(NC):
                        load_q(g, j, c, s["group_in"])

            def put_shift(u, place):
                sp.wait_ge(s["shift_split"], u + 1)
                for part in range(2):
                    row = KROWS + part
                    sp.dma_start(cols_from(QS[row:row + 1, :], place * (GH * BANK), GH * BANK),
                                 shift_parts[:, part * P:(part + 1) * P]).then_inc(s["shift_in"], 16)

            for n in range(NC + 1):
                parts_out(n)
            sp.wait_ge(s["parts_out"], 16 * (NC + 3))
            sp.wait_ge(s["pads_done"], 3)
            for j in range(GH):
                load_k(0, j, s[f"first_head_in{j}"])
                load_q(0, j, 0, s[f"first_head_in{j}"])
            for n in range(NC + 1, 2 * NC):
                parts_out(n)
            sp.wait_ge(s["parts_out"], 16 * 4 * NC)
            for j in range(GH):
                for c in range(1, NC):
                    load_q(0, j, c, s["group_in"])
            put_shift(0, 0)
            sp.wait_ge(s["group_in"], group_in(0))
            load_heads(1, (0, 1))
            put_shift(1, 1)
            load_heads(1, (2, 3))
            with sp.Fori(2, GH + 1) as u:
                put_shift(u, u)
            for g in range(2, H // GH):
                sp.wait_ge(s["group_in"], group_in(GH * (g - 1)))
                sp.wait_ge(s["pv_done"], (g - 1) * NC * KEY_TILES)
                load_heads(g, (0, 1))
                put_shift((g - 1) * NC + 1, ((g - 1) * NC + 1) % 8)
                load_heads(g, (2, 3))
                for u in range((g - 1) * NC + 2, g * NC + 1):
                    put_shift(u, u % 8)
            for u in range(UNITS - 3, UNITS):
                put_shift(u, u % 8)

        tensor_of = {"top2": top2_tensor, "linear": linear_tensor, "top1": top1_tensor, "softmax": softmax_tensor}
        vector_of = {"top2": top2_vector, "linear": linear_vector, "top1": top1_vector, "softmax": softmax_vector}
        scalar_of = {"top2": top2_scalar, "linear": linear_scalar, "top1": top1_scalar, "softmax": softmax_scalar}

        block = ctx.enter_context(nc.Block())

        @block.sync
        def _(sp):
            x_rows = x_in.rearrange("a (t p) d -> p (a t) d", p=P)
            X3 = X[:, :].rearrange("p (t d) -> p t d", d=D)
            for c in range(NC):
                sp.dma_start(X3[:, c * TC:(c + 1) * TC, :], x_rows[:, c * TC:(c + 1) * TC, :]).then_inc(x_loaded[c], 16)
            sp.dma_start(WR0[:, :], wr0).then_inc(w_router, 16)
            sp.dma_start(WE0[:, :].rearrange("p (e f) -> p e f", e=E), we0.rearrange("e d f -> d e f")).then_inc(w_top2, 16)
            for i, w in enumerate((wq0, wk0, wv0)):
                sp.dma_start(WQKV0[:, i * D:(i + 1) * D], w).then_inc(w_linear, 16)
            sp.dma_start(WO0[:, :], wo0).then_inc(w_linear, 16)
            sp.dma_start(WR1[:, :], wr1).then_inc(w_top1, 16)
            sp.dma_start(BR1[:, :], br1.partition_broadcast(P)).then_inc(w_top1, 16)
            w1_table = W1[:, :].rearrange("p (e h) -> p e h", e=E)
            sp.dma_start(w1_table[:, :, 0:HID], w11.rearrange("e d h -> d e h")).then_inc(w_top1, 16)
            sp.dma_start(w1_table[:, :, HID:], b11.rearrange("p (e c) -> p e c", e=E)).then_inc(w_top1, 16)
            sp.dma_start(W2[:, :].rearrange("p (a d) -> p a d", d=D), w21.rearrange("e (c p) d -> p (e c) d", p=P)).then_inc(w_top1, 16)
            for i, w in enumerate((wq1, wk1, wv1)):
                sp.dma_start(WQKV1[:, i * D:(i + 1) * D], w).then_inc(w_softmax, 16)
            sp.dma_start(WO1[:, :], wo1).then_inc(w_softmax, 16)
            for i, b in enumerate((bq1, bk1, bv1)):
                sp.dma_start(QKV_BIAS[:, i:i + 1], b).then_inc(w_softmax, 16)
            sp.dma_start(BO1[:, :], bo1.partition_broadcast(P)).then_inc(w_softmax, 16)
            sp.wait_ge(blank_rows_ready, 2)
            for rows in sorted_in.values():
                sp.dma_start(rows.rearrange("(j p) c -> p j c", p=P), blank_rows).then_inc(zero_rows_done, 16)
            for s in S:
                if s["kind"] == "top1":
                    top1_sync(sp, s)
                if s["kind"] == "softmax":
                    softmax_sync(sp, s)
            out_rows = out.rearrange("a (t p) d -> p (a t) d", p=P)
            for c in range(NC):
                wait_x(sp, len(LAYERS), (c + 1) * TC - 1)
                sp.dma_start(out_rows[:, c * TC:(c + 1) * TC, :], X3[:, c * TC:(c + 1) * TC, :]).then_inc(out_stored, 16)
            sp.wait_ge(out_stored, 16 * NC)

        @block.gpsimd
        def _(pool):
            nc.gpsimd.memset(ident[:, :], 0.0).then_inc(consts_done, 1)
            nc.gpsimd.memset(upper[:, :], 1.0).then_inc(consts_done, 1)
            nc.gpsimd.memset(ones[:, :], 1.0).then_inc(consts_done, 1)
            nc.gpsimd.memset(block_diag[:, :], 1.0).then_inc(consts_done, 1)
            nc.gpsimd.memset(ones8[:, :], 1.0).then_inc(consts_done, 1)
            nc.gpsimd.memset(mask[:, T * E:], 0.0).then_inc(consts_done, 1)
            for e in range(E):
                nc.gpsimd.memset(desc[:, :].rearrange("p (t e) -> p t e", e=E)[:, :, e:e + 1],
                                 float(E - e)).then_inc(consts_done, 1)
            pool.wait_ge(consts_done, 14)
            nc.gpsimd.affine_select(out=ident[:, :], in_=ident[:, :], compare_op=ALU.not_equal, fill=1.0, base=0,
                                    pattern=[[-1, P]], channel_multiplier=1).then_inc(consts_done, 1)
            nc.gpsimd.affine_select(out=upper[:, :], in_=upper[:, :], compare_op=ALU.is_gt, fill=0.0, base=0,
                                    pattern=[[1, P]], channel_multiplier=-1).then_inc(consts_done, 1)
            blocks = block_diag[:, :].rearrange("p (h d) -> p h d", d=HD)
            nc.gpsimd.affine_select(out=blocks, in_=blocks, compare_op=ALU.is_ge, fill=0.0, base=0,
                                    pattern=[[-HD, H], [0, HD]], channel_multiplier=1).then_inc(consts_done, 1)
            pool.wait_ge(consts_done, 17)
            nc.gpsimd.affine_select(out=blocks, in_=blocks, compare_op=ALU.is_ge, fill=0.0, base=HD - 1,
                                    pattern=[[HD, H], [0, HD]], channel_multiplier=-1).then_inc(consts_done, 1)
            iota_a = route[:, 0:E * T].bitcast(I32)
            iota_b = plan_big[:, :].bitcast(I32)
            nc.gpsimd.iota(iota_a.rearrange("p (e j) -> p e j", e=E), [[0, E], [P, T]], base=0,
                           channel_multiplier=0).then_inc(consts_done, 1)
            nc.gpsimd.iota(iota_b.rearrange("p (j e) -> p j e", e=E), [[1, NT], [0, E]], base=0,
                           channel_multiplier=0).then_inc(consts_done, 1)
            iota_c = route[:, E * T:E * T + T + NT].bitcast(I32)
            nc.gpsimd.iota(iota_c, [[P, T + NT]], base=0, channel_multiplier=1).then_inc(consts_done, 1)
            pool.wait_ge(consts_done, 21)
            nc.gpsimd.tensor_copy(steps128[:, :], iota_a).then_inc(consts_done, 1)
            nc.gpsimd.tensor_copy(tile_no[:, :], iota_b).then_inc(consts_done, 1)
            nc.gpsimd.tensor_copy(row_no[:, :], iota_c).then_inc(consts_done, 1)
            pool.wait_ge(consts_done, CONSTS)
            nc.gpsimd.memset(blank_rows, 0.0).then_inc(blank_rows_ready, 1)
            pool.wait_ge(blank_rows_ready, 1)
            nc.gpsimd.tensor_copy(blank_rows[:, :, D:], row_no[:, T:].unsqueeze(2)).then_inc(blank_rows_ready, 1)
            for s in S:
                for later in S[s["k"]:]:
                    linears = [b["k"] for b in S[:later["k"]] if b["kind"] == "linear"]
                    if later["kind"] == "softmax" and s["k"] == max(linears, default=-1) + 1:
                        softmax_pads(pool, later)
                if s["kind"] == "top2":
                    top2_gpsimd(pool, s)
                if s["kind"] == "top1":
                    top1_gpsimd(pool, s)
                if s["kind"] == "softmax":
                    softmax_gpsimd(pool, s)

        @block.tensor
        def _(pe):
            for s in S:
                tensor_of[s["kind"]](pe, s)

        @block.vector
        def _(vec):
            for s in S:
                vector_of[s["kind"]](vec, s)

        @block.scalar
        def _(act):
            for s in S:
                scalar_of[s["kind"]](act, s)


def kernel(L0_attn_x, L0_attn_Wq, L0_attn_Wk, L0_attn_Wv, L0_attn_Wo, L0_ffn_Wr, L0_ffn_We, L1_attn_Wq,
           L1_attn_bq, L1_attn_Wk, L1_attn_bk, L1_attn_Wv, L1_attn_bv, L1_attn_Wo, L1_attn_bo, L1_ffn_Wr,
           L1_ffn_br, L1_ffn_W1, L1_ffn_b1, L1_ffn_W2, L1_ffn_b2):
    import numpy as np
    import concourse.bacc as bacc
    from concourse.bass_utils import run_bass_kernel_spmd

    def a(x):
        return np.ascontiguousarray(x)

    def turned(x):
        return np.ascontiguousarray(np.asarray(x).T)

    def row(x):
        return np.ascontiguousarray(x).reshape(-1)

    def column(x):
        return np.ascontiguousarray(x).reshape(-1, 1)

    arrays = {
        "x_in": a(L0_attn_x),
        "wq0": turned(L0_attn_Wq), "wk0": turned(L0_attn_Wk), "wv0": turned(L0_attn_Wv), "wo0": turned(L0_attn_Wo),
        "wr0": turned(L0_ffn_Wr), "we0": a(L0_ffn_We),
        "wq1": turned(L1_attn_Wq), "bq1": column(L1_attn_bq), "wk1": turned(L1_attn_Wk), "bk1": column(L1_attn_bk),
        "wv1": turned(L1_attn_Wv), "bv1": column(L1_attn_bv), "wo1": turned(L1_attn_Wo), "bo1": row(L1_attn_bo),
        "wr1": a(L1_ffn_Wr), "br1": row(L1_ffn_br), "w11": a(L1_ffn_W1), "b11": np.ascontiguousarray(np.asarray(L1_ffn_b1).reshape(E * HC, P).T),
        "w21": a(L1_ffn_W2), "b21": row(L1_ffn_b2),
    }
    nc = bacc.Bacc("TRN2", target_bir_lowering=False, num_devices=1)
    args = [nc.dram_tensor(name, v.shape, mybir.dt.from_np(v.dtype), kind="ExternalInput").ap()
            for name, v in arrays.items()]
    out = nc.dram_tensor("out", (1, N, D), F32, kind="ExternalOutput").ap()
    macaron(nc, *args, out)
    r = run_bass_kernel_spmd(nc, [arrays], core_ids=[0])
    return r.results[0]["out"]
```
